# Optimizing a Trainium2 kernel written in Bass

```python
import numpy as np
import jax
import jax.numpy as jnp

def _softmax(x, axis=-1):
    return jax.nn.softmax(x, axis=axis)

def _gelu(x):
    return jax.nn.gelu(x, approximate=True)

def _silu(x):
    return jax.nn.silu(x)

def _sigmoid(x):
    return jax.nn.sigmoid(x)

def _layernorm(x, axis=-1, eps=1e-05):
    m = jnp.mean(x, axis=axis, keepdims=True)
    v = jnp.var(x, axis=axis, keepdims=True)
    return (x - m) / jnp.sqrt(v + eps)

def _scatter_add(tgt, idx, src, axis=0):
    return tgt.at[idx].add(src)

def _segment_sum(src, seg, n):
    return jax.ops.segment_sum(src, seg, n)
kernel_name = 'mk_prb_d1_jaxref_r8_e60e9e'

def setup_inputs(seed: int=0):
    np.random.seed(seed)
    _w = jnp.asarray

    def _L0_attn_setup():
        import jax, jax.numpy as jnp
        import numpy as np
        from jax import lax
        B, T, D = (2, 128, 256)
        H, DK, DV = (16, 128, 128)
        K_CONV = 4

        def _causal_dwconv(y, w, b):
            yc = y.transpose(0, 2, 1)
            out = lax.conv_general_dilated(yc, w, (1,), [(w.shape[-1] - 1, 0)], feature_group_count=yc.shape[1], dimension_numbers=('NCH', 'OIH', 'NCH'))
            return (out + b[None, :, None]).transpose(0, 2, 1)

        def _recurrence(q, k, v, a, beta):

            def step(S, xs):
                q_t, k_t, v_t, a_t, b_t = xs
                Sk = jnp.einsum('bhvk,bhk->bhv', S, k_t)
                S = a_t[..., None] * S - (b_t[..., None] * (Sk - v_t))[..., None] * k_t[:, :, None, :]
                o_t = jnp.einsum('bhvk,bhk->bhv', S, q_t)
                return (S, o_t)
            tfirst = lambda u: jnp.moveaxis(u, 1, 0)
            S0 = jnp.zeros((q.shape[0], q.shape[2], v.shape[3], q.shape[3]), q.dtype)
            _, o = lax.scan(step, S0, (tfirst(q), tfirst(k), tfirst(v), tfirst(a), tfirst(beta)))
            return jnp.moveaxis(o, 0, 1)

        def _forward(x, Wq, Wk, Wv, Wa, ba, Wb, bb, conv_q_w, conv_q_b, conv_k_w, conv_k_b, conv_v_w, conv_v_b, Wg, ln_g, ln_b, Wo):
            B_, T_, _ = x.shape
            q = jax.nn.silu(_causal_dwconv(x @ Wq.T, conv_q_w, conv_q_b))
            k = jax.nn.silu(_causal_dwconv(x @ Wk.T, conv_k_w, conv_k_b))
            v = jax.nn.silu(_causal_dwconv(x @ Wv.T, conv_v_w, conv_v_b))
            q = q.reshape(B_, T_, H, DK)
            k = k.reshape(B_, T_, H, DK) * DK ** (-0.5)
            v = v.reshape(B_, T_, H, DV)
            a = jax.nn.sigmoid(x @ Wa.T + ba).reshape(B_, T_, H, DV)
            beta = jax.nn.sigmoid(x @ Wb.T + bb)
            o = _recurrence(q, k, v, a, beta)
            mu = o.mean(-1, keepdims=True)
            var = ((o - mu) ** 2).mean(-1, keepdims=True)
            o = (o - mu) * lax.rsqrt(var + 1e-05) * ln_g + ln_b
            g = jax.nn.sigmoid(x @ Wg.T).reshape(B_, T_, H, DV)
            o = (o * g).reshape(B_, T_, H * DV)
            return o @ Wo.T
        key = jax.random.key(seed)
        ks = jax.random.split(key, 12)
        s = 0.02
        w = lambda k, shape: jax.random.normal(k, shape, jnp.float32) * s
        return {'x': jax.random.normal(ks[0], (B, T, D), jnp.float32), 'Wq': w(ks[1], (H * DK, D)), 'Wk': w(ks[2], (H * DK, D)), 'Wv': w(ks[3], (H * DV, D)), 'Wa': w(ks[4], (H * DV, D)), 'ba': jnp.zeros((H * DV,), jnp.float32), 'Wb': w(ks[5], (H, D)), 'bb': jnp.zeros((H,), jnp.float32), 'conv_q_w': w(ks[6], (H * DK, 1, K_CONV)), 'conv_q_b': jnp.zeros((H * DK,), jnp.float32), 'conv_k_w': w(ks[7], (H * DK, 1, K_CONV)), 'conv_k_b': jnp.zeros((H * DK,), jnp.float32), 'conv_v_w': w(ks[8], (H * DV, 1, K_CONV)), 'conv_v_b': jnp.zeros((H * DV,), jnp.float32), 'Wg': w(ks[9], (H * DV, D)), 'ln_g': jnp.ones((DV,), jnp.float32), 'ln_b': jnp.zeros((DV,), jnp.float32), 'Wo': w(ks[10], (D, H * DV))}
    _L0_attn_in = _L0_attn_setup()

    def _L0_ffn_setup():
        import jax, jax.numpy as jnp
        import numpy as np
        B, L, D = (2, 128, 256)
        E, TOP_K, RANK, DFF = (8, 2, 8, 688)

        def _lora(x, A, Bm, scale):
            return x @ A @ Bm * scale

        def _expert_lora(x, A, Bm, w, scale):
            xA = jnp.einsum('bld,edr->bler', x, A)
            xAB = jnp.einsum('bler,erd->bled', xA, Bm) * scale
            return (xAB * w).sum(axis=2)
        key = jax.random.key(seed)
        ks = jax.random.split(key, 18)
        r = lambda k, s, sc: jax.random.normal(k, s, dtype=jnp.float32) * sc
        inv_d = 1.0 / np.sqrt(D)
        inv_f = 1.0 / np.sqrt(DFF)
        return {'x': r(ks[0], (B, L, D), 1.0), 'W_router': r(ks[1], (D, E), inv_d), 'W_gate': r(ks[2], (D, DFF), inv_d), 'W_up': r(ks[3], (D, DFF), inv_d), 'W_down': r(ks[4], (DFF, D), inv_f), 'sA_gate': r(ks[5], (D, RANK), inv_d), 'sB_gate': r(ks[6], (RANK, DFF), 0.02), 'sA_up': r(ks[7], (D, RANK), inv_d), 'sB_up': r(ks[8], (RANK, DFF), 0.02), 'sA_down': r(ks[9], (DFF, RANK), inv_f), 'sB_down': r(ks[10], (RANK, D), 0.02), 'A_gate': r(ks[11], (E, D, RANK), inv_d), 'B_gate': r(ks[12], (E, RANK, DFF), 0.02), 'A_up': r(ks[13], (E, D, RANK), inv_d), 'B_up': r(ks[14], (E, RANK, DFF), 0.02), 'A_down': r(ks[15], (E, DFF, RANK), inv_f), 'B_down': r(ks[16], (E, RANK, D), 0.02), 'expert_bias': jnp.zeros((E,), dtype=jnp.float32)}
    _L0_ffn_in = _L0_ffn_setup()
    _d = {'L0_attn_x': _L0_attn_in['x'], 'L0_attn_Wq': _L0_attn_in['Wq'], 'L0_attn_Wk': _L0_attn_in['Wk'], 'L0_attn_Wv': _L0_attn_in['Wv'], 'L0_attn_Wa': _L0_attn_in['Wa'], 'L0_attn_ba': _L0_attn_in['ba'], 'L0_attn_Wb': _L0_attn_in['Wb'], 'L0_attn_bb': _L0_attn_in['bb'], 'L0_attn_conv_q_w': _L0_attn_in['conv_q_w'], 'L0_attn_conv_q_b': _L0_attn_in['conv_q_b'], 'L0_attn_conv_k_w': _L0_attn_in['conv_k_w'], 'L0_attn_conv_k_b': _L0_attn_in['conv_k_b'], 'L0_attn_conv_v_w': _L0_attn_in['conv_v_w'], 'L0_attn_conv_v_b': _L0_attn_in['conv_v_b'], 'L0_attn_Wg': _L0_attn_in['Wg'], 'L0_attn_ln_g': _L0_attn_in['ln_g'], 'L0_attn_ln_b': _L0_attn_in['ln_b'], 'L0_attn_Wo': _L0_attn_in['Wo'], 'L0_ffn_W_router': _L0_ffn_in['W_router'], 'L0_ffn_W_gate': _L0_ffn_in['W_gate'], 'L0_ffn_W_up': _L0_ffn_in['W_up'], 'L0_ffn_W_down': _L0_ffn_in['W_down'], 'L0_ffn_sA_gate': _L0_ffn_in['sA_gate'], 'L0_ffn_sB_gate': _L0_ffn_in['sB_gate'], 'L0_ffn_sA_up': _L0_ffn_in['sA_up'], 'L0_ffn_sB_up': _L0_ffn_in['sB_up'], 'L0_ffn_sA_down': _L0_ffn_in['sA_down'], 'L0_ffn_sB_down': _L0_ffn_in['sB_down'], 'L0_ffn_A_gate': _L0_ffn_in['A_gate'], 'L0_ffn_B_gate': _L0_ffn_in['B_gate'], 'L0_ffn_A_up': _L0_ffn_in['A_up'], 'L0_ffn_B_up': _L0_ffn_in['B_up'], 'L0_ffn_A_down': _L0_ffn_in['A_down'], 'L0_ffn_B_down': _L0_ffn_in['B_down'], 'L0_ffn_expert_bias': _L0_ffn_in['expert_bias']}
    _x0 = _d['L0_attn_x']
    _d['L0_attn_x'] = jax.random.normal(jax.random.fold_in(jax.random.key(seed), 1), (4, 512, 256), dtype=_x0.dtype)
    del _x0
    return _d

def reference(L0_attn_x, L0_attn_Wq, L0_attn_Wk, L0_attn_Wv, L0_attn_Wa, L0_attn_ba, L0_attn_Wb, L0_attn_bb, L0_attn_conv_q_w, L0_attn_conv_q_b, L0_attn_conv_k_w, L0_attn_conv_k_b, L0_attn_conv_v_w, L0_attn_conv_v_b, L0_attn_Wg, L0_attn_ln_g, L0_attn_ln_b, L0_attn_Wo, L0_ffn_W_router, L0_ffn_W_gate, L0_ffn_W_up, L0_ffn_W_down, L0_ffn_sA_gate, L0_ffn_sB_gate, L0_ffn_sA_up, L0_ffn_sB_up, L0_ffn_sA_down, L0_ffn_sB_down, L0_ffn_A_gate, L0_ffn_B_gate, L0_ffn_A_up, L0_ffn_B_up, L0_ffn_A_down, L0_ffn_B_down, L0_ffn_expert_bias):

    def _L0_attn_ref(x, Wq, Wk, Wv, Wa, ba, Wb, bb, conv_q_w, conv_q_b, conv_k_w, conv_k_b, conv_v_w, conv_v_b, Wg, ln_g, ln_b, Wo):
        import jax, jax.numpy as jnp
        import numpy as np
        from jax import lax
        B, T, D = (2, 128, 256)
        H, DK, DV = (16, 128, 128)
        K_CONV = 4

        def _causal_dwconv(y, w, b):
            yc = y.transpose(0, 2, 1)
            out = lax.conv_general_dilated(yc, w, (1,), [(w.shape[-1] - 1, 0)], feature_group_count=yc.shape[1], dimension_numbers=('NCH', 'OIH', 'NCH'))
            return (out + b[None, :, None]).transpose(0, 2, 1)

        def _recurrence(q, k, v, a, beta):

            def step(S, xs):
                q_t, k_t, v_t, a_t, b_t = xs
                Sk = jnp.einsum('bhvk,bhk->bhv', S, k_t)
                S = a_t[..., None] * S - (b_t[..., None] * (Sk - v_t))[..., None] * k_t[:, :, None, :]
                o_t = jnp.einsum('bhvk,bhk->bhv', S, q_t)
                return (S, o_t)
            tfirst = lambda u: jnp.moveaxis(u, 1, 0)
            S0 = jnp.zeros((q.shape[0], q.shape[2], v.shape[3], q.shape[3]), q.dtype)
            _, o = lax.scan(step, S0, (tfirst(q), tfirst(k), tfirst(v), tfirst(a), tfirst(beta)))
            return jnp.moveaxis(o, 0, 1)

        def _forward(x, Wq, Wk, Wv, Wa, ba, Wb, bb, conv_q_w, conv_q_b, conv_k_w, conv_k_b, conv_v_w, conv_v_b, Wg, ln_g, ln_b, Wo):
            B_, T_, _ = x.shape
            q = jax.nn.silu(_causal_dwconv(x @ Wq.T, conv_q_w, conv_q_b))
            k = jax.nn.silu(_causal_dwconv(x @ Wk.T, conv_k_w, conv_k_b))
            v = jax.nn.silu(_causal_dwconv(x @ Wv.T, conv_v_w, conv_v_b))
            q = q.reshape(B_, T_, H, DK)
            k = k.reshape(B_, T_, H, DK) * DK ** (-0.5)
            v = v.reshape(B_, T_, H, DV)
            a = jax.nn.sigmoid(x @ Wa.T + ba).reshape(B_, T_, H, DV)
            beta = jax.nn.sigmoid(x @ Wb.T + bb)
            o = _recurrence(q, k, v, a, beta)
            mu = o.mean(-1, keepdims=True)
            var = ((o - mu) ** 2).mean(-1, keepdims=True)
            o = (o - mu) * lax.rsqrt(var + 1e-05) * ln_g + ln_b
            g = jax.nn.sigmoid(x @ Wg.T).reshape(B_, T_, H, DV)
            o = (o * g).reshape(B_, T_, H * DV)
            return o @ Wo.T
        return _forward(x, Wq, Wk, Wv, Wa, ba, Wb, bb, conv_q_w, conv_q_b, conv_k_w, conv_k_b, conv_v_w, conv_v_b, Wg, ln_g, ln_b, Wo)

    def _L0_ffn_ref(x, W_router, W_gate, W_up, W_down, sA_gate, sB_gate, sA_up, sB_up, sA_down, sB_down, A_gate, B_gate, A_up, B_up, A_down, B_down, expert_bias):
        import jax, jax.numpy as jnp
        import numpy as np
        B, L, D = (2, 128, 256)
        E, TOP_K, RANK, DFF = (8, 2, 8, 688)

        def _lora(x, A, Bm, scale):
            return x @ A @ Bm * scale

        def _expert_lora(x, A, Bm, w, scale):
            xA = jnp.einsum('bld,edr->bler', x, A)
            xAB = jnp.einsum('bler,erd->bled', xA, Bm) * scale
            return (xAB * w).sum(axis=2)
        scale = 1.0 / RANK
        logits = x @ W_router
        scores = jax.nn.sigmoid(logits)
        biased = scores + expert_bias
        _, topk_idx = jax.lax.top_k(biased, TOP_K)
        topk_scores = jnp.take_along_axis(scores, topk_idx, axis=-1)
        topk_w = topk_scores / (topk_scores.sum(-1, keepdims=True) + 1e-08)
        one_hot = jax.nn.one_hot(topk_idx, E, dtype=x.dtype)
        expert_weights = (one_hot * topk_w[..., None]).sum(axis=2)
        w = expert_weights[..., None]
        gate = x @ W_gate + _lora(x, sA_gate, sB_gate, scale) + _expert_lora(x, A_gate, B_gate, w, scale)
        up = x @ W_up + _lora(x, sA_up, sB_up, scale) + _expert_lora(x, A_up, B_up, w, scale)
        hidden = jax.nn.silu(gate) * up
        out = hidden @ W_down + _lora(hidden, sA_down, sB_down, scale) + _expert_lora(hidden, A_down, B_down, w, scale)
        return out
    x = L0_attn_x
    xn = _layernorm(x, axis=-1)
    x = x + _L0_attn_ref(xn, L0_attn_Wq, L0_attn_Wk, L0_attn_Wv, L0_attn_Wa, L0_attn_ba, L0_attn_Wb, L0_attn_bb, L0_attn_conv_q_w, L0_attn_conv_q_b, L0_attn_conv_k_w, L0_attn_conv_k_b, L0_attn_conv_v_w, L0_attn_conv_v_b, L0_attn_Wg, L0_attn_ln_g, L0_attn_ln_b, L0_attn_Wo) + _L0_ffn_ref(xn, L0_ffn_W_router, L0_ffn_W_gate, L0_ffn_W_up, L0_ffn_W_down, L0_ffn_sA_gate, L0_ffn_sB_gate, L0_ffn_sA_up, L0_ffn_sB_up, L0_ffn_sA_down, L0_ffn_sB_down, L0_ffn_A_gate, L0_ffn_B_gate, L0_ffn_A_up, L0_ffn_B_up, L0_ffn_A_down, L0_ffn_B_down, L0_ffn_expert_bias)
    return x

_drawn_inputs = setup_inputs


def setup_inputs(seed=0):
    import zlib

    import numpy as np

    out = dict(_drawn_inputs(seed))
    spreads = {'L0_attn_ba': (0.0, 0.8),
     'L0_attn_bb': (0.0, 0.8),
     'L0_attn_conv_q_b': (0.0, 0.513),
     'L0_attn_conv_k_b': (0.0, 0.509),
     'L0_attn_conv_v_b': (0.0, 0.509),
     'L0_attn_ln_g': (1.0, 0.6),
     'L0_attn_ln_b': (0.0, 0.1),
     'L0_ffn_expert_bias': (0.0, 0.8)}
    factors = {'L0_attn_Wq': 8.0,
     'L0_attn_Wk': 8.0,
     'L0_attn_Wv': 8.0,
     'L0_attn_Wa': 8.0,
     'L0_attn_Wb': 8.0,
     'L0_attn_conv_q_w': 8.0,
     'L0_attn_conv_k_w': 8.0,
     'L0_attn_conv_v_w': 8.0,
     'L0_attn_Wg': 8.0,
     'L0_ffn_W_router': 8.0,
     'L0_ffn_sA_gate': 8.0,
     'L0_ffn_sB_gate': 8.0,
     'L0_ffn_sA_up': 8.0,
     'L0_ffn_sB_up': 8.0,
     'L0_ffn_sA_down': 8.0,
     'L0_ffn_sB_down': 8.0,
     'L0_ffn_A_gate': 8.0,
     'L0_ffn_B_gate': 8.0,
     'L0_ffn_A_up': 8.0,
     'L0_ffn_B_up': 8.0,
     'L0_ffn_A_down': 8.0,
     'L0_ffn_B_down': 8.0}
    for name, (base, spread) in spreads.items():
        noise = np.random.default_rng([zlib.crc32(name.encode()), seed]).standard_normal(out[name].shape)
        drawn = base * np.exp(spread * noise) if base else spread * noise
        out[name] = jnp.asarray(drawn.astype(out[name].dtype))
    for name, factor in factors.items():
        out[name] = (out[name] * factor).astype(out[name].dtype)
    return out
```

```python
from contextlib import ExitStack

import concourse.bass as bass
from concourse import mybir

F32 = mybir.dt.float32
ALU = mybir.AluOpType
ACT = mybir.ActivationFunctionType
AX = mybir.AxisListType

B, T, D, H, DH = 4, 512, 256, 16, 128
NP = B * H
NT = B * T
KC = 4
E, R, DFF = 8, 8, 688
C = 16
BL = 4
NB = C // BL
NSUP = T // C
TOK = C * B
HALO = (KC - 1) * B
NI = 2 * C
LR = E * R + R
NF = (DFF + 127) // 128
FW = (DFF + NF - 1) // NF
FT = [min(FW, DFF - FW * f) for f in range(NF)]
NX = NT // 128
CH = 512
NCH = NT // CH
OFF = [0, 7, 12, 15]
K_SCALE = float(DH) ** -0.5
HALF = NP // 2

CW0, CB0 = 0, 3 * KC * H
BA0 = CB0 + 3 * H
BB0 = BA0 + H
LN0 = BB0 + H
WB0 = LN0 + 2
EB0 = WB0 + 2 * H
WR0 = EB0 + E
NSMALL = WR0 + 2 * E

PIECES = []
for m in range(NB - 1):
    lo = 2 * BL * (m + 1)
    cuts = [(i, min(i + 16, NI)) for i in range(lo, NI, 16)]
    PIECES.append([(half, a, b) for half in range(2) for a, b in cuts])
NPIECE = [len(x) for x in PIECES]
NWK = 2 * sum(NPIECE)
WK0 = [2 * sum(NPIECE[:m]) for m in range(NB)]

PROJ = ([("q", i) for i in range(4)] + [("v", i) for i in range(4)] + [("b", i) for i in range(2)]
        + [("k", i) for i in range(4)] + [("a", i) for i in range(2)] + [("g", i) for i in range(2)])
NPR = len(PROJ)
WSLOT = {"q": 0, "k": 1, "v": 2, "a": 3, "g": 4}


def last_piece(kind):
    return max(i for i, (k, _) in enumerate(PROJ) if k == kind)


def build(nc, x_tm, wqT, wkT, wvT, waT, wgT, woT, small, w_gate, w_up, w_down, a_gate, b_gate,
          a_up, b_up, a_down, b_down, out):
    xnT_d = nc.dram_tensor("xnT_d", (2, 128, HALO + NT), F32, kind="Internal").ap()
    base_d = nc.dram_tensor("base_d", (NT, D), F32, kind="Internal").ap()

    with ExitStack() as ctx:
        def sb(name, shape):
            return ctx.enter_context(nc.sbuf_tensor(name, shape, F32))

        def sem(name):
            return ctx.enter_context(nc.semaphore(name))

        W5 = sb("W5", [128, 5, 2, H * DH])
        WO = sb("WO", [128, H, D])
        SM = sb("SM", [128, NSMALL])
        ident = sb("ident", [128, 128])
        ones = sb("ones", [128, 128])
        maskG = sb("maskG", [128, HALF])
        maskKT = sb("maskKT", [128, 2])
        tri = sb("tri", [128, E, E])
        eps = sb("eps", [128, 1])
        ACH = sb("ACH", [128, NP])
        XC = sb("XC", [128, 2, HALO + TOK])
        RES = sb("RES", [2 * TOK, 128])
        OUTT = sb("OUTT", [2 * TOK, 128])
        YT = sb("YT", [128, 2, TOK])
        NARENA = 25216
        arena = sb("arena", [128, NARENA])
        CW = SM[:, CW0:CW0 + 3 * KC * H].rearrange("p (x i h) -> p x i h", x=3, i=KC)
        CB = SM[:, CB0:CB0 + 3 * H].rearrange("p (x h) -> p x h", x=3)
        BA = SM[:, BA0:BA0 + H]
        BB = SM[:, BB0:BB0 + H]
        LNG, LNB = SM[:, LN0:LN0 + 1], SM[:, LN0 + 1:LN0 + 2]
        WB = SM[:, WB0:WB0 + 2 * H].rearrange("p (c h) -> p c h", c=2)
        EB = SM[:, EB0:EB0 + E]
        WR = SM[:, WR0:WR0 + 2 * E].rearrange("p (c e) -> p c e", c=2)

        pos = [0]

        def take(n):
            pos[0] += n
            assert pos[0] <= NARENA
            return arena[:, pos[0] - n:pos[0]]

        S = take(NP * DH).rearrange("v (p k) -> v p k", p=NP)
        STR = take(2 * 4 * DH).rearrange("k (s q v) -> k s q v", s=2, q=4)
        Xf = take(NI * NP)
        X = Xf.rearrange("v (i p) -> v i p", p=NP)
        Xo = Xf.rearrange("v (t e p) -> v t e p", e=2, p=NP)[:, :, 1, :]
        TMP, SIGV = Xf[:, 0:C * NP], Xf[:, C * NP:2 * C * NP]
        KQf = take(NI * NP)
        KQ = KQf.rearrange("k (i p) -> k i p", p=NP)
        KQte = KQf.rearrange("k (t e p) -> k t e p", e=2, p=NP)
        DD, RS = KQf[:, 0:C * NP], KQf[:, C * NP:2 * C * NP]
        KRf = take(C * NP)
        KR = KRf.rearrange("k (a t p) -> k a t p", a=2, p=HALF)
        BVf = take(C * NP)
        BV = BVf.rearrange("v (t p) -> v t p", p=NP)
        Af = take(C * NP)
        A = Af.rearrange("v (t p) -> v t p", p=NP)
        Wf = take(C * NP)
        W = Wf.rearrange("v (a t p) -> v a t p", a=2, p=HALF)
        BETA = Wf.rearrange("v (t a p) -> v a t p", a=2, p=HALF)
        PRE0 = take((C + KC - 1) * NP)
        PRE1 = take((C + KC - 1) * NP)
        ACC0 = take(C * NP)
        ACC1 = take(C * NP)
        PRf = take(C * NP)
        PR = PRf.rearrange("k (i p) -> k i p", p=NP)
        PT = PRf.rearrange("r (s v) -> r s v", s=8)
        U1 = take(2048)
        PREK = U1[:, 0:(C + KC - 1) * NP]
        GBD = U1[:, 0:2 * 24 * HALF].rearrange("r (a i p) -> r a i p", a=2, i=24)
        KTB = U1.rearrange("r (s e k) -> r s e k", s=8, e=2)
        WHT = take(256)
        PP = PRE0[:, 0:C * NP].rearrange("v (p t) -> v p t", t=C)
        KP = PRE1[:, 0:C * NP].rearrange("k (p t) -> k p t", t=C)
        PREs = {"q": PRE0, "v": PRE1, "k": PREK}
        ACCs = {"q": ACC0, "v": BVf, "k": PRf}
        SIGs = {"q": ACC1, "v": SIGV, "k": ACC1}
        CWI = {"q": 0, "k": 1, "v": 2}
        SFX = ACC0[:, 0:NB * 3 * NP // 1][:, 0:768].rearrange("v (m j p) -> v m j p", m=NB, j=3)
        ABL = ACC0[:, 768:1024].rearrange("v (m p) -> v m p", m=NB)
        TT = ACC1[:, 0:448].rearrange("v (a i p) -> v a i p", a=2, i=7)
        ASF = ACC1[:, 448:448 + NB * NP].rearrange("v (m p) -> v m p", m=NB)

        pos[0] = 0
        XIN = take(NX * D).rearrange("p (n d) -> p n d", n=NX)
        XNf = take(NX * D)
        XN = XNf.rearrange("p (n d) -> p n d", n=NX)
        GT = XNf[:, 0:NX * 64].rearrange("p (n a b) -> p n a b", n=NX, a=E)
        EQ = XNf[:, 1024:1024 + NX * 64].rearrange("p (n a b) -> p n a b", n=NX, a=E)
        WEXP = XNf[:, 2048:2048 + NX * LR].rearrange("p (n l) -> p n l", n=NX)
        HID = XNf[:, 0:NF * CH].rearrange("p (f t) -> p f t", f=NF)
        XNT = take(2 * (HALO + NT)).rearrange("p (c t) -> p c t", c=2)
        WG = take(2 * DFF).rearrange("p (c f) -> p c f", c=2)
        WU = take(2 * DFF).rearrange("p (c f) -> p c f", c=2)
        WD = take(NF * D).rearrange("p (f d) -> p f d", f=NF)
        BG = take(DFF)
        BU = take(DFF)
        AD = take(NF * LR).rearrange("p (f l) -> p f l", f=NF)
        AG = take(2 * LR).rearrange("p (c l) -> p c l", c=2)
        AU = take(2 * LR).rearrange("p (c l) -> p c l", c=2)
        BD = take(D)
        WT = take(NT)
        XAG = take(CH)
        XAU = take(CH)
        SG = take(2 * CH).rearrange("p (s t) -> p s t", s=2)
        SQ = SG.rearrange("p s t -> p (s t)")
        HAD = take(CH)
        BASE = take(2 * D).rearrange("p (s d) -> p s d", s=2)
        ST8 = take(8 * NX).rearrange("p (k n) -> p k n", k=8)
        SC = take(NX * E).rearrange("p (n e) -> p n e", n=NX)
        BI = take(NX * E).rearrange("p (n e) -> p n e", n=NX)
        RK = take(NX * E).rearrange("p (n e) -> p n e", n=NX)

        PS = ctx.enter_context(nc.psum_tensor("PS", [128, 8 * 512], F32))

        def bank(i, n=512, k=1):
            return PS[:, 512 * i:512 * i + n * k]

        ld_x = [sem(f"ld_x{c}") for c in range(4)]
        ld_small, ld_ffn, ld_attn = sem("ld_small"), sem("ld_ffn"), sem("ld_attn")
        consts, masks = sem("consts"), sem("masks")
        ln_step, ln_var, ln_std, xn_ready = sem("ln_step"), sem("ln_var"), sem("ln_std"), sem("xn_ready")
        xnT_psum, xnT_ready, xnT_stored = sem("xnT_psum"), sem("xnT_ready"), sem("xnT_stored")
        logits, scores, rt_step = sem("logits"), sem("scores"), sem("rt_step")
        wT_psum, wT_ready = sem("wT_psum"), sem("wT_ready")
        xa_psum, xa_ready = sem("xa_psum"), sem("xa_ready")
        gu_psum, gu_sig, gu_silu, hid_ready = sem("gu_psum"), sem("gu_sig"), sem("gu_silu"), sem("hid_ready")
        had_psum, had_ready = sem("had_psum"), sem("had_ready")
        ffn_psum, base_ready = sem("ffn_psum"), sem("base_ready")
        base_stored = [sem(f"base_stored{i}") for i in range(2)]
        xc_in, res_in, out_stored = sem("xc_in"), sem("res_in"), sem("out_stored")
        proj_full, proj_free = sem("proj_full"), sem("proj_free")
        tap3 = sem("tap3")
        tap_mul, tap_add, sig_ready, silu_ready = sem("tap_mul"), sem("tap_add"), sem("sig_ready"), sem("silu_ready")
        bv_ready, kq_ready = sem("bv_ready"), sem("kq_ready")
        sfx = sem("suffix_products")
        st_psum, st_ready, ro_psum, x_ready = sem("st_psum"), sem("st_ready"), sem("ro_psum"), sem("x_ready")
        prod_ready, bcast_psum = sem("prod_ready"), sem("bcast_psum")
        wk_full, wk_free = sem("work_full"), sem("work_free")
        w_ready, x_decayed, wg_ready, x_step = sem("w_ready"), sem("x_decayed"), sem("wg_ready"), sem("x_step")
        what_ready, x_blk = sem("what_ready"), sem("x_block_decayed")
        wht_psum, wht_ready = sem("wht_psum"), sem("wht_ready")
        s_scaled = sem("s_scaled")
        kp_ready, kt_psum, kt_ready = sem("kp_ready"), sem("kt_psum"), sem("kt_ready")
        p_ready, pt_psum, pt_ready = sem("p_ready"), sem("pt_psum"), sem("pt_ready")
        up_psum, s_updated = sem("up_psum"), sem("s_updated")
        mean_psum, centred, squared, var_psum, std = sem("mean_psum"), sem("centred"), sem("squared"), sem("var_psum"), sem("std")
        rstd, normed, affine, gate_ready, gated = sem("rstd"), sem("normed"), sem("affine"), sem("gate_ready"), sem("gated")
        y_psum, y_ready, yt_psum, fin = sem("y_psum"), sem("y_ready"), sem("yt_psum"), sem("out_tile")

        block = ctx.enter_context(nc.Block())
        x_v = x_tm.rearrange("(n p) d -> p n d", p=128)

        @block.sync
        def _(sp):
            for c in range(4):
                sp.dma_start(XIN[:, 4 * c:4 * c + 4, :], x_v[:, 4 * c:4 * c + 4, :]).then_inc(ld_x[c], 16)
            n_ffn = 0
            for dst, src in ((WG, w_gate.rearrange("(c p) f -> p c f", p=128)),
                             (WU, w_up.rearrange("(c p) f -> p c f", p=128)),
                             (AG, a_gate.rearrange("(c p) l -> p c l", p=128)),
                             (AU, a_up.rearrange("(c p) l -> p c l", p=128)),
                             (BG[0:LR, :], b_gate), (BU[0:LR, :], b_up), (BD[0:LR, :], b_down),
                             (WD[0:FW, 0:NF - 1, :], w_down[0:FW * (NF - 1), :].rearrange("(f p) d -> p f d", p=FW)),
                             (WD[0:FT[-1], NF - 1, :], w_down[FW * (NF - 1):DFF, :]),
                             (AD[0:FW, 0:NF - 1, :], a_down[0:FW * (NF - 1), :].rearrange("(f p) l -> p f l", p=FW)),
                             (AD[0:FT[-1], NF - 1, :], a_down[FW * (NF - 1):DFF, :])):
                sp.dma_start(dst, src).then_inc(ld_ffn, 16)
                n_ffn += 1
            assert n_ffn == 11
            for i, w in enumerate((wqT, wkT, wvT, waT, wgT)):
                sp.dma_start(W5[:, i, :, :], w.rearrange("(c p) n -> p c n", p=128)).then_inc(ld_attn, 16)
            sp.dma_start(WO[:, :, :], woT.rearrange("(h p) d -> p h d", p=128)).then_inc(ld_attn, 16)
            for stored in base_stored + [out_stored]:
                sp.sem_inc(stored, 32 if stored is out_stored else 16)
            sp.wait_ge(xnT_ready, 8)
            sp.dma_start(xnT_d.rearrange("c p t -> p c t"), XNT[:, :, :]).then_inc(xnT_stored, 16)
            with sp.Fori(0, NCH) as c:
                for q in range(4):
                    sp.wait_ge(base_ready, c * 4 + q + 1)
                    sp.dma_start(base_d[bass.ds(c * CH + 128 * q, 128), :], BASE[:, q % 2, :]).then_inc(base_stored[q % 2], 16)
            with sp.Fori(0, NSUP) as n:
                sp.wait_ge(fin, n + 2)
                for dh in range(2):
                    sp.dma_start(out[bass.ds(n * TOK, TOK), 128 * dh:128 * (dh + 1)], OUTT[TOK * dh:TOK * (dh + 1), :]).then_inc(out_stored, 16)
            sp.wait_ge(out_stored, 32 * NSUP + 32)

        @block.gpsimd
        def _(pool):
            pool.dma_start(SM[:, :], small).then_inc(ld_small, 16)
            nc.gpsimd.memset(ident[:, :], 0.0).then_inc(consts, 1)
            nc.gpsimd.memset(tri[:, :, :], 1.0).then_inc(consts, 1)
            nc.gpsimd.memset(ones[:, :], 1.0).then_inc(consts, 1)
            nc.gpsimd.memset(eps[:, :], 1e-5).then_inc(consts, 1)
            nc.gpsimd.memset(XNT[:, :, 0:HALO], 0.0).then_inc(consts, 1)
            pool.wait_ge(consts, 5)
            nc.gpsimd.affine_select(out=ident[:, :], in_=ident[:, :], compare_op=ALU.not_equal, fill=1.0,
                                    base=0, pattern=[[-1, 128]], channel_multiplier=1).then_inc(consts, 1)
            nc.gpsimd.affine_select(out=tri[:, :, :], in_=tri[:, :, :], compare_op=ALU.is_gt, fill=0.0,
                                    base=0, pattern=[[1, E], [-1, E]], channel_multiplier=0).then_inc(consts, 1)
            pool.wait_ge(xnT_stored, 16)
            for stored in base_stored:
                pool.wait_ge(stored, 16 * NX // 2 + 16)
            with pool.Fori(0, NSUP) as n:
                pool.wait_ge(proj_full, n * NPR + 1)
                pool.dma_start(XC[:, :, :], xnT_d[:, :, bass.ds(n * TOK, HALO + TOK)].rearrange("c p t -> p c t")).then_inc(xc_in, 16)
                pool.wait_ge(fin, n + 1)
                for dh in range(2):
                    pool.dma_start(RES[TOK * dh:TOK * (dh + 1), :], base_d[bass.ds(n * TOK, TOK), 128 * dh:128 * (dh + 1)]).then_inc(res_in, 16)

        @block.scalar
        def _(act):
            act.wait_ge(consts, 4)
            for c in range(4):
                act.wait_ge(ln_var, c + 1)
                nc.scalar.activation(ST8[:, 2, 4 * c:4 * c + 4], ST8[:, 1, 4 * c:4 * c + 4], ACT.Sqrt,
                                     bias=eps[:, 0:1], scale=1.0 / D).then_inc(ln_std, 1)
                if c > 0:
                    for k in range(2):
                        act.wait_ge(xnT_psum, 2 * (c - 1) + k + 1)
                        nc.scalar.copy(XNT[:, k, HALO + CH * (c - 1):HALO + CH * c], bank(2 * (c - 1) + k)).then_inc(xnT_ready, 1)
            for k in range(2):
                act.wait_ge(xnT_psum, 6 + k + 1)
                nc.scalar.copy(XNT[:, k, HALO + CH * 3:HALO + CH * 4], bank(6 + k)).then_inc(xnT_ready, 1)
            act.wait_ge(logits, 1)
            nc.scalar.activation(SC[:, :, :], bank(0, 128).rearrange("p (n e) -> p n e", n=NX), ACT.Sigmoid).then_inc(scores, 1)
            for i in range(4):
                act.wait_ge(wT_psum, i + 1)
                nc.scalar.copy(WT[0:LR, CH * i:CH * (i + 1)], bank(1 + i)[0:LR, :]).then_inc(wT_ready, 1)
            with act.Fori(0, NCH) as c:
                for f in range(NF):
                    act.wait_ge(gu_psum, c * NF + f + 1)
                    if f >= 2:
                        act.wait_ge(hid_ready, c * NF + f - 1)
                    nc.scalar.activation(SG[0:FT[f], f % 2, :], bank(2 * (f % 2))[0:FT[f], :], ACT.Sigmoid).then_inc(gu_sig, 1)
            act.wait_ge(s_updated, 1)
            for _ in range(2):
                nc.scalar.nop().then_inc(proj_free, 1)
            with act.Fori(0, NSUP) as n:
                def evacuate(kind):
                    for g, (kd, i) in enumerate(PROJ):
                        if kd != kind:
                            continue
                        act.wait_ge(proj_full, n * NPR + g + 2)
                        bk = bank(g % 2)
                        if kind in "qvk":
                            ps = bk[:, 0:4 * (HALO + TOK)].rearrange("p (h n) -> p h n", h=4)
                            nc.scalar.copy(PREs[kind].rearrange("p (n h) -> p n h", h=H)[:, :, 4 * i:4 * i + 4],
                                           ps.rearrange("p h n -> p n h")).then_inc(tap3, 1)
                            for h in range(4):
                                hh = 4 * i + h
                                ins = nc.scalar.activation(
                                    ACCs[kind].rearrange("p (n h) -> p n h", h=H)[:, :, hh], ps[:, h, HALO:],
                                    ACT.Identity, bias=CB[:, CWI[kind], hh:hh + 1], scale=CW[:, CWI[kind], KC - 1, hh:hh + 1])
                            ins.then_inc(proj_free, 1)
                        elif kind == "g":
                            nc.scalar.activation(BVf.rearrange("p (n h) -> p n h", h=H)[:, :, 8 * i:8 * i + 8],
                                                 bk.rearrange("p (h n) -> p n h", h=8), ACT.Sigmoid).then_inc(proj_free, 1)
                        else:
                            dst, bias = (Wf, BB) if kind == "b" else (Af, BA)
                            for h in range(8):
                                hh = 8 * i + h
                                ins = nc.scalar.activation(dst.rearrange("p (n h) -> p n h", h=H)[:, :, hh],
                                                           bk[:, TOK * h:TOK * (h + 1)], ACT.Sigmoid, bias=bias[:, hh:hh + 1])
                            ins.then_inc(proj_free, 1)

                def sigmoid_of(kind, j):
                    act.wait_ge(tap_add, n * 9 + 3 * j + 3)
                    nc.scalar.activation(SIGs[kind], ACCs[kind], ACT.Sigmoid).then_inc(sig_ready, 1)

                def scale_state(lo, hi):
                    for p in range(lo, hi):
                        nc.scalar.mul(S[:, p, :], S[:, p, :], ACH[:, p:p + 1]).then_inc(s_scaled, 1)

                evacuate("q")
                evacuate("v")
                evacuate("b")
                sigmoid_of("q", 0)
                act.wait_ge(s_updated, n * 16 + 1)
                evacuate("k")
                evacuate("a")
                sigmoid_of("v", 1)
                act.wait_ge(silu_ready, n * 3 + 1)
                sigmoid_of("k", 2)
                for j in range(16):
                    act.wait_ge(st_psum, n * 16 + j + 1)
                    if j >= 2:
                        act.wait_ge(ro_psum, n * 16 + j - 1)
                    nc.scalar.copy(STR[:, j % 2, :, :], bank(6 + j % 2).rearrange("k (q v) -> k q v", q=4)).then_inc(st_ready, 1)
                    if j >= 4 and j % 4 == 1:
                        r = j // 4 - 1
                        act.wait_ge(ro_psum, n * 16 + 4 * r + 4)
                        nc.scalar.copy(X[:, :, 16 * r:16 * r + 16], bank(4 + r % 2).rearrange("v (i p) -> v i p", p=16)).then_inc(x_ready, 1)
                act.wait_ge(ro_psum, n * 16 + 16)
                nc.scalar.copy(X[:, :, 48:64], bank(5).rearrange("v (i p) -> v i p", p=16)).then_inc(x_ready, 1)
                act.wait_ge(sfx, n * 8 + 8)
                for m in range(NB - 1):
                    scale_state(16 * m, 16 * m + 16)
                    act.wait_ge(wht_psum, n * 3 + m + 1)
                    nc.scalar.copy(WHT[:, :], bank(6, 256)).then_inc(wht_ready, 1)
                scale_state(48, 64)
                nc.scalar.copy(KP.rearrange("k (a p) t -> k a t p", a=2), KR).then_inc(kp_ready, 1)
                act.wait_ge(kt_psum, n + 1)
                for s in range(8):
                    for e in range(2):
                        ins = nc.scalar.mul(KTB[:, s, e, :], PS[:, 2048 + 128 * s:2048 + 128 * (s + 1)],
                                            maskKT[:, e:e + 1])
                ins.then_inc(kt_ready, 1)
                act.wait_ge(w_ready, n * C + C)
                evacuate("g")
                act.wait_ge(centred, n + 1)
                nc.scalar.activation(RS, DD, ACT.Square).then_inc(squared, 1)
                for i in range(2):
                    act.wait_ge(pt_psum, n * 2 + i + 1)
                    nc.scalar.copy(PT[:, 4 * i:4 * i + 4, :], bank(2 + i).rearrange("r (s v) -> r s v", s=4)).then_inc(pt_ready, 1)
                act.wait_ge(var_psum, n + 1)
                nc.scalar.activation(RS, PS[:, 3072:4096], ACT.Sqrt, bias=eps[:, 0:1], scale=1.0 / DH).then_inc(std, 1)
                act.wait_ge(normed, n + 1)
                nc.scalar.activation(DD, DD, ACT.Identity, bias=LNB, scale=LNG).then_inc(affine, 1)
                act.wait_ge(y_psum, n + 1)
                nc.scalar.copy(YT[:, :, :], bank(6, 2 * TOK).rearrange("p (c t) -> p c t", c=2)).then_inc(y_ready, 1)

        @block.vector
        def _(dve):
            tt = nc.vector.tensor_tensor
            for c in range(4):
                cs = slice(4 * c, 4 * c + 4)
                dve.wait_ge(ld_x[c], 16)
                nc.vector.tensor_reduce(ST8[:, 0, cs], XIN[:, cs, :], AX.X, ALU.add).then_inc(ln_step, 1)
                dve.wait_ge(ln_step, 5 * c + 1)
                nc.vector.tensor_scalar(ST8[:, 3, cs], ST8[:, 0, cs], -1.0 / D, None, ALU.mult).then_inc(ln_step, 1)
                dve.wait_ge(ln_step, 5 * c + 2)
                tt(XN[:, cs, :], XIN[:, cs, :], ST8[:, 3, cs].unsqueeze(2).to_broadcast([128, 4, D]), ALU.add).then_inc(ln_step, 1)
                dve.wait_ge(ln_step, 5 * c + 3)
                tt(SQ.rearrange("p (n d) -> p n d", n=4), XN[:, cs, :], XN[:, cs, :], ALU.mult).then_inc(ln_step, 1)
                dve.wait_ge(ln_step, 5 * c + 4)
                nc.vector.tensor_reduce(ST8[:, 1, cs], SQ.rearrange("p (n d) -> p n d", n=4), AX.X, ALU.add).then_inc(ln_var, 1)
                dve.wait_ge(ln_std, c + 1)
                nc.vector.reciprocal(ST8[:, 4, cs], ST8[:, 2, cs]).then_inc(ln_step, 1)
                dve.wait_ge(ln_step, 5 * c + 5)
                tt(XN[:, cs, :], XN[:, cs, :], ST8[:, 4, cs].unsqueeze(2).to_broadcast([128, 4, D]), ALU.mult).then_inc(xn_ready, 1)
            dve.wait_ge(consts, 7)
            nc.vector.tensor_reduce(maskG[:, :], ident[:, :].rearrange("r (j p) -> r p j", p=HALF), AX.X, ALU.add).then_inc(masks, 1)
            nc.vector.tensor_reduce(maskKT[:, :], ident[:, :].rearrange("r (g e i) -> r e g i", g=4, e=2), AX.XY, ALU.add).then_inc(masks, 1)
            dve.wait_ge(ld_small, 16)
            dve.wait_ge(scores, 1)
            steps = [0]

            def link(ins):
                ins.then_inc(rt_step, 1)
                steps[0] += 1
                dve.wait_ge(rt_step, steps[0])

            link(tt(BI[:, :, :], SC[:, :, :], EB.unsqueeze(1).to_broadcast([128, NX, E]), ALU.add))
            other = BI.unsqueeze(2).to_broadcast([128, NX, E, E])
            own = BI.unsqueeze(3).to_broadcast([128, NX, E, E])
            dve.wait_ge(xnT_ready, 8)
            link(tt(GT, other, own, ALU.is_gt))
            link(tt(EQ, other, own, ALU.is_equal))
            link(tt(EQ, EQ, tri[:, :, :].unsqueeze(1).to_broadcast([128, NX, E, E]), ALU.mult))
            link(tt(GT, GT, EQ, ALU.add))
            link(nc.vector.tensor_reduce(RK[:, :, :], GT, AX.X, ALU.add))
            link(nc.vector.tensor_scalar(RK[:, :, :], RK[:, :, :], 1.5, None, ALU.is_lt))
            link(tt(RK[:, :, :], RK[:, :, :], SC[:, :, :], ALU.mult))
            link(nc.vector.tensor_reduce(ST8[:, 5, :], RK[:, :, :], AX.X, ALU.add))
            link(nc.vector.tensor_scalar(ST8[:, 5, :], ST8[:, 5, :], 1e-8, None, ALU.add))
            link(nc.vector.reciprocal(ST8[:, 6, :], ST8[:, 5, :]))
            link(nc.vector.tensor_scalar(ST8[:, 6, :], ST8[:, 6, :], 1.0 / R, None, ALU.mult))
            link(tt(RK[:, :, :], RK[:, :, :], ST8[:, 6, :].unsqueeze(2).to_broadcast([128, NX, E]), ALU.mult))
            link(nc.vector.memset(WEXP[:, :, E * R:LR], 1.0 / R))
            link(nc.vector.tensor_copy(WEXP[:, :, 0:E * R].rearrange("p n (e r) -> p n e r", e=E),
                                       RK.unsqueeze(3).to_broadcast([128, NX, E, R])))
            assert steps[0] == 15
            dve.wait_ge(wT_ready, 4)
            nc.vector.nop().then_inc(had_ready, 1)
            with dve.Fori(0, NCH) as c:
                wt = WT[0:LR, bass.ds(c * CH, CH)]
                for k, dst in enumerate((XAG, XAU)):
                    dve.wait_ge(xa_psum, c * 2 + k + 1)
                    tt(dst[0:LR, :], bank(4 + k)[0:LR, :], wt, ALU.mult).then_inc(xa_ready, 1)
                for f in range(NF):
                    fr = slice(0, FT[f])
                    dve.wait_ge(gu_sig, c * NF + f + 1)
                    tt(SG[fr, f % 2, :], SG[fr, f % 2, :], bank(2 * (f % 2))[fr, :], ALU.mult).then_inc(gu_silu, 1)
                    dve.wait_ge(gu_silu, c * NF + f + 1)
                    tt(HID[fr, f, :], SG[fr, f % 2, :], bank(2 * (f % 2) + 1)[fr, :], ALU.mult).then_inc(hid_ready, 1)
                dve.wait_ge(had_psum, c + 1)
                tt(HAD[0:LR, :], bank(5)[0:LR, :], wt, ALU.mult).then_inc(had_ready, 1)
                for q in range(4):
                    dve.wait_ge(ffn_psum, c * 4 + q + 1)
                    dve.wait_ge(base_stored[q % 2], c * 32 + 16 * (q // 2) + 16)
                    tt(BASE[:, q % 2, :], bank(6 + q % 2, D), XIN[:, bass.ds(c * 4 + q, 1), :].rearrange("p a d -> p (a d)"), ALU.add).then_inc(base_ready, 1)
            for stored in base_stored:
                dve.wait_ge(stored, 16 * NX // 2 + 16)
            dve.wait_ge(xnT_stored, 16)
            nc.vector.memset(S[:, :, :], 0.0).then_inc(s_updated, 1)
            nc.vector.nop().then_inc(fin, 1)
            dve.wait_ge(s_updated, 1)
            with dve.Fori(0, NSUP) as n:
                def conv(kind, j):
                    dve.wait_ge(proj_free, n * NPR + 2 + last_piece(kind) + 1)
                    for i in range(KC - 1):
                        w = CW[:, CWI[kind], i, :].unsqueeze(1).to_broadcast([128, TOK, H])
                        if i > 0:
                            dve.wait_ge(tap_add, n * 9 + 3 * j + i)
                        elif j > 0:
                            dve.wait_ge(tap_add, n * 9 + 3 * j)
                        tt(TMP.rearrange("p (n h) -> p n h", h=H),
                           PREs[kind][:, NP * i:NP * (i + C)].rearrange("p (n h) -> p n h", h=H), w, ALU.mult).then_inc(tap_mul, 1)
                        dve.wait_ge(tap_mul, n * 9 + 3 * j + i + 1)
                        tt(ACCs[kind], ACCs[kind], TMP, ALU.add).then_inc(tap_add, 1)

                conv("q", 0)
                conv("v", 1)
                dve.wait_ge(sig_ready, n * 3 + 1)
                tt(KQte[:, :, 1, :], ACC0.rearrange("p (t q) -> p t q", q=NP), SIGs["q"].rearrange("p (t q) -> p t q", q=NP), ALU.mult).then_inc(silu_ready, 1)
                conv("k", 2)
                dve.wait_ge(sig_ready, n * 3 + 2)
                tt(BVf, BVf, SIGV, ALU.mult).then_inc(silu_ready, 1)
                dve.wait_ge(silu_ready, n * 3 + 2)
                tt(BVf, BVf, Wf, ALU.mult).then_inc(bv_ready, 1)
                dve.wait_ge(proj_free, n * NPR + 2 + last_piece("a") + 1)
                A4 = Af.rearrange("v (m j p) -> v m j p", m=NB, j=BL)
                nc.vector.tensor_copy(SFX[:, :, 2, :], A4[:, :, 3, :]).then_inc(sfx, 1)
                tt(SFX[:, :, 1, :], A4[:, :, 2, :], A4[:, :, 3, :], ALU.mult).then_inc(sfx, 1)
                dve.wait_ge(sig_ready, n * 3 + 3)
                for a in range(2):
                    ins = nc.vector.scalar_tensor_tensor(KR[:, a, :, :], SIGs["k"].rearrange("k (t a p) -> k a t p", a=2, p=HALF)[:, a], K_SCALE,
                                                         PRf.rearrange("k (t a p) -> k a t p", a=2, p=HALF)[:, a], ALU.mult, ALU.mult)
                ins.then_inc(silu_ready, 1)
                dve.wait_ge(sfx, n * 8 + 2)
                tt(SFX[:, :, 0, :], A4[:, :, 1, :], SFX[:, :, 1, :], ALU.mult).then_inc(sfx, 1)
                dve.wait_ge(silu_ready, n * 3 + 3)
                tt(KQte[:, :, 0, :].rearrange("k t (a p) -> k a t p", a=2), KR, BETA, ALU.mult).then_inc(kq_ready, 1)
                dve.wait_ge(sfx, n * 8 + 3)
                tt(ABL, A4[:, :, 0, :], SFX[:, :, 0, :], ALU.mult).then_inc(sfx, 1)
                dve.wait_ge(kq_ready, n + 1)

                def prods(m, j):
                    t = BL * m + j
                    e, hi = 2 * t + 1, 2 * BL * (m + 1)
                    tt(PR[:, OFF[j]:OFF[j] + hi - e, :].rearrange("k i (a p) -> k a i p", a=2), KQ[:, e:hi, :].rearrange("k i (a p) -> k a i p", a=2),
                       KR[:, :, t, :].unsqueeze(2).to_broadcast([128, 2, hi - e, HALF]), ALU.mult).then_inc(prod_ready, 1)

                def mask_piece(m, u):
                    half, a, b = PIECES[m][u]
                    dve.wait_ge(wk_full, n * NWK + WK0[m] + u + 1)
                    tt(GBD[:, half, a - 8:b - 8, :], bank(4 + u % 2)[:, 0:HALF * (b - a)].rearrange("r (i p) -> r i p", p=HALF),
                       maskG[:, :].unsqueeze(1).to_broadcast([128, b - a, HALF]), ALU.mult).then_inc(wk_free, 1)

                for j in range(BL):
                    prods(0, j)
                dve.wait_ge(sfx, n * 8 + 4)
                nc.vector.memset(ASF[:, 3, :], 1.0)
                nc.vector.tensor_copy(ASF[:, 2, :], ABL[:, 3, :]).then_inc(sfx, 1)
                tt(ASF[:, 1, :], ABL[:, 2, :], ABL[:, 3, :], ALU.mult).then_inc(sfx, 1)
                dve.wait_ge(sfx, n * 8 + 6)
                tt(ASF[:, 0, :], ABL[:, 1, :], ASF[:, 1, :], ALU.mult).then_inc(sfx, 1)
                dve.wait_ge(sfx, n * 8 + 7)
                tt(ACH[:, :], ABL[:, 0, :], ASF[:, 0, :], ALU.mult).then_inc(sfx, 1)
                dve.wait_ge(x_ready, n * 4 + 4)
                for m in range(NB):
                    hi = 2 * BL * (m + 1)
                    for j in range(BL):
                        t = BL * m + j
                        e = 2 * t + 1
                        if j > 0:
                            dve.wait_ge(x_step, n * C + t)
                        tt(W[:, :, t, :], BV[:, t, :].rearrange("v (a p) -> v a p", a=2), X[:, 2 * t, :].rearrange("v (a p) -> v a p", a=2), ALU.subtract).then_inc(w_ready, 1)
                        tt(X[:, e:hi, :], X[:, e:hi, :], A[:, t, :].unsqueeze(1).to_broadcast([128, hi - e, NP]), ALU.mult).then_inc(x_decayed, 1)
                        if m < NB - 1:
                            for u in range(NPIECE[m]):
                                if u == j or (u > j and j == BL - 1):
                                    mask_piece(m, u)
                        if j == 0:
                            dve.wait_ge(bcast_psum, n * 8 + 2 * m + 2)
                        dve.wait_ge(w_ready, n * C + t + 1)
                        g = PS[:, 1024:2048].rearrange("v (a i p) -> v a i p", a=2, p=HALF)[:, :, OFF[j]:OFF[j] + hi - e, :]
                        wb = W[:, :, t, :].unsqueeze(2).to_broadcast([128, 2, hi - e, HALF])
                        tt(TT[:, :, 0:hi - e, :], g, wb, ALU.mult).then_inc(wg_ready, 1)
                        if m < NB - 1:
                            prods(m + 1, j)
                        dve.wait_ge(wg_ready, n * C + t + 1)
                        dve.wait_ge(x_decayed, n * C + t + 1)
                        xs = X[:, e:hi, :].rearrange("v i (a p) -> v a i p", a=2)
                        tt(xs, xs, TT[:, :, 0:hi - e, :], ALU.add).then_inc(x_step, 1)
                    wl = W[:, :, BL * m:BL * m + 3, :]
                    tt(wl, wl, SFX[:, m, :, :].rearrange("v j (a p) -> v a j p", a=2), ALU.mult).then_inc(what_ready, 1)
                    if m < NB - 1:
                        tt(X[:, hi:NI, :], X[:, hi:NI, :], ABL[:, m, :].unsqueeze(1).to_broadcast([128, NI - hi, NP]), ALU.mult).then_inc(x_blk, 1)
                        dve.wait_ge(x_blk, n * 3 + m + 1)
                        for u, (half, a, b) in enumerate(PIECES[m]):
                            k = WK0[m] + NPIECE[m] + u
                            dve.wait_ge(wk_full, n * NWK + k + 1)
                            xs = X[:, a:b, HALF * half:HALF * (half + 1)]
                            tt(xs, xs, bank(4 + k % 2)[:, 0:HALF * (b - a)].rearrange("v (i p) -> v i p", p=HALF), ALU.add).then_inc(wk_free, 1)
                        dve.wait_ge(wk_free, n * NWK + WK0[m + 1] if m < NB - 2 else n * NWK + NWK)
                dve.wait_ge(what_ready, n * NB + NB)
                for a in range(2):
                    ps = slice(HALF * a, HALF * (a + 1))
                    tt(PP[:, ps, :].rearrange("v p (m j) -> v m j p", j=BL), W[:, a, :, :].rearrange("v (m j) p -> v m j p", j=BL),
                       ASF[:, :, ps].unsqueeze(2).to_broadcast([128, NB, BL, HALF]), ALU.mult).then_inc(p_ready, 1)
                dve.wait_ge(mean_psum, n + 1)
                nc.vector.scalar_tensor_tensor(DD.rearrange("v (t p) -> v t p", p=NP), PS[:, 3072:4096].rearrange("v (t p) -> v t p", p=NP),
                                               -1.0 / DH, Xo, ALU.mult, ALU.add).then_inc(centred, 1)

                def update(u):
                    for r in range(4):
                        dve.wait_ge(up_psum, n * 16 + 4 * u + r + 1)
                        dve.wait_ge(s_scaled, n * NP + 16 * (u + 1))
                        sv = S.rearrange("v (u a r e) k -> v u r a e k", u=4, a=2, r=4)[:, u, r]
                        sv = sv.rearrange("v a e k -> v a (e k)")
                        tt(sv, sv, bank(2 + r).rearrange("v (a x) -> v a x", a=2), ALU.add).then_inc(s_updated, 1)

                update(0)
                dve.wait_ge(std, n + 1)
                nc.vector.reciprocal(RS, RS).then_inc(rstd, 1)
                dve.wait_ge(rstd, n + 1)
                tt(DD, DD, RS, ALU.mult).then_inc(normed, 1)
                update(1)
                dve.wait_ge(affine, n + 1)
                dve.wait_ge(proj_free, n * NPR + NPR + 2)
                tt(DD, DD, BVf, ALU.mult).then_inc(gated, 1)
                update(2)
                update(3)
                dve.wait_ge(yt_psum, n + 1)
                dve.wait_ge(res_in, n * 32 + 32)
                dve.wait_ge(out_stored, n * 32 + 32)
                tt(OUTT[:, :], bank(7, 128), RES[:, :], ALU.add).then_inc(fin, 1)

        @block.tensor
        def _(pe):
            mm = nc.tensor.matmul
            pe.wait_ge(consts, 7)
            for c in range(4):
                pe.wait_ge(xn_ready, c + 1)
                for k in range(2):
                    for i in range(4):
                        ins = nc.tensor.transpose(bank(2 * c + k)[:, 128 * i:128 * (i + 1)], XN[:, 4 * c + i, 128 * k:128 * (k + 1)], ident[:, :])
                    ins.then_inc(xnT_psum, 1)
            pe.wait_ge(ld_small, 16)
            pe.wait_ge(xnT_ready, 8)
            for i in range(NX):
                for k in range(2):
                    ins = mm(bank(0)[:, E * i:E * (i + 1)], XNT[:, k, HALO + 128 * i:HALO + 128 * (i + 1)], WR[:, k, :], start=(k == 0), stop=(k == 1))
            ins.then_inc(logits, 1)
            pe.wait_ge(rt_step, 15)
            for i in range(NX):
                ins = nc.tensor.transpose(bank(1 + i // 4)[0:LR, 128 * (i % 4):128 * (i % 4 + 1)], WEXP[:, i, :], ident[:, :])
                if i % 4 == 3:
                    ins.then_inc(wT_psum, 1)
            pe.wait_ge(ld_ffn, 16 * 11)
            pe.wait_ge(wT_ready, 4)
            with pe.Fori(0, NCH) as c:
                xs = [XNT[:, k, bass.ds(c * CH + HALO, CH)] for k in range(2)]
                for j, a in enumerate((AG, AU)):
                    pe.wait_ge(had_ready, c + 1)
                    for k in range(2):
                        ins = mm(bank(4 + j)[0:LR, :], a[:, k, :], xs[k], start=(k == 0), stop=(k == 1))
                    ins.then_inc(xa_psum, 1)
                for f in range(NF):
                    if f >= 2:
                        pe.wait_ge(hid_ready, c * NF + f - 1)
                    fs = slice(FW * f, FW * f + FT[f])
                    for j, (w, b, xa) in enumerate(((WG, BG, XAG), (WU, BU, XAU))):
                        o = bank(2 * (f % 2) + j)[0:FT[f], :]
                        for k in range(2):
                            mm(o, w[:, k, fs], xs[k], start=(k == 0), stop=False)
                        if f == 0:
                            pe.wait_ge(xa_ready, c * 2 + j + 1)
                        ins = mm(o, b[0:LR, fs], xa[0:LR, :], start=False, stop=True)
                    ins.then_inc(gu_psum, 1)
                for f in range(NF):
                    pe.wait_ge(hid_ready, c * NF + f + 1)
                    ins = mm(bank(5)[0:LR, :], AD[0:FT[f], f, :], HID[0:FT[f], f, :], start=(f == 0), stop=(f == NF - 1))
                ins.then_inc(had_psum, 1)
                for q in range(4):
                    if q >= 2:
                        pe.wait_ge(base_ready, c * 4 + q - 1)
                    for f in range(NF):
                        mm(bank(6 + q % 2, D), HID[0:FT[f], f, 128 * q:128 * (q + 1)], WD[0:FT[f], f, :], start=(f == 0), stop=False)
                    if q == 0:
                        pe.wait_ge(had_ready, c + 2)
                    mm(bank(6 + q % 2, D), HAD[0:LR, 128 * q:128 * (q + 1)], BD[0:LR, :], start=False, stop=True).then_inc(ffn_psum, 1)
            pe.wait_ge(base_ready, NX)
            pe.wait_ge(ld_attn, 16 * 6)
            pe.wait_ge(masks, 2)
            nc.tensor.nop().then_inc(proj_full, 1)
            with pe.Fori(0, NSUP) as n:
                def project(kinds):
                    for g, (kind, i) in enumerate(PROJ):
                        if kind not in kinds:
                            continue
                        pe.wait_ge(proj_free, n * NPR + g + 1)
                        nh, cols = (4, HALO + TOK) if kind in "qvk" else (8, TOK)
                        for h in range(nh):
                            hh = nh * i + h
                            for k in range(2):
                                if kind == "b":
                                    w = WB[:, k, hh:hh + 1].to_broadcast([128, 128])
                                else:
                                    w = W5[:, WSLOT[kind], k, DH * hh:DH * (hh + 1)]
                                ins = mm(bank(g % 2)[:, cols * h:cols * (h + 1)], w, XC[:, k, HALO + TOK - cols:], start=(k == 0), stop=(k == 1))
                        ins.then_inc(proj_full, 1)

                pe.wait_ge(xc_in, n * 16 + 16)
                project("qvbka")
                pe.wait_ge(s_updated, n * 16 + 1)
                pe.wait_ge(fin, n + 1)

                def transposed_state(j):
                    if j >= 2:
                        pe.wait_ge(st_ready, n * 16 + j - 1)
                    for q in range(4):
                        ins = nc.tensor.transpose(bank(6 + j % 2)[:, DH * q:DH * (q + 1)], S[:, 4 * j + q, :], ident[:, :])
                    ins.then_inc(st_psum, 1)

                def read_out(j):
                    pe.wait_ge(st_ready, n * 16 + j + 1)
                    if j == 0:
                        pe.wait_ge(kq_ready, n + 1)
                        pe.wait_ge(silu_ready, n * 3 + 3)
                    if j % 4 == 0 and j >= 8:
                        pe.wait_ge(x_ready, n * 4 + j // 4 - 1)
                    o = bank(4 + (j // 4) % 2).rearrange("v (i p) -> v i p", p=16)
                    for q in range(4):
                        ins = mm(o[:, :, 4 * (j % 4) + q], STR[:, j % 2, q, :], KQ[:, :, 4 * j + q], start=True, stop=True)
                    ins.then_inc(ro_psum, 1)

                def broadcast_products(m):
                    pe.wait_ge(prod_ready, n * C + BL * (m + 1))
                    if m > 0:
                        pe.wait_ge(wg_ready, n * C + BL * m)
                    for a in range(2):
                        mm(bank(2 + a).rearrange("v (i p) -> v i p", p=HALF), ones[:, :], PR[:, :, HALF * a:HALF * (a + 1)], start=True, stop=True).then_inc(bcast_psum, 1)

                def key_products(m):
                    for u, (half, a, b) in enumerate(PIECES[m]):
                        k = WK0[m] + u
                        if k < 2:
                            pe.wait_ge(x_ready, n * 4 + 4)
                        else:
                            pe.wait_ge(wk_free, n * NWK + k - 1)
                        ps = slice(HALF * half, HALF * (half + 1))
                        mm(bank(4 + k % 2)[:, 0:HALF * (b - a)].rearrange("r (i p) -> r i p", p=HALF), KR[:, half, BL * m:BL * (m + 1), :].rearrange("k t p -> k (t p)"), KQ[:, a:b, ps],
                           start=True, stop=True).then_inc(wk_full, 1)

                def hand_over(m):
                    pe.wait_ge(what_ready, n * NB + m + 1)
                    for a in range(2):
                        ins = nc.tensor.transpose(bank(6)[:, 128 * a:128 * (a + 1)], W[:, a, BL * m:BL * (m + 1), :].rearrange("v t p -> v (t p)"), ident[:, :])
                    ins.then_inc(wht_psum, 1)
                    pe.wait_ge(wht_ready, n * 3 + m + 1)
                    for u, (half, a, b) in enumerate(PIECES[m]):
                        k = WK0[m] + NPIECE[m] + u
                        pe.wait_ge(wk_free, n * NWK + k - 1)
                        mm(bank(4 + k % 2)[:, 0:HALF * (b - a)].rearrange("r (i p) -> r i p", p=HALF), WHT[:, 128 * half:128 * (half + 1)], GBD[:, half, a - 8:b - 8, :],
                           start=True, stop=True).then_inc(wk_full, 1)

                transposed_state(0)
                transposed_state(1)
                for j in range(16):
                    read_out(j)
                    if j + 2 < 16:
                        transposed_state(j + 2)
                broadcast_products(0)
                key_products(0)
                for m in range(NB - 1):
                    hand_over(m)
                    if m == 0:
                        project("g")
                    broadcast_products(m + 1)
                    if m < NB - 2:
                        key_products(m + 1)
                pe.wait_ge(wk_free, n * NWK + NWK)
                pe.wait_ge(kp_ready, n + 1)
                for s in range(8):
                    ins = nc.tensor.transpose(PS[:, 2048 + 128 * s:2048 + 128 * (s + 1)], KP[:, 8 * s:8 * s + 8, :].rearrange("k q t -> k (q t)"), ident[:, :])
                ins.then_inc(kt_psum, 1)
                pe.wait_ge(x_step, n * C + C)
                for i in range(2):
                    ins = mm(bank(6 + i).rearrange("v (t p) -> v t p", p=NP), ones[:, :], Xo[:, 8 * i:8 * i + 8, :], start=True, stop=True)
                ins.then_inc(mean_psum, 1)
                pe.wait_ge(p_ready, n * 2 + 2)
                for s in range(8):
                    ins = nc.tensor.transpose(bank(2 + s // 4)[:, 128 * (s % 4):128 * (s % 4 + 1)], PP[:, 8 * s:8 * s + 8, :].rearrange("v q t -> v (q t)"), ident[:, :])
                    if s % 4 == 3:
                        ins.then_inc(pt_psum, 1)
                pe.wait_ge(kt_ready, n + 1)

                def update(u):
                    for a in range(2):
                        s = 2 * u + a
                        for r in range(4):
                            if a == 0 and u > 0:
                                pe.wait_ge(s_updated, n * 16 + 4 * (u - 1) + r + 2)
                            if s % 4 == 0 and r == 0:
                                pe.wait_ge(pt_ready, n * 2 + 2)
                            ins = mm(bank(2 + r)[:, 256 * a:256 * (a + 1)], PT[32 * r:32 * r + 32, s, :],
                                     KTB[32 * r:32 * r + 32, s, :, :].rearrange("r e k -> r (e k)"), start=True, stop=True)
                            if a == 1:
                                ins.then_inc(up_psum, 1)

                update(0)
                pe.wait_ge(squared, n + 1)
                for i in range(2):
                    ins = mm(bank(6 + i), ones[:, :], RS[:, 512 * i:512 * (i + 1)], start=True, stop=True)
                ins.then_inc(var_psum, 1)
                update(1)
                update(2)
                update(3)
                pe.wait_ge(gated, n + 1)
                for dh in range(2):
                    for h in range(H):
                        ins = mm(bank(6)[:, TOK * dh:TOK * (dh + 1)], WO[:, h, 128 * dh:128 * (dh + 1)],
                                 DD.rearrange("v (n h) -> v n h", h=H)[:, :, h], start=(h == 0), stop=(h == H - 1))
                ins.then_inc(y_psum, 1)
                pe.wait_ge(y_ready, n + 1)
                nc.tensor.transpose(bank(7, 128), YT.rearrange("d c t -> d (c t)"), ident[:, :]).then_inc(yt_psum, 1)


def kernel(**inputs):
    import numpy as np
    import concourse.bacc as bacc
    from concourse.bass_utils import run_bass_kernel_spmd

    a = {k: np.asarray(v) for k, v in inputs.items()}

    def attn(k):
        return a["L0_attn_" + k]

    def ffn(k):
        return a["L0_ffn_" + k]

    def per_head(v):
        return np.moveaxis(v.reshape(H, DH, -1), 0, -1).reshape(DH, -1)

    def two_tiles(v):
        return v.reshape(2, 128, -1).transpose(1, 0, 2).reshape(128, -1)

    def rows(v):
        return np.broadcast_to(v[None, :], (128, v.shape[0]))

    def lora_a(experts, shared):
        return np.concatenate([experts.transpose(1, 0, 2).reshape(shared.shape[0], -1), shared], axis=1)

    def lora_b(experts, shared):
        return np.concatenate([experts.reshape(-1, shared.shape[1]), shared], axis=0)

    small = np.concatenate(
        [per_head(attn(f"conv_{t}_w").reshape(H * DH, KC)) for t in "qkv"]
        + [per_head(attn(f"conv_{t}_b")) for t in "qkv"]
        + [per_head(attn("ba")), rows(attn("bb")), attn("ln_g")[:, None], attn("ln_b")[:, None],
           two_tiles(attn("Wb").T), rows(ffn("expert_bias")), two_tiles(ffn("W_router"))], axis=1)
    arrays = {
        "x_tm": attn("x").transpose(1, 0, 2).reshape(NT, D),
        "wqT": attn("Wq").T, "wkT": attn("Wk").T, "wvT": attn("Wv").T, "waT": attn("Wa").T,
        "wgT": attn("Wg").T, "woT": attn("Wo").T, "small": small,
        "w_gate": ffn("W_gate"), "w_up": ffn("W_up"), "w_down": ffn("W_down"),
        "a_gate": lora_a(ffn("A_gate"), ffn("sA_gate")), "b_gate": lora_b(ffn("B_gate"), ffn("sB_gate")),
        "a_up": lora_a(ffn("A_up"), ffn("sA_up")), "b_up": lora_b(ffn("B_up"), ffn("sB_up")),
        "a_down": lora_a(ffn("A_down"), ffn("sA_down")), "b_down": lora_b(ffn("B_down"), ffn("sB_down")),
    }
    arrays = {k: np.ascontiguousarray(v) for k, v in arrays.items()}
    nc = bacc.Bacc("TRN2", target_bir_lowering=False, num_devices=1)
    args = [nc.dram_tensor(k, v.shape, mybir.dt.from_np(v.dtype), kind="ExternalInput").ap() for k, v in arrays.items()]
    args.append(nc.dram_tensor("out", (NT, D), F32, kind="ExternalOutput").ap())
    build(nc, *args)
    r = run_bass_kernel_spmd(nc, [arrays], core_ids=[0])
    y = r.results[0]["out"]
    return y.reshape(T, B, D).transpose(1, 0, 2)
```

```python
from contextlib import ExitStack

import concourse.bass as bass
from concourse import mybir

F32 = mybir.dt.float32
ALU = mybir.AluOpType
ACT = mybir.ActivationFunctionType
AX = mybir.AxisListType

B, T, D, H, DH = 4, 512, 256, 16, 128
NP = B * H
NT = B * T
KC = 4
E, R, DFF = 8, 8, 688
C = 16
BL = 4
NB = C // BL
NSUP = T // C
HALO = (KC - 1) * B
NI = 2 * C
LR = E * R + R
NF = (DFF + 127) // 128
FW = (DFF + NF - 1) // NF
FT = [min(FW, DFF - FW * f) for f in range(NF)]
NX = NT // 128
CH = 512
NCH = NT // CH
OFF = [0, 7, 12, 15]
K_SCALE = float(DH) ** -0.5
HALF = NP // 2
PC = 256
NPC = NT // PC
PT_ = PC // B
PSC = PT_ // C
OSC = CH // B // C

CW0, CB0 = 0, 3 * KC * H
BA0 = CB0 + 3 * H
BB0 = BA0 + H
LN0 = BB0 + H
WB0 = LN0 + 2
EB0 = WB0 + 2 * H
WR0 = EB0 + E
NSMALL = WR0 + 2 * E

PIECES = []
for m in range(NB - 1):
    lo = 2 * BL * (m + 1)
    cuts = [(i, min(i + 16, NI)) for i in range(lo, NI, 16)]
    PIECES.append([(half, a, b) for half in range(2) for a, b in cuts])
NPIECE = [len(x) for x in PIECES]
NXP = 4
NWK = 2 * sum(NPIECE) + 2 * NXP
WK0 = [2 * sum(NPIECE[:m]) for m in range(NB)]

NR = 16
SLOTS = [list(range(0, 5)), list(range(5, 10)), list(range(10, 14)), list(range(14, 18))]
ADD_AT = {5: [(0, 1), (1, 0), (1, 1), (2, 1), (3, 0)], 4: [(0, 1), (1, 1), (2, 1), (3, 0)]}

JOBS = ([("b", 2 * i, 2) for i in range(H // 2)] + [(x, i, 1) for x in "qkv" for i in range(H)]
        + [("a", 2 * i, 2) for i in range(H // 2)])
NJ = len(JOBS)
WSLOT = {"q": 0, "k": 1, "v": 2, "a": 3}
NQ = 3 * H // 4
CONV_JOB0 = H // 2
TAPS = KC - 1


def build(nc, x_tm, wqT, wkT, wvT, waT, wgT, woT, small, w_gate, w_up, w_down, a_gate, b_gate,
          a_up, b_up, a_down, b_down, out):
    def dram(name, shape):
        return nc.dram_tensor(name, shape, F32, kind="Internal").ap()

    base_d = dram("base_d", (NT, D))
    kq_d = dram("kq_d", (NSUP, 128, NI * NP))
    kr_d = dram("kr_d", (NSUP, 128, C * NP))
    bv_d = dram("bv_d", (NSUP, 128, C * NP))
    a_d = dram("a_d", (NSUP, 128, C * NP))
    o_d = dram("o_d", (NSUP, 128, C * NP))

    with ExitStack() as ctx:
        def sb(name, shape):
            return ctx.enter_context(nc.sbuf_tensor(name, shape, F32))

        def sem(name):
            return ctx.enter_context(nc.semaphore(name))

        XNT = sb("XNT", [128, 2, HALO + NT])
        SM = sb("SM", [128, NSMALL])
        ident = sb("ident", [128, 128])
        ones = sb("ones", [128, 128])
        maskG = sb("maskG", [128, HALF])
        maskKT = sb("maskKT", [128, 2])
        mask8 = sb("mask8", [128, 8])
        eps = sb("eps", [128, 1])
        NARENA = 48256
        arena = sb("arena", [128, NARENA])
        CW = SM[:, CW0:CW0 + 3 * KC * H].rearrange("p (x i h) -> p x i h", x=3, i=KC)
        CB = SM[:, CB0:CB0 + 3 * H].rearrange("p (x h) -> p x h", x=3)
        BA = SM[:, BA0:BA0 + H]
        BB = SM[:, BB0:BB0 + H]
        LNG, LNB = SM[:, LN0:LN0 + 1], SM[:, LN0 + 1:LN0 + 2]
        WB = SM[:, WB0:WB0 + 2 * H].rearrange("p (c h) -> p c h", c=2)
        EB = SM[:, EB0:EB0 + E]
        WR = SM[:, WR0:WR0 + 2 * E].rearrange("p (c e) -> p c e", c=2)

        pos = [0]

        def take(n):
            pos[0] += n
            assert pos[0] <= NARENA
            return arena[:, pos[0] - n:pos[0]]

        W4 = take(4 * 2 * H * DH).rearrange("p (x c n) -> p x c n", x=4, c=2)
        after_w4 = pos[0]
        KQST = take(PSC * NI * NP)
        KRST = take(PSC * C * NP)
        BVST = take(PSC * C * NP)
        AST = take(PSC * C * NP)
        BETA = take(PSC * C * NP)
        PRE = take(2 * 4 * (HALO + PC)).rearrange("p (s h n) -> p s h n", s=2, h=4)
        ACC = take(3 * 4 * PC).rearrange("p (s h n) -> p s h n", s=3, h=4)
        SIG = take(2 * 4 * PC).rearrange("p (s h n) -> p s h n", s=2, h=4)

        def by_head(tile, h, nh=1, te=1, e=0):
            v = tile.rearrange("p (t e g b h) -> p e g h t b", e=te, g=2, b=B, h=8)[:, e, h // 8]
            return v[:, h % 8:h % 8 + nh]

        pos[0] = 0
        S = take(NP * DH).rearrange("v (p k) -> v p k", p=NP)
        Sr = S.rearrange("v (u a r e) k -> v u r a e k", u=4, a=2, r=4)
        STR = take(2 * 4 * DH).rearrange("k (s a e v) -> k s a e v", s=2, a=2, e=2)
        Xf = [take(NI * NP) for _ in range(2)]
        X = [x.rearrange("v (i p) -> v i p", p=NP) for x in Xf]
        KQf = [take(NI * NP) for _ in range(2)]
        KQ = [x.rearrange("k (i p) -> k i p", p=NP) for x in KQf]
        KRf = [take(C * NP) for _ in range(2)]
        KR = [x.rearrange("k (a t p) -> k a t p", a=2, p=HALF) for x in KRf]
        BVf = [take(C * NP) for _ in range(2)]
        BV = [x.rearrange("v (t p) -> v t p", p=NP) for x in BVf]
        Af = [take(C * NP) for _ in range(2)]
        A = [x.rearrange("v (t p) -> v t p", p=NP) for x in Af]
        W = take(C * NP).rearrange("v (a t p) -> v a t p", a=2, p=HALF)
        PR = take(16 * NP).rearrange("k (i p) -> k i p", p=NP)
        TT = take(7 * NP).rearrange("v (a i p) -> v a i p", a=2, i=7)
        GBD = take(2 * 24 * HALF).rearrange("r (a i p) -> r a i p", a=2, i=24)
        G2 = take(8 * NI * 8).rearrange("r (s i p) -> r s i p", s=8, p=8)
        KTB = [take(2048).rearrange("r (s e k) -> r s e k", s=8, e=2) for _ in range(2)]
        PP = take(C * NP).rearrange("v (p t) -> v p t", t=C)
        KP = take(C * NP).rearrange("k (p t) -> k p t", t=C)
        PTf = take(8 * DH)
        PT = PTf.rearrange("r (s v) -> r s v", s=8)
        WHT = take(256)
        OT = take(C * NP)
        SFX = [take(NB * 3 * NP).rearrange("v (m j p) -> v m j p", m=NB, j=3) for _ in range(2)]
        ABL = [take(NB * NP).rearrange("v (m p) -> v m p", m=NB) for _ in range(2)]
        ASF = [take(NB * NP).rearrange("v (m p) -> v m p", m=NB) for _ in range(2)]
        ACH = [take(NP) for _ in range(2)]
        WGT = take(2 * H * DH).rearrange("p (c n) -> p c n", c=2)

        wgt_at = pos[0] - 2 * H * DH
        pos[0] = 0
        WO = take(H * D).rearrange("p (h d) -> p h d", h=H)
        OC = take(OSC * C * NP)
        GATE = take(H * CH).rearrange("p (h n) -> p h n", h=H)
        BASEC = take(4 * D).rearrange("p (q d) -> p q d", q=4)
        SQO = take(2 * CH).rearrange("p (s n) -> p s n", s=2)
        STD = take(2 * CH).rearrange("p (s n) -> p s n", s=2)
        RSTD = take(2 * CH).rearrange("p (s n) -> p s n", s=2)
        NRM = take(2 * CH).rearrange("p (s n) -> p s n", s=2)
        AFF = take(2 * CH).rearrange("p (s n) -> p s n", s=2)
        Z = take(2 * CH).rearrange("p (s n) -> p s n", s=2)
        YT = take(2 * CH).rearrange("p (c n) -> p c n", c=2)
        centre = take(128)
        assert pos[0] <= wgt_at

        pos[0] = after_w4
        XIN = take(NX * D).rearrange("p (n d) -> p n d", n=NX)
        XNf = take(NX * D)
        XN = XNf.rearrange("p (n d) -> p n d", n=NX)
        GT = XNf[:, 0:NX * 64].rearrange("p (n a b) -> p n a b", n=NX, a=E)
        EQ = XNf[:, 1024:1024 + NX * 64].rearrange("p (n a b) -> p n a b", n=NX, a=E)
        WEXP = XNf[:, 2048:2048 + NX * LR].rearrange("p (n l) -> p n l", n=NX)
        HID = XNf[:, 0:NF * CH].rearrange("p (f t) -> p f t", f=NF)
        WG = take(2 * DFF).rearrange("p (c f) -> p c f", c=2)
        WU = take(2 * DFF).rearrange("p (c f) -> p c f", c=2)
        WD = take(NF * D).rearrange("p (f d) -> p f d", f=NF)
        BG = take(DFF)
        BU = take(DFF)
        AD = take(NF * LR).rearrange("p (f l) -> p f l", f=NF)
        AG = take(2 * LR).rearrange("p (c l) -> p c l", c=2)
        AU = take(2 * LR).rearrange("p (c l) -> p c l", c=2)
        BD = take(D)
        WT = take(NT)
        XAG = take(CH)
        XAU = take(CH)
        SG = take(2 * CH).rearrange("p (s t) -> p s t", s=2)
        SQ = SG.rearrange("p s t -> p (s t)")
        HAD = take(CH)
        BASE = take(2 * D).rearrange("p (s d) -> p s d", s=2)
        ST8 = take(8 * NX).rearrange("p (k n) -> p k n", k=8)
        SC = take(NX * E).rearrange("p (n e) -> p n e", n=NX)
        BI = take(NX * E).rearrange("p (n e) -> p n e", n=NX)
        RK = take(NX * E).rearrange("p (n e) -> p n e", n=NX)
        tri = take(E * E).rearrange("p (e f) -> p e f", e=E)

        PS = ctx.enter_context(nc.psum_tensor("PS", [128, 8 * 512], F32))

        def bank(i, n=512, k=1):
            return PS[:, 512 * i:512 * i + n * k]

        ld_x = [sem(f"ld_x{c}") for c in range(4)]
        ld_small, ld_ffn, ld_attn = sem("ld_small"), sem("ld_ffn"), sem("ld_attn")
        consts, masks = sem("consts"), sem("masks")
        ln_step, ln_var, ln_std, xn_ready = sem("ln_step"), sem("ln_var"), sem("ln_std"), sem("xn_ready")
        xnT_psum, xnT_ready = sem("xnT_psum"), sem("xnT_ready")
        logits, scores, rt_step = sem("logits"), sem("scores"), sem("rt_step")
        wT_psum, wT_ready = sem("wT_psum"), sem("wT_ready")
        xa_psum, xa_ready = sem("xa_psum"), sem("xa_ready")
        gu_psum, gu_sig, gu_silu, hid_ready = sem("gu_psum"), sem("gu_sig"), sem("gu_silu"), sem("hid_ready")
        had_psum, had_ready = sem("had_psum"), sem("had_ready")
        ffn_psum, base_ready = sem("ffn_psum"), sem("base_ready")
        base_stored = [sem(f"base_stored{i}") for i in range(2)]
        job_full, job_free = sem("job_full"), sem("job_free")
        tap_add, sig_ready, silu_done = sem("tap_add"), sem("sig_ready"), sem("silu_done")
        k_scaled, v_silu, kr_staged = sem("k_scaled"), sem("v_silu"), sem("kr_staged")
        kq_stored, kr_stored, bv_stored, a_stored = sem("kq_stored"), sem("kr_stored"), sem("bv_stored"), sem("a_stored")
        in_ready = [sem(f"in_ready{i}") for i in range(2)]
        zeros, sfx = sem("zeros"), sem("suffix_products")
        up_psum, s_updated, s_scaled = sem("up_psum"), sem("s_updated"), sem("s_scaled")
        st_psum, st_ready, ro_psum, x_ready = sem("st_psum"), sem("st_ready"), sem("ro_psum"), sem("x_ready")
        prod_ready, bcast_psum = sem("prod_ready"), sem("bcast_psum")
        wk_full, wk_free = sem("work_full"), sem("work_free")
        w_ready, x_decayed, wg_ready, x_step = sem("w_ready"), sem("x_decayed"), sem("wg_ready"), sem("x_step")
        what_ready, x_blk = sem("what_ready"), sem("x_block_decayed")
        wht_psum, wht_ready = sem("wht_psum"), sem("wht_ready")
        kp_ready, kt_psum, kt_ready = sem("kp_ready"), sem("kt_psum"), sem("kt_ready")
        p_ready, pt_psum, pt_ready = sem("p_ready"), sem("pt_psum"), sem("pt_ready")
        o_ready, o_stored = sem("o_ready"), sem("o_stored")
        ld_last, oc_in, centre_ready = sem("ld_last"), sem("oc_in"), sem("centre_ready")
        gate_psum, gate_ready = sem("gate_psum"), sem("gate_ready")
        cen_psum, squared, var_psum, std = sem("cen_psum"), sem("squared"), sem("var_psum"), sem("std")
        rstd, normed, affine, gated = sem("rstd"), sem("normed"), sem("affine"), sem("gated")
        y_step, y_ready, yt_psum, fin, out_stored = sem("y_step"), sem("y_ready"), sem("yt_psum"), sem("out_tile"), sem("out_stored")

        block = ctx.enter_context(nc.Block())
        x_v = x_tm.rearrange("(n p) d -> p n d", p=128)

        @block.sync
        def _(sp):
            for c in range(4):
                sp.dma_start(XIN[:, 4 * c:4 * c + 4, :], x_v[:, 4 * c:4 * c + 4, :]).then_inc(ld_x[c], 16)
            n_ffn = 0
            for dst, src in ((WG, w_gate.rearrange("(c p) f -> p c f", p=128)),
                             (WU, w_up.rearrange("(c p) f -> p c f", p=128)),
                             (AG, a_gate.rearrange("(c p) l -> p c l", p=128)),
                             (AU, a_up.rearrange("(c p) l -> p c l", p=128)),
                             (BG[0:LR, :], b_gate), (BU[0:LR, :], b_up), (BD[0:LR, :], b_down),
                             (WD[0:FW, 0:NF - 1, :], w_down[0:FW * (NF - 1), :].rearrange("(f p) d -> p f d", p=FW)),
                             (WD[0:FT[-1], NF - 1, :], w_down[FW * (NF - 1):DFF, :]),
                             (AD[0:FW, 0:NF - 1, :], a_down[0:FW * (NF - 1), :].rearrange("(f p) l -> p f l", p=FW)),
                             (AD[0:FT[-1], NF - 1, :], a_down[FW * (NF - 1):DFF, :])):
                sp.dma_start(dst, src).then_inc(ld_ffn, 16)
                n_ffn += 1
            assert n_ffn == 11
            for i, w in enumerate((wqT, wkT, wvT, waT)):
                sp.dma_start(W4[:, i, :, :], w.rearrange("(c p) n -> p c n", p=128)).then_inc(ld_attn, 16)
            for stored in base_stored + [kq_stored, kr_stored, bv_stored, a_stored, o_stored, out_stored]:
                sp.sem_inc(stored, 16)
            with sp.Fori(0, NCH) as c:
                for q in range(4):
                    sp.wait_ge(base_ready, c * 4 + q + 1)
                    sp.dma_start(base_d[bass.ds(c * CH + 128 * q, 128), :], BASE[:, q % 2, :]).then_inc(base_stored[q % 2], 16)
            with sp.Fori(0, NPC) as c:
                for dst, tile, staged, count, stored in (
                        (kq_d, KQST, silu_done, c * NQ + 2 * NQ // 3 + 3, kq_stored),
                        (kr_d, KRST, kr_staged, c * (NQ // 3) + NQ // 3, kr_stored),
                        (bv_d, BVST, silu_done, c * NQ + NQ + 3, bv_stored),
                        (a_d, AST, job_free, c * NJ + NJ + 8, a_stored)):
                    sp.wait_ge(staged, count)
                    sp.dma_start(dst[bass.ds(c * PSC, PSC)].rearrange("s k x -> k s x"),
                                 tile.rearrange("k (s x) -> k s x", s=PSC)).then_inc(stored, 16)

            def load(n, c):
                for dst, src in ((KQf, kq_d), (KRf, kr_d), (BVf, bv_d), (Af, a_d)):
                    s = src[n] if isinstance(n, int) else src[bass.ds(n, 1)].rearrange("s k x -> k (s x)")
                    sp.dma_start(dst[c], s).then_inc(in_ready[c], 16)

            def store_outputs(n):
                sp.wait_ge(o_ready, n + 2)
                sp.dma_start(o_d[bass.ds(n, 1)].rearrange("s v x -> v (s x)"), OT).then_inc(o_stored, 16)

            for stored in (kq_stored, kr_stored, bv_stored, a_stored):
                sp.wait_ge(stored, 16 * NPC + 16)
            for stored in base_stored:
                sp.wait_ge(stored, 16 * NX // 2 + 16)
            load(0, 0)
            load(1, 1)
            sp.dma_start(WGT, wgT.rearrange("(c p) n -> p c n", p=128)).then_inc(ld_last, 16)
            with sp.Fori(0, NSUP // 2 - 1) as i:
                for c in range(2):
                    n = i * 2 + c
                    sp.wait_ge(x_step, n * C + C)
                    load(n + 2, c)
                    store_outputs(n)
            sp.wait_ge(x_step, (NSUP - 1) * C)
            load(0, 0)
            for c in range(2):
                sp.wait_ge(o_ready, NSUP - 2 + c + 2)
                sp.dma_start(o_d[NSUP - 2 + c], OT).then_inc(o_stored, 16)
            sp.wait_ge(o_stored, 16 * NSUP + 16)
            sp.wait_ge(wk_free, NWK * NSUP)
            sp.wait_ge(wk_full, NWK * NSUP + 2)
            sp.dma_start(WO, woT.rearrange("(h p) d -> p h d", p=128)).then_inc(ld_last, 16)
            with sp.Fori(0, NCH) as c:
                sp.dma_start(OC.rearrange("v (s x) -> v s x", s=OSC), o_d[bass.ds(c * OSC, OSC)].rearrange("s v x -> v s x")).then_inc(oc_in, 16)
                sp.wait_ge(out_stored, c * 64 + 16)
                sp.dma_start(BASEC[:, :, :], base_d[bass.ds(c * CH, CH), :].rearrange("(q p) d -> p q d", p=128)).then_inc(oc_in, 16)
                for q in range(4):
                    sp.wait_ge(fin, c * 4 + q + 2)
                    sp.dma_start(out[bass.ds(c * CH + 128 * q, 128), :], BASEC[:, q, :]).then_inc(out_stored, 16)
            sp.wait_ge(out_stored, NCH * 64 + 16)

        @block.gpsimd
        def _(pool):
            pool.dma_start(SM[:, :], small).then_inc(ld_small, 16)
            nc.gpsimd.memset(ident[:, :], 0.0).then_inc(consts, 1)
            nc.gpsimd.memset(tri[:, :, :], 1.0).then_inc(consts, 1)
            nc.gpsimd.memset(ones[:, :], 1.0).then_inc(consts, 1)
            nc.gpsimd.memset(eps[:, :], 1e-5).then_inc(consts, 1)
            nc.gpsimd.memset(XNT[:, :, 0:HALO], 0.0).then_inc(consts, 1)
            pool.wait_ge(consts, 5)
            nc.gpsimd.affine_select(out=ident[:, :], in_=ident[:, :], compare_op=ALU.not_equal, fill=1.0,
                                    base=0, pattern=[[-1, 128]], channel_multiplier=1).then_inc(consts, 1)
            nc.gpsimd.affine_select(out=tri[:, :, :], in_=tri[:, :, :], compare_op=ALU.is_gt, fill=0.0,
                                    base=0, pattern=[[1, E], [-1, E]], channel_multiplier=0).then_inc(consts, 1)

        @block.scalar
        def _(act):
            act.wait_ge(consts, 4)
            for c in range(4):
                act.wait_ge(ln_var, c + 1)
                nc.scalar.activation(ST8[:, 2, 4 * c:4 * c + 4], ST8[:, 1, 4 * c:4 * c + 4], ACT.Sqrt,
                                     bias=eps[:, 0:1], scale=1.0 / D).then_inc(ln_std, 1)
                if c > 0:
                    for k in range(2):
                        act.wait_ge(xnT_psum, 2 * (c - 1) + k + 1)
                        nc.scalar.copy(XNT[:, k, HALO + CH * (c - 1):HALO + CH * c], bank(2 * (c - 1) + k)).then_inc(xnT_ready, 1)
            for k in range(2):
                act.wait_ge(xnT_psum, 6 + k + 1)
                nc.scalar.copy(XNT[:, k, HALO + CH * 3:HALO + CH * 4], bank(6 + k)).then_inc(xnT_ready, 1)
            act.wait_ge(logits, 1)
            nc.scalar.activation(SC[:, :, :], bank(0, 128).rearrange("p (n e) -> p n e", n=NX), ACT.Sigmoid).then_inc(scores, 1)
            for i in range(4):
                act.wait_ge(wT_psum, i + 1)
                nc.scalar.copy(WT[0:LR, CH * i:CH * (i + 1)], bank(1 + i)[0:LR, :]).then_inc(wT_ready, 1)
            with act.Fori(0, NCH) as c:
                for f in range(NF):
                    act.wait_ge(gu_psum, c * NF + f + 1)
                    if f >= 2:
                        act.wait_ge(hid_ready, c * NF + f - 1)
                    nc.scalar.activation(SG[0:FT[f], f % 2, :], bank(2 * (f % 2))[0:FT[f], :], ACT.Sigmoid).then_inc(gu_sig, 1)
            for stored in base_stored:
                act.wait_ge(stored, 16 * NX // 2 + 16)
            for _ in range(8):
                nc.scalar.nop().then_inc(job_free, 1)
            with act.Fori(0, NPC) as c:
                def job(g):
                    kind, h0, nh = JOBS[g]
                    act.wait_ge(job_full, c * NJ + g + 1)
                    bk = bank(g % 8)
                    if kind in "ab":
                        dst, bias = (BETA, BB) if kind == "b" else (AST, BA)
                        for k in range(nh):
                            ins = nc.scalar.activation(by_head(dst, h0 + k)[:, 0], bk[:, PC * k:PC * (k + 1)].rearrange("p (t b) -> p t b", b=B),
                                                       ACT.Sigmoid, bias=bias[:, h0 + k:h0 + k + 1])
                        ins.then_inc(job_free, 1)
                    else:
                        x, h = divmod(g - CONV_JOB0, 4)
                        nc.scalar.copy(PRE[:, x % 2, h, :], bk[:, 0:HALO + PC])
                        w = "qkv".index(kind)
                        nc.scalar.activation(ACC[:, x % 3, h, :], bk[:, HALO:HALO + PC], ACT.Identity, bias=CB[:, w, h0:h0 + 1],
                                             scale=CW[:, w, KC - 1, h0:h0 + 1]).then_inc(job_free, 1)

                def sigmoid(x):
                    act.wait_ge(tap_add, (c * NQ + x + 1) * (4 * TAPS))
                    nc.scalar.activation(SIG[:, x % 2], ACC[:, x % 3], ACT.Sigmoid).then_inc(sig_ready, 1)

                def stage_keys(x):
                    act.wait_ge(k_scaled, c * (NQ // 3) + x - NQ // 3 + 1)
                    if x == NQ // 3:
                        act.wait_ge(kr_stored, c * 16 + 16)
                    for h in range(4):
                        hh = 4 * (x - NQ // 3) + h
                        ins = nc.scalar.copy(KRST.rearrange("k (s g t b h) -> k g h s t b", s=PSC, g=2, b=B, h=8)[:, hh // 8, hh % 8],
                                             ACC[:, x % 3, h, :].rearrange("k (s t b) -> k s t b", s=PSC, b=B))
                    ins.then_inc(kr_staged, 1)

                act.wait_ge(silu_done, c * NQ + 3)
                for g in range(CONV_JOB0):
                    job(g)
                for x in range(NQ):
                    act.wait_ge(silu_done, c * NQ + x + 1)
                    if NQ // 3 <= x - 3 < 2 * NQ // 3:
                        act.wait_ge(kr_staged, c * (NQ // 3) + x - 3 - NQ // 3 + 1)
                    for h in range(4):
                        job(CONV_JOB0 + 4 * x + h)
                    if x > 0:
                        sigmoid(x - 1)
                    if NQ // 3 <= x - 2 < 2 * NQ // 3:
                        stage_keys(x - 2)
                act.wait_ge(a_stored, c * 16 + 16)
                for g in range(CONV_JOB0 + 4 * NQ, NJ):
                    job(g)
                    if g == CONV_JOB0 + 4 * NQ + 2:
                        sigmoid(NQ - 1)
            act.wait_ge(zeros, 6)
            nc.scalar.nop().then_inc(o_ready, 1)
            with act.Fori(0, NSUP // 2) as i:
                for c in range(2):
                    n = i * 2 + c
                    d = 1 - c

                    def slot(k):
                        if k < NR:
                            u, r = divmod(k, 4)
                            act.wait_ge(s_updated, n * NR + k + 1)
                            for a in range(2):
                                for e in range(2):
                                    p = 16 * u + 8 * a + 2 * r + e
                                    ins = nc.scalar.mul(S[:, p, :], S[:, p, :], ACH[c][:, p:p + 1])
                            ins.then_inc(s_scaled, 1)
                        j = k - 1
                        if 0 <= j < NR:
                            act.wait_ge(st_psum, n * NR + j + 1)
                            if j >= 2:
                                act.wait_ge(ro_psum, n * NR + j - 1)
                            nc.scalar.copy(STR[:, j % 2], bank(6).rearrange("k (a e v) -> k a e v", a=2, e=2)).then_inc(st_ready, 1)
                        j = k - 2
                        if 0 <= j < NR:
                            u, r = divmod(j, 4)
                            act.wait_ge(ro_psum, n * NR + j + 1)
                            for e in range(2):
                                ins = nc.scalar.copy(X[d].rearrange("v i (u a r e) -> v u r e a i", u=4, a=2, r=4)[:, u, r, e],
                                                     bank(5).rearrange("v (a e i q) -> v e q a i", a=2, e=2, q=4)[:, e, 2 * (r % 2) + e])
                            ins.then_inc(x_ready, 1)

                    act.wait_ge(in_ready[c], i * 64 + 64)
                    nc.scalar.copy(KP.rearrange("k (a p) t -> k a t p", a=2), KR[c]).then_inc(kp_ready, 1)
                    act.wait_ge(o_ready, n + 1)
                    for m in range(NB):
                        for k in SLOTS[m]:
                            slot(k)
                        if m < NB - 1:
                            act.wait_ge(wht_psum, n * 3 + m + 1)
                            nc.scalar.copy(WHT, bank(0, 256)).then_inc(wht_ready, 1)
                        if m < 2:
                            act.wait_ge(kt_psum, n * 2 + m + 1)
                            for s in range(4):
                                for e in range(2):
                                    ins = nc.scalar.mul(KTB[c][:, 4 * m + s, e, :], bank(0)[:, DH * s:DH * (s + 1)], maskKT[:, e:e + 1])
                            ins.then_inc(kt_ready, 1)
                    for k in range(2):
                        act.wait_ge(pt_psum, n * 2 + k + 1)
                        nc.scalar.copy(PT[:, 4 * k:4 * k + 4, :], bank(7 * k).rearrange("r (s v) -> r s v", s=4)).then_inc(pt_ready, 1)
                    act.wait_ge(x_step, n * C + C)
                    act.wait_ge(o_stored, n * 16 + 16)
                    nc.scalar.copy(OT.rearrange("v (t p) -> v t p", p=NP), X[c].rearrange("v (t e) p -> v e t p", e=2)[:, 1]).then_inc(o_ready, 1)
            with act.Fori(0, NCH) as c:
                for h in range(H):
                    act.wait_ge(gate_psum, c * H + h + 1)
                    nc.scalar.activation(GATE[:, h, :], bank(h % 4), ACT.Sigmoid).then_inc(gate_ready, 1)
                for h in range(H + 2):
                    if h < H:
                        act.wait_ge(cen_psum, c * H + h + 1)
                        nc.scalar.activation(SQO[:, h % 2, :], bank(h % 4), ACT.Square).then_inc(squared, 1)
                    if 0 <= h - 1 < H:
                        act.wait_ge(var_psum, c * H + h)
                        nc.scalar.activation(STD[:, (h - 1) % 2, :], bank(4 + (h - 1) % 2), ACT.Sqrt, bias=eps[:, 0:1], scale=1.0 / DH).then_inc(std, 1)
                    if 0 <= h - 2:
                        act.wait_ge(normed, c * H + h - 1)
                        nc.scalar.activation(AFF[:, h % 2, :], NRM[:, h % 2, :], ACT.Identity, bias=LNB, scale=LNG).then_inc(affine, 1)
                act.wait_ge(y_step, c * H + H)
                for dh in range(2):
                    nc.scalar.copy(YT[:, dh, :], bank(6 + dh)).then_inc(y_ready, 1)

        @block.vector
        def _(dve):
            tt = nc.vector.tensor_tensor
            for c in range(4):
                cs = slice(4 * c, 4 * c + 4)
                dve.wait_ge(ld_x[c], 16)
                nc.vector.tensor_reduce(ST8[:, 0, cs], XIN[:, cs, :], AX.X, ALU.add).then_inc(ln_step, 1)
                dve.wait_ge(ln_step, 5 * c + 1)
                nc.vector.tensor_scalar(ST8[:, 3, cs], ST8[:, 0, cs], -1.0 / D, None, ALU.mult).then_inc(ln_step, 1)
                dve.wait_ge(ln_step, 5 * c + 2)
                tt(XN[:, cs, :], XIN[:, cs, :], ST8[:, 3, cs].unsqueeze(2).to_broadcast([128, 4, D]), ALU.add).then_inc(ln_step, 1)
                dve.wait_ge(ln_step, 5 * c + 3)
                tt(SQ.rearrange("p (n d) -> p n d", n=4), XN[:, cs, :], XN[:, cs, :], ALU.mult).then_inc(ln_step, 1)
                dve.wait_ge(ln_step, 5 * c + 4)
                nc.vector.tensor_reduce(ST8[:, 1, cs], SQ.rearrange("p (n d) -> p n d", n=4), AX.X, ALU.add).then_inc(ln_var, 1)
                dve.wait_ge(ln_std, c + 1)
                nc.vector.reciprocal(ST8[:, 4, cs], ST8[:, 2, cs]).then_inc(ln_step, 1)
                dve.wait_ge(ln_step, 5 * c + 5)
                tt(XN[:, cs, :], XN[:, cs, :], ST8[:, 4, cs].unsqueeze(2).to_broadcast([128, 4, D]), ALU.mult).then_inc(xn_ready, 1)
            dve.wait_ge(consts, 7)
            nc.vector.tensor_reduce(maskG[:, :], ident[:, :].rearrange("r (j p) -> r p j", p=HALF), AX.X, ALU.add).then_inc(masks, 1)
            nc.vector.tensor_reduce(mask8[:, :], ident[:, :].rearrange("r (p t) -> r p t", p=8), AX.X, ALU.add).then_inc(masks, 1)
            nc.vector.tensor_reduce(maskKT[:, :], ident[:, :].rearrange("r (g e i) -> r e g i", g=4, e=2), AX.XY, ALU.add).then_inc(masks, 1)
            dve.wait_ge(ld_small, 16)
            dve.wait_ge(scores, 1)
            steps = [0]

            def link(ins):
                ins.then_inc(rt_step, 1)
                steps[0] += 1
                dve.wait_ge(rt_step, steps[0])

            link(tt(BI[:, :, :], SC[:, :, :], EB.unsqueeze(1).to_broadcast([128, NX, E]), ALU.add))
            other = BI.unsqueeze(2).to_broadcast([128, NX, E, E])
            own = BI.unsqueeze(3).to_broadcast([128, NX, E, E])
            dve.wait_ge(xnT_ready, 8)
            link(tt(GT, other, own, ALU.is_gt))
            link(tt(EQ, other, own, ALU.is_equal))
            link(tt(EQ, EQ, tri[:, :, :].unsqueeze(1).to_broadcast([128, NX, E, E]), ALU.mult))
            link(tt(GT, GT, EQ, ALU.add))
            link(nc.vector.tensor_reduce(RK[:, :, :], GT, AX.X, ALU.add))
            link(nc.vector.tensor_scalar(RK[:, :, :], RK[:, :, :], 1.5, None, ALU.is_lt))
            link(tt(RK[:, :, :], RK[:, :, :], SC[:, :, :], ALU.mult))
            link(nc.vector.tensor_reduce(ST8[:, 5, :], RK[:, :, :], AX.X, ALU.add))
            link(nc.vector.tensor_scalar(ST8[:, 5, :], ST8[:, 5, :], 1e-8, None, ALU.add))
            link(nc.vector.reciprocal(ST8[:, 6, :], ST8[:, 5, :]))
            link(nc.vector.tensor_scalar(ST8[:, 6, :], ST8[:, 6, :], 1.0 / R, None, ALU.mult))
            link(tt(RK[:, :, :], RK[:, :, :], ST8[:, 6, :].unsqueeze(2).to_broadcast([128, NX, E]), ALU.mult))
            link(nc.vector.memset(WEXP[:, :, E * R:LR], 1.0 / R))
            link(nc.vector.tensor_copy(WEXP[:, :, 0:E * R].rearrange("p n (e r) -> p n e r", e=E),
                                       RK.unsqueeze(3).to_broadcast([128, NX, E, R])))
            assert steps[0] == 15
            dve.wait_ge(wT_ready, 4)
            nc.vector.nop().then_inc(had_ready, 1)
            with dve.Fori(0, NCH) as c:
                wt = WT[0:LR, bass.ds(c * CH, CH)]
                for k, dst in enumerate((XAG, XAU)):
                    dve.wait_ge(xa_psum, c * 2 + k + 1)
                    tt(dst[0:LR, :], bank(4 + k)[0:LR, :], wt, ALU.mult).then_inc(xa_ready, 1)
                for f in range(NF):
                    fr = slice(0, FT[f])
                    dve.wait_ge(gu_sig, c * NF + f + 1)
                    tt(SG[fr, f % 2, :], SG[fr, f % 2, :], bank(2 * (f % 2))[fr, :], ALU.mult).then_inc(gu_silu, 1)
                    dve.wait_ge(gu_silu, c * NF + f + 1)
                    tt(HID[fr, f, :], SG[fr, f % 2, :], bank(2 * (f % 2) + 1)[fr, :], ALU.mult).then_inc(hid_ready, 1)
                dve.wait_ge(had_psum, c + 1)
                tt(HAD[0:LR, :], bank(5)[0:LR, :], wt, ALU.mult).then_inc(had_ready, 1)
                for q in range(4):
                    dve.wait_ge(ffn_psum, c * 4 + q + 1)
                    dve.wait_ge(base_stored[q % 2], c * 32 + 16 * (q // 2) + 16)
                    tt(BASE[:, q % 2, :], bank(6 + q % 2, D), XIN[:, bass.ds(c * 4 + q, 1), :].rearrange("p a d -> p (a d)"), ALU.add).then_inc(base_ready, 1)
            for _ in range(3):
                nc.vector.nop().then_inc(silu_done, 1)
            with dve.Fori(0, NPC) as c:
                def conv(x):
                    kind = JOBS[CONV_JOB0 + 4 * x][0]
                    w = "qkv".index(kind)
                    dve.wait_ge(job_free, c * NJ + 8 + CONV_JOB0 + 4 * x + 4)
                    for i in range(TAPS):
                        for h in range(4):
                            hh = 4 * (x % (NQ // 3)) + h
                            if i > 0:
                                dve.wait_ge(tap_add, (c * NQ + x) * (4 * TAPS) + 4 * (i - 1) + h + 1)
                            acc = ACC[:, x % 3, h, :]
                            nc.vector.scalar_tensor_tensor(acc, PRE[:, x % 2, h, B * i:B * i + PC], CW[:, w, i, hh:hh + 1], acc, ALU.mult, ALU.add).then_inc(tap_add, 1)

                def finish(x):
                    kind, h0, _ = JOBS[CONV_JOB0 + 4 * x]
                    acc, sig = ACC[:, x % 3], SIG[:, x % 2]
                    acc_t = acc.rearrange("p h (t b) -> p h t b", b=B)
                    dve.wait_ge(sig_ready, c * NQ + x + 1)
                    if kind == "q":
                        if x == 0:
                            dve.wait_ge(kq_stored, c * 16 + 16)
                        tt(by_head(KQST, h0, 4, 2, 1), acc_t, sig.rearrange("p h (t b) -> p h t b", b=B), ALU.mult).then_inc(silu_done, 1)
                    elif kind == "k":
                        nc.vector.scalar_tensor_tensor(acc, sig, K_SCALE, acc, ALU.mult, ALU.mult).then_inc(k_scaled, 1)
                        dve.wait_ge(k_scaled, c * (NQ // 3) + x - NQ // 3 + 1)
                        tt(by_head(KQST, h0, 4, 2, 0), acc_t, by_head(BETA, h0, 4), ALU.mult).then_inc(silu_done, 1)
                    else:
                        tt(acc, acc, sig, ALU.mult).then_inc(v_silu, 1)
                        dve.wait_ge(v_silu, c * (NQ // 3) + x - 2 * NQ // 3 + 1)
                        if x == 2 * NQ // 3:
                            dve.wait_ge(bv_stored, c * 16 + 16)
                        tt(by_head(BVST, h0, 4), acc_t, by_head(BETA, h0, 4), ALU.mult).then_inc(silu_done, 1)

                for x in range(NQ):
                    conv(x)
                    if x > 0:
                        finish(x - 1)
                finish(NQ - 1)

            def decays(base, c):
                A4 = Af[c].rearrange("v (m j p) -> v m j p", m=NB, j=BL)
                nc.vector.tensor_copy(SFX[c][:, :, 2, :], A4[:, :, 3, :]).then_inc(sfx, 1)
                tt(SFX[c][:, :, 1, :], A4[:, :, 2, :], A4[:, :, 3, :], ALU.mult).then_inc(sfx, 1)
                dve.wait_ge(sfx, base + 2)
                tt(SFX[c][:, :, 0, :], A4[:, :, 1, :], SFX[c][:, :, 1, :], ALU.mult).then_inc(sfx, 1)
                dve.wait_ge(sfx, base + 3)
                tt(ABL[c], A4[:, :, 0, :], SFX[c][:, :, 0, :], ALU.mult).then_inc(sfx, 1)
                dve.wait_ge(sfx, base + 4)
                nc.vector.tensor_copy(ASF[c][:, 2, :], ABL[c][:, 3, :]).then_inc(sfx, 1)
                tt(ASF[c][:, 1, :], ABL[c][:, 2, :], ABL[c][:, 3, :], ALU.mult).then_inc(sfx, 1)
                dve.wait_ge(sfx, base + 6)
                tt(ASF[c][:, 0, :], ABL[c][:, 1, :], ASF[c][:, 1, :], ALU.mult).then_inc(sfx, 1)
                dve.wait_ge(sfx, base + 7)
                tt(ACH[c], ABL[c][:, 0, :], ASF[c][:, 0, :], ALU.mult).then_inc(sfx, 1)

            def prods(m, j, c):
                t = BL * m + j
                e, hi = 2 * t + 1, 2 * BL * (m + 1)
                tt(PR[:, OFF[j]:OFF[j] + hi - e, :].rearrange("k i (a p) -> k a i p", a=2), KQ[c][:, e:hi, :].rearrange("k i (a p) -> k a i p", a=2),
                   KR[c][:, :, t, :].unsqueeze(2).to_broadcast([128, 2, hi - e, HALF]), ALU.mult).then_inc(prod_ready, 1)

            dve.wait_ge(in_ready[0], 64)
            nc.vector.memset(S[:, :, :], 0.0).then_inc(zeros, 1)
            nc.vector.memset(PTf, 0.0).then_inc(zeros, 1)
            nc.vector.memset(KTB[1], 0.0).then_inc(zeros, 1)
            nc.vector.memset(Xf[0], 0.0).then_inc(zeros, 1)
            for c in range(2):
                nc.vector.memset(ASF[c][:, NB - 1, :], 1.0).then_inc(zeros, 1)
            dve.wait_ge(zeros, 6)
            decays(0, 0)
            for j in range(BL):
                prods(0, j, 0)
            with dve.Fori(0, NSUP // 2) as i:
                for c in range(2):
                    n = i * 2 + c
                    d = 1 - c
                    Xc = X[c]
                    wk = n * NWK

                    def mask_piece(m, u):
                        if m < NB - 1:
                            half, a, b = PIECES[m][u]
                            k = WK0[m] + u
                            dve.wait_ge(wk_full, wk + k + 1)
                            tt(GBD[:, half, a - 8:b - 8, :], bank(3 + k % 2)[:, 0:HALF * (b - a)].rearrange("r (i p) -> r i p", p=HALF),
                               maskG[:, :].unsqueeze(1).to_broadcast([128, b - a, HALF]), ALU.mult).then_inc(wk_free, 1)
                        else:
                            k = WK0[m] + u
                            dve.wait_ge(wk_full, wk + k + 1)
                            tt(G2[:, 2 * u:2 * u + 2].rearrange("r s i p -> r (s i) p"), bank(3 + k % 2).rearrange("r (x p) -> r x p", p=8),
                               mask8[:, :].unsqueeze(1).to_broadcast([128, 2 * NI, 8]), ALU.mult).then_inc(wk_free, 1)

                    def add_updates(m, at):
                        for k, x in zip(SLOTS[m], ADD_AT[len(SLOTS[m])]):
                            if x == at and k < NR:
                                u, r = divmod(k, 4)
                                dve.wait_ge(up_psum, n * NR + k + 1)
                                sv = Sr[:, u, r].rearrange("v a e k -> v a (e k)")
                                tt(sv, sv, bank(7).rearrange("v (a x) -> v a x", a=2), ALU.add).then_inc(s_updated, 1)

                    for m in range(NB):
                        hi = 2 * BL * (m + 1)
                        for j in range(BL):
                            t = BL * m + j
                            e = 2 * t + 1
                            if j > 0:
                                dve.wait_ge(x_step, n * C + t)
                            tt(W[:, :, t, :], BV[c][:, t, :].rearrange("v (a p) -> v a p", a=2), Xc[:, 2 * t, :].rearrange("v (a p) -> v a p", a=2), ALU.subtract).then_inc(w_ready, 1)
                            tt(Xc[:, e:hi, :], Xc[:, e:hi, :], A[c][:, t, :].unsqueeze(1).to_broadcast([128, hi - e, NP]), ALU.mult).then_inc(x_decayed, 1)
                            if j < (NPIECE[m] if m < NB - 1 else NXP):
                                mask_piece(m, j)
                            add_updates(m, (j, 0))
                            if j == 0:
                                dve.wait_ge(bcast_psum, n * 8 + 2 * m + 2)
                            dve.wait_ge(w_ready, n * C + t + 1)
                            g = PS[:, 512:1536].rearrange("v (a i p) -> v a i p", a=2, p=HALF)[:, :, OFF[j]:OFF[j] + hi - e, :]
                            wb = W[:, :, t, :].unsqueeze(2).to_broadcast([128, 2, hi - e, HALF])
                            tt(TT[:, :, 0:hi - e, :], g, wb, ALU.mult).then_inc(wg_ready, 1)
                            if m < NB - 1:
                                prods(m + 1, j, c)
                            else:
                                if j == 0:
                                    dve.wait_ge(in_ready[d], (i + 1 + c) * 64)
                                prods(0, j, d)
                            dve.wait_ge(wg_ready, n * C + t + 1)
                            dve.wait_ge(x_decayed, n * C + t + 1)
                            xs = Xc[:, e:hi, :].rearrange("v i (a p) -> v a i p", a=2)
                            tt(xs, xs, TT[:, :, 0:hi - e, :], ALU.add).then_inc(x_step, 1)
                            add_updates(m, (j, 1))
                        wl = W[:, :, BL * m:BL * m + 3, :]
                        tt(wl, wl, SFX[c][:, m, :, :].rearrange("v j (a p) -> v a j p", a=2), ALU.mult).then_inc(what_ready, 1)
                        if m < NB - 1:
                            tt(Xc[:, hi:NI, :], Xc[:, hi:NI, :], ABL[c][:, m, :].unsqueeze(1).to_broadcast([128, NI - hi, NP]), ALU.mult).then_inc(x_blk, 1)
                            dve.wait_ge(x_blk, n * 3 + m + 1)
                            for u, (half, a, b) in enumerate(PIECES[m]):
                                k = WK0[m] + NPIECE[m] + u
                                dve.wait_ge(wk_full, wk + k + 1)
                                xs = Xc[:, a:b, HALF * half:HALF * (half + 1)]
                                tt(xs, xs, bank(3 + k % 2)[:, 0:HALF * (b - a)].rearrange("v (i p) -> v i p", p=HALF), ALU.add).then_inc(wk_free, 1)
                            dve.wait_ge(wk_free, wk + WK0[m + 1])
                    dve.wait_ge(what_ready, n * NB + NB)
                    for a in range(2):
                        ps = slice(HALF * a, HALF * (a + 1))
                        tt(PP[:, ps, :].rearrange("v p (m j) -> v m j p", j=BL), W[:, a, :, :].rearrange("v (m j) p -> v m j p", j=BL),
                           ASF[c][:, :, ps].unsqueeze(2).to_broadcast([128, NB, BL, HALF]), ALU.mult).then_inc(p_ready, 1)
                    decays(n * 8 + 8, d)
                    dve.wait_ge(x_ready, n * NR + NR)
                    for u in range(NXP):
                        k = WK0[NB - 1] + NXP + u
                        dve.wait_ge(wk_full, wk + k + 1)
                        xs = X[d][:, :, 16 * u:16 * u + 16].rearrange("v i (a p) -> v a i p", a=2)
                        tt(xs, xs, bank(3 + k % 2).rearrange("v (a i p) -> v a i p", a=2, p=8), ALU.add).then_inc(wk_free, 1)
                    dve.wait_ge(wk_free, wk + NWK)
            nc.vector.nop().then_inc(fin, 1)
            dve.wait_ge(oc_in, 32)
            nc.vector.tensor_scalar(centre, ident[:, :], -1.0 / DH, None, ALU.add).then_inc(centre_ready, 1)
            with dve.Fori(0, NCH) as c:
                dve.wait_ge(gate_ready, c * H + H)
                for h in range(H + 1):
                    if h < H:
                        dve.wait_ge(std, c * H + h + 1)
                        nc.vector.reciprocal(RSTD[:, h % 2, :], STD[:, h % 2, :]).then_inc(rstd, 1)
                        dve.wait_ge(rstd, c * H + h + 1)
                        tt(NRM[:, h % 2, :], bank(h % 4), RSTD[:, h % 2, :], ALU.mult).then_inc(normed, 1)
                    if h > 0:
                        j = h - 1
                        dve.wait_ge(affine, c * H + j + 1)
                        if j >= 2:
                            dve.wait_ge(y_step, c * H + j - 1)
                        tt(Z[:, j % 2, :], AFF[:, j % 2, :], GATE[:, j, :], ALU.mult).then_inc(gated, 1)
                dve.wait_ge(oc_in, c * 32 + 32)
                for q in range(4):
                    dve.wait_ge(yt_psum, c * 4 + 2 * (q // 2) + 2)
                    tt(BASEC[:, q, :], bank(4 + q // 2)[:, D * (q % 2):D * (q % 2 + 1)], BASEC[:, q, :], ALU.add).then_inc(fin, 1)

        @block.tensor
        def _(pe):
            mm = nc.tensor.matmul
            pe.wait_ge(consts, 7)
            for c in range(4):
                pe.wait_ge(xn_ready, c + 1)
                for k in range(2):
                    for i in range(4):
                        ins = nc.tensor.transpose(bank(2 * c + k)[:, 128 * i:128 * (i + 1)], XN[:, 4 * c + i, 128 * k:128 * (k + 1)], ident[:, :])
                    ins.then_inc(xnT_psum, 1)
            pe.wait_ge(ld_small, 16)
            pe.wait_ge(xnT_ready, 8)
            for i in range(NX):
                for k in range(2):
                    ins = mm(bank(0)[:, E * i:E * (i + 1)], XNT[:, k, HALO + 128 * i:HALO + 128 * (i + 1)], WR[:, k, :], start=(k == 0), stop=(k == 1))
            ins.then_inc(logits, 1)
            pe.wait_ge(rt_step, 15)
            for i in range(NX):
                ins = nc.tensor.transpose(bank(1 + i // 4)[0:LR, 128 * (i % 4):128 * (i % 4 + 1)], WEXP[:, i, :], ident[:, :])
                if i % 4 == 3:
                    ins.then_inc(wT_psum, 1)
            pe.wait_ge(ld_ffn, 16 * 11)
            pe.wait_ge(wT_ready, 4)
            with pe.Fori(0, NCH) as c:
                xs = [XNT[:, k, bass.ds(c * CH + HALO, CH)] for k in range(2)]
                for j, a in enumerate((AG, AU)):
                    pe.wait_ge(had_ready, c + 1)
                    for k in range(2):
                        ins = mm(bank(4 + j)[0:LR, :], a[:, k, :], xs[k], start=(k == 0), stop=(k == 1))
                    ins.then_inc(xa_psum, 1)
                for f in range(NF):
                    if f >= 2:
                        pe.wait_ge(hid_ready, c * NF + f - 1)
                    fs = slice(FW * f, FW * f + FT[f])
                    for j, (w, b, xa) in enumerate(((WG, BG, XAG), (WU, BU, XAU))):
                        o = bank(2 * (f % 2) + j)[0:FT[f], :]
                        for k in range(2):
                            mm(o, w[:, k, fs], xs[k], start=(k == 0), stop=False)
                        if f == 0:
                            pe.wait_ge(xa_ready, c * 2 + j + 1)
                        ins = mm(o, b[0:LR, fs], xa[0:LR, :], start=False, stop=True)
                    ins.then_inc(gu_psum, 1)
                for f in range(NF):
                    pe.wait_ge(hid_ready, c * NF + f + 1)
                    ins = mm(bank(5)[0:LR, :], AD[0:FT[f], f, :], HID[0:FT[f], f, :], start=(f == 0), stop=(f == NF - 1))
                ins.then_inc(had_psum, 1)
                for q in range(4):
                    if q >= 2:
                        pe.wait_ge(base_ready, c * 4 + q - 1)
                    for f in range(NF):
                        mm(bank(6 + q % 2, D), HID[0:FT[f], f, 128 * q:128 * (q + 1)], WD[0:FT[f], f, :], start=(f == 0), stop=False)
                    if q == 0:
                        pe.wait_ge(had_ready, c + 2)
                    mm(bank(6 + q % 2, D), HAD[0:LR, 128 * q:128 * (q + 1)], BD[0:LR, :], start=False, stop=True).then_inc(ffn_psum, 1)
            pe.wait_ge(base_ready, NX)
            pe.wait_ge(ld_attn, 16 * 4)
            with pe.Fori(0, NPC) as c:
                for g, (kind, h0, nh) in enumerate(JOBS):
                    pe.wait_ge(job_free, c * NJ + g + 1)
                    cols = HALO + PC if kind in "qkv" else PC
                    for k in range(nh):
                        for kt in range(2):
                            if kind == "b":
                                w = WB[:, kt, h0 + k:h0 + k + 1].to_broadcast([128, 128])
                            else:
                                w = W4[:, WSLOT[kind], kt, DH * (h0 + k):DH * (h0 + k + 1)]
                            ins = mm(bank(g % 8)[:, cols * k:cols * (k + 1)], w,
                                     XNT[:, kt, bass.ds(c * PC + (HALO + PC - cols), cols)], start=(kt == 0), stop=(kt == 1))
                    ins.then_inc(job_full, 1)

            def broadcast_products(prod_count):
                pe.wait_ge(prod_ready, prod_count)
                for a in range(2):
                    mm(bank(1 + a).rearrange("v (i p) -> v i p", p=HALF), ones[:, :], PR[:, :, HALF * a:HALF * (a + 1)], start=True, stop=True).then_inc(bcast_psum, 1)

            def key_products(m, u, c):
                half, a, b = PIECES[m][u]
                k = WK0[m] + u
                mm(bank(3 + k % 2)[:, 0:HALF * (b - a)].rearrange("r (i p) -> r i p", p=HALF), KR[c][:, half, BL * m:BL * (m + 1), :].rearrange("k t p -> k (t p)"),
                   KQ[c][:, a:b, HALF * half:HALF * (half + 1)], start=True, stop=True).then_inc(wk_full, 1)

            pe.wait_ge(in_ready[0], 64)
            pe.wait_ge(zeros, 6)
            broadcast_products(BL)
            for u in range(2):
                key_products(0, u, 0)
            with pe.Fori(0, NSUP // 2) as i:
                for c in range(2):
                    n = i * 2 + c
                    d = 1 - c
                    wk = n * NWK

                    def slot(k):
                        if k < NR:
                            u, r = divmod(k, 4)
                            if k > 0:
                                pe.wait_ge(s_updated, n * NR + k)
                            for a in range(2):
                                s = 2 * u + a
                                ins = mm(bank(7)[:, 256 * a:256 * (a + 1)], PT[32 * r:32 * r + 32, s, :],
                                         KTB[d][32 * r:32 * r + 32, s, :, :].rearrange("r e k -> r (e k)"), start=True, stop=True)
                            ins.then_inc(up_psum, 1)
                        j = k - 1
                        if 0 <= j < NR:
                            u, r = divmod(j, 4)
                            pe.wait_ge(s_scaled, n * NR + j + 1)
                            if j > 0:
                                pe.wait_ge(st_ready, n * NR + j)
                            for a in range(2):
                                for e in range(2):
                                    q = 2 * a + e
                                    ins = nc.tensor.transpose(bank(6)[:, DH * q:DH * (q + 1)], Sr[:, u, r, a, e, :], ident[:, :])
                            ins.then_inc(st_psum, 1)
                        j = k - 2
                        if 0 <= j < NR:
                            u, r = divmod(j, 4)
                            if j == 0:
                                pe.wait_ge(in_ready[d], (i + 1 + c) * 64)
                            else:
                                pe.wait_ge(x_ready, n * NR + j)
                            pe.wait_ge(st_ready, n * NR + j + 1)
                            for a in range(2):
                                for e in range(2):
                                    q = 2 * a + e
                                    p0 = 16 * u + 8 * a + 4 * (r // 2)
                                    ins = mm(bank(5)[:, 4 * NI * q:4 * NI * (q + 1)].rearrange("v (i p) -> v i p", p=4), STR[:, j % 2, a, e, :],
                                             KQ[d][:, :, p0:p0 + 4], start=True, stop=True)
                            ins.then_inc(ro_psum, 1)

                    def products(m, u):
                        k = WK0[m] + u
                        pe.wait_ge(wk_free, wk + k - 1)
                        if m < NB - 1:
                            key_products(m, u, c)
                        else:
                            for a in range(2):
                                s = 2 * u + a
                                ins = mm(bank(3 + k % 2)[:, 256 * a:256 * (a + 1)].rearrange("r (i p) -> r i p", p=8), KP[:, 8 * s:8 * s + 8, :].rearrange("k p t -> k (p t)"),
                                         KQ[d][:, :, 8 * s:8 * s + 8], start=True, stop=True)
                            ins.then_inc(wk_full, 1)

                    for m in range(NB):
                        np_ = NPIECE[m] if m < NB - 1 else NXP
                        for x, k in enumerate(SLOTS[m]):
                            slot(k)
                            if 2 + x < np_:
                                products(m, 2 + x)
                        if m < NB - 1:
                            if m > 0:
                                pe.wait_ge(kt_ready, n * 2 + m)
                            pe.wait_ge(what_ready, n * NB + m + 1)
                            for a in range(2):
                                ins = nc.tensor.transpose(bank(0)[:, 128 * a:128 * (a + 1)], W[:, a, BL * m:BL * (m + 1), :].rearrange("v t p -> v (t p)"), ident[:, :])
                            ins.then_inc(wht_psum, 1)
                            pe.wait_ge(wg_ready, n * C + BL * (m + 1))
                            broadcast_products(n * C + BL * (m + 2))
                            pe.wait_ge(wht_ready, n * 3 + m + 1)
                            for u, (half, a, b) in enumerate(PIECES[m]):
                                k = WK0[m] + NPIECE[m] + u
                                pe.wait_ge(wk_free, wk + k - 1)
                                mm(bank(3 + k % 2)[:, 0:HALF * (b - a)].rearrange("r (i p) -> r i p", p=HALF), WHT[:, 128 * half:128 * (half + 1)], GBD[:, half, a - 8:b - 8, :],
                                   start=True, stop=True).then_inc(wk_full, 1)
                            if m < 2:
                                pe.wait_ge(kp_ready, n + 1)
                                for s in range(4):
                                    ins = nc.tensor.transpose(bank(0)[:, 128 * s:128 * (s + 1)], KP[:, 8 * (4 * m + s):8 * (4 * m + s) + 8, :].rearrange("k q t -> k (q t)"), ident[:, :])
                                ins.then_inc(kt_psum, 1)
                            for u in range(2):
                                products(m + 1, u)
                        else:
                            pe.wait_ge(wg_ready, n * C + C)
                            broadcast_products(n * C + C + BL)
                            pe.wait_ge(s_updated, n * NR + NR)
                            pe.wait_ge(p_ready, n * 2 + 2)
                            for s in range(8):
                                ins = nc.tensor.transpose(bank(7 * (s // 4))[:, 128 * (s % 4):128 * (s % 4 + 1)], PP[:, 8 * s:8 * s + 8, :].rearrange("v q t -> v (q t)"), ident[:, :])
                                if s % 4 == 3:
                                    ins.then_inc(pt_psum, 1)
                            pe.wait_ge(pt_ready, n * 2 + 2)
                            for u in range(NXP):
                                k = WK0[m] + NXP + u
                                pe.wait_ge(wk_free, wk + k - 1)
                                for a in range(2):
                                    s = 2 * u + a
                                    ins = mm(bank(3 + k % 2)[:, 256 * a:256 * (a + 1)], PT[:, s, :], G2[:, s].rearrange("r i p -> r (i p)"), start=True, stop=True)
                                ins.then_inc(wk_full, 1)
                            for u in range(2):
                                pe.wait_ge(wk_free, wk + NWK + u - 1)
                                key_products(0, u, d)
            pe.wait_ge(ld_last, 32)
            pe.wait_ge(centre_ready, 1)
            with pe.Fori(0, NCH) as c:
                for h in range(H):
                    if h >= 4:
                        pe.wait_ge(gate_ready, c * H + h - 3)
                    for kt in range(2):
                        ins = mm(bank(h % 4), WGT[:, kt, DH * h:DH * (h + 1)], XNT[:, kt, bass.ds(c * CH + HALO, CH)], start=(kt == 0), stop=(kt == 1))
                    ins.then_inc(gate_psum, 1)
                for h in range(H + 3):
                    if h < H:
                        if h == 0:
                            pe.wait_ge(gate_ready, c * H + H)
                            pe.wait_ge(oc_in, c * 32 + 32)
                        if h >= 4:
                            pe.wait_ge(normed, c * H + h - 3)
                        mm(bank(h % 4).rearrange("v (t b) -> v t b", b=B), centre,
                           OC.rearrange("v (t g b h) -> v g h t b", g=2, b=B, h=8)[:, h // 8, h % 8], start=True, stop=True).then_inc(cen_psum, 1)
                    j = h - 1
                    if 0 <= j < H:
                        if j == 0:
                            pe.wait_ge(fin, c * 4 + 1)
                        if j >= 2:
                            pe.wait_ge(std, c * H + j - 1)
                        pe.wait_ge(squared, c * H + j + 1)
                        mm(bank(4 + j % 2), ones[:, :], SQO[:, j % 2, :], start=True, stop=True).then_inc(var_psum, 1)
                    j = h - 3
                    if j >= 0:
                        pe.wait_ge(gated, c * H + j + 1)
                        for dh in range(2):
                            ins = mm(bank(6 + dh), WO[:, j, 128 * dh:128 * (dh + 1)], Z[:, j % 2, :], start=(j == 0), stop=(j == H - 1))
                        ins.then_inc(y_step, 1)
                pe.wait_ge(y_ready, c * 2 + 2)
                for q in range(4):
                    for dh in range(2):
                        ins = nc.tensor.transpose(bank(4 + q // 2)[:, D * (q % 2) + 128 * dh:D * (q % 2) + 128 * (dh + 1)], YT[:, dh, 128 * q:128 * (q + 1)], ident[:, :])
                    ins.then_inc(yt_psum, 1)


def kernel(**inputs):
    import numpy as np
    import concourse.bacc as bacc
    from concourse.bass_utils import run_bass_kernel_spmd

    a = {k: np.asarray(v) for k, v in inputs.items()}

    def attn(k):
        return a["L0_attn_" + k]

    def ffn(k):
        return a["L0_ffn_" + k]

    def per_head(v):
        return np.moveaxis(v.reshape(H, DH, -1), 0, -1).reshape(DH, -1)

    def two_tiles(v):
        return v.reshape(2, 128, -1).transpose(1, 0, 2).reshape(128, -1)

    def rows(v):
        return np.broadcast_to(v[None, :], (128, v.shape[0]))

    def lora_a(experts, shared):
        return np.concatenate([experts.transpose(1, 0, 2).reshape(shared.shape[0], -1), shared], axis=1)

    def lora_b(experts, shared):
        return np.concatenate([experts.reshape(-1, shared.shape[1]), shared], axis=0)

    small = np.concatenate(
        [per_head(attn(f"conv_{t}_w").reshape(H * DH, KC)) for t in "qkv"]
        + [per_head(attn(f"conv_{t}_b")) for t in "qkv"]
        + [per_head(attn("ba")), rows(attn("bb")), attn("ln_g")[:, None], attn("ln_b")[:, None],
           two_tiles(attn("Wb").T), rows(ffn("expert_bias")), two_tiles(ffn("W_router"))], axis=1)
    arrays = {
        "x_tm": attn("x").transpose(1, 0, 2).reshape(NT, D),
        "wqT": attn("Wq").T, "wkT": attn("Wk").T, "wvT": attn("Wv").T, "waT": attn("Wa").T,
        "wgT": attn("Wg").T, "woT": attn("Wo").T, "small": small,
        "w_gate": ffn("W_gate"), "w_up": ffn("W_up"), "w_down": ffn("W_down"),
        "a_gate": lora_a(ffn("A_gate"), ffn("sA_gate")), "b_gate": lora_b(ffn("B_gate"), ffn("sB_gate")),
        "a_up": lora_a(ffn("A_up"), ffn("sA_up")), "b_up": lora_b(ffn("B_up"), ffn("sB_up")),
        "a_down": lora_a(ffn("A_down"), ffn("sA_down")), "b_down": lora_b(ffn("B_down"), ffn("sB_down")),
    }
    arrays = {k: np.ascontiguousarray(v) for k, v in arrays.items()}
    nc = bacc.Bacc("TRN2", target_bir_lowering=False, num_devices=1)
    args = [nc.dram_tensor(k, v.shape, mybir.dt.from_np(v.dtype), kind="ExternalInput").ap() for k, v in arrays.items()]
    args.append(nc.dram_tensor("out", (NT, D), F32, kind="ExternalOutput").ap())
    build(nc, *args)
    r = run_bass_kernel_spmd(nc, [arrays], core_ids=[0])
    y = r.results[0]["out"]
    return y.reshape(T, B, D).transpose(1, 0, 2)
```

```python
from contextlib import ExitStack

import concourse.bass as bass
from concourse import mybir

F32 = mybir.dt.float32
ALU = mybir.AluOpType
ACT = mybir.ActivationFunctionType
AX = mybir.AxisListType

B, T, D, H, DH = 4, 512, 256, 16, 128
NP = B * H
NT = B * T
KC = 4
E, R, DFF = 8, 8, 688
C = 16
BL = 4
NB = C // BL
NSUP = T // C
HALO = (KC - 1) * B
NI = 2 * C
LR = E * R + R
NF = (DFF + 127) // 128
FW = (DFF + NF - 1) // NF
FT = [min(FW, DFF - FW * f) for f in range(NF)]
NX = NT // 128
CH = 512
NCH = NT // CH
OFF = [0, 7, 12, 15]
K_SCALE = float(DH) ** -0.5
HALF = NP // 2
PC = 256
NPC = NT // PC
PSC = PC // B // C
OSC = CH // B // C

CW0, CB0 = 0, 3 * KC * H
BA0 = CB0 + 3 * H
BB0 = BA0 + H
LN0 = BB0 + H
WB0 = LN0 + 2
EB0 = WB0 + 2 * H
WR0 = EB0 + E
NSMALL = WR0 + 2 * E

PIECES = []
for m in range(NB - 1):
    lo = 2 * BL * (m + 1)
    cuts = [(i, min(i + 16, NI)) for i in range(lo, NI, 16)]
    PIECES.append([(half, a, b) for half in range(2) for a, b in cuts])
NPIECE = [len(x) for x in PIECES]
NXP = 4
NWK = 2 * sum(NPIECE) + 2 * NXP
WK0 = [2 * sum(NPIECE[:m]) for m in range(NB)]

NR = 16
SLOTS = [list(range(0, 5)), list(range(5, 10)), list(range(10, 14)), list(range(14, 18))]
ADD_AT = [[(0, 0), (1, 0), (1, 1), (2, 1), (3, 2)], [(0, 1), (1, 1), (2, 1), (3, 1), (3, 2)],
          [(0, 1), (1, 1), (2, 1), (3, 2)], [(0, 1), (1, 1), (2, 1), (3, 2)]]

NQ = 3 * H // 4
JOBS, FIRST, EXTRA = [], [], []
for x in range(NQ):
    FIRST.append(len(JOBS))
    JOBS += [("qkv"[4 * x // H], (4 * x + h) % H, 1) for h in range(4)]
    more = [("b", 4 * x + 2 * i, 2) for i in range(2)] if x < NQ // 3 else [("a", 2 * (x - NQ // 3), 2)]
    EXTRA.append(range(len(JOBS), len(JOBS) + len(more)))
    JOBS += more
NJ = len(JOBS)
WSLOT = {"q": 0, "k": 1, "v": 2, "a": 3}
TAPS = KC - 1


def build(nc, x_tm, wqT, wkT, wvT, waT, wgT, woT, small, w_gate, w_up, w_down, a_gate, b_gate,
          a_up, b_up, a_down, b_down, out):
    def dram(name, shape):
        return nc.dram_tensor(name, shape, F32, kind="Internal").ap()

    base_d = dram("base_d", (NT, D))
    kq_d = dram("kq_d", (NSUP, 128, NI * NP))
    kr_d = dram("kr_d", (NSUP, 128, C * NP))
    bv_d = dram("bv_d", (NSUP, 128, C * NP))
    a_d = dram("a_d", (NSUP, 128, C * NP))
    o_d = dram("o_d", (NSUP, 128, C * NP))

    with ExitStack() as ctx:
        def sb(name, shape):
            return ctx.enter_context(nc.sbuf_tensor(name, shape, F32))

        def sem(name):
            return ctx.enter_context(nc.semaphore(name))

        XNT = sb("XNT", [128, 2, HALO + NT])
        SM = sb("SM", [128, NSMALL])
        ident = sb("ident", [128, 128])
        ones = sb("ones", [128, 128])
        maskG = sb("maskG", [128, HALF])
        maskKT = sb("maskKT", [128, 2])
        mask8 = sb("mask8", [128, 8])
        mask4 = sb("mask4", [128, 4])
        eps = sb("eps", [128, 1])
        NARENA = 48256
        arena = sb("arena", [128, NARENA])
        CW = SM[:, CW0:CW0 + 3 * KC * H].rearrange("p (x i h) -> p x i h", x=3, i=KC)
        CB = SM[:, CB0:CB0 + 3 * H].rearrange("p (x h) -> p x h", x=3)
        BA = SM[:, BA0:BA0 + H]
        BB = SM[:, BB0:BB0 + H]
        LNG, LNB = SM[:, LN0:LN0 + 1], SM[:, LN0 + 1:LN0 + 2]
        WB = SM[:, WB0:WB0 + 2 * H].rearrange("p (c h) -> p c h", c=2)
        EB = SM[:, EB0:EB0 + E]
        WR = SM[:, WR0:WR0 + 2 * E].rearrange("p (c e) -> p c e", c=2)

        pos = [0]

        def take(n):
            pos[0] += n
            assert pos[0] <= NARENA
            return arena[:, pos[0] - n:pos[0]]

        W4 = take(4 * 2 * H * DH).rearrange("p (x c n) -> p x c n", x=4, c=2)
        after_w4 = pos[0]
        KQST = take(PSC * NI * NP)
        KRST = take(PSC * C * NP)
        BVST = take(PSC * C * NP)
        AST = take(PSC * C * NP)
        BETA = take(PSC * C * NP)
        PRE = take(2 * 4 * (HALO + PC)).rearrange("p (s h n) -> p s h n", s=2, h=4)
        ACC = take(3 * 4 * PC).rearrange("p (s h n) -> p s h n", s=3, h=4)
        SIG = take(2 * 4 * PC).rearrange("p (s h n) -> p s h n", s=2, h=4)

        def by_head(tile, h, nh=1, te=1, e=0):
            v = tile.rearrange("p (t e g b h) -> p e g h t b", e=te, g=2, b=B, h=8)[:, e, h // 8]
            return v[:, h % 8:h % 8 + nh]

        pos[0] = 0
        S = take(NP * DH).rearrange("v (p k) -> v p k", p=NP)
        Sr = S.rearrange("v (u a r e) k -> v u r a e k", u=4, a=2, r=4)
        Xf = [take(NI * NP)]
        PTZ = take(4 * 8 * DH).rearrange("r (g s v) -> r g s v", g=4, s=8)
        KTBf = [take(2048)]
        assert pos[0] <= after_w4
        KQf = [take(NI * NP) for _ in range(2)]
        KRf = [take(C * NP) for _ in range(2)]
        BVf = [take(C * NP)]
        Af = [take(C * NP)]
        assert pos[0] <= after_w4 + PSC * NI * NP
        BVf.append(take(C * NP))
        Af.append(take(C * NP))
        assert pos[0] <= after_w4 + PSC * (NI + C) * NP
        STR = take(2 * 4 * DH).rearrange("k (s a e v) -> k s a e v", s=2, a=2, e=2)
        Xf.append(take(NI * NP))
        KTBf.insert(0, take(2048))
        X = [x.rearrange("v (i p) -> v i p", p=NP) for x in Xf]
        KTB = [x.rearrange("r (s e k) -> r s e k", s=8, e=2) for x in KTBf]
        KQ = [x.rearrange("k (i p) -> k i p", p=NP) for x in KQf]
        KR = [x.rearrange("k (a t p) -> k a t p", a=2, p=HALF) for x in KRf]
        BV = [x.rearrange("v (t p) -> v t p", p=NP) for x in BVf]
        A = [x.rearrange("v (t p) -> v t p", p=NP) for x in Af]
        W = take(C * NP).rearrange("v (a t p) -> v a t p", a=2, p=HALF)
        PR = take(16 * NP).rearrange("k (i p) -> k i p", p=NP)
        GBD = take(2 * 24 * HALF).rearrange("r (a i p) -> r a i p", a=2, i=24)
        G2 = take(8 * NI * 8).rearrange("r (s i p) -> r s i p", s=8, p=8)
        PPf = take(C * NP)
        PP = PPf.rearrange("v (p t) -> v p t", t=C)
        WHT = PPf[:, 0:256]
        TT = PPf[:, 256:256 + 7 * NP].rearrange("v (a i p) -> v a i p", a=2, i=7)
        KP = take(C * NP).rearrange("k (p t) -> k p t", t=C)
        PTf = take(8 * DH)
        PT = PTf.rearrange("r (s v) -> r s v", s=8)
        OT = take(C * NP)
        SFX = [take(NB * 3 * NP).rearrange("v (m j p) -> v m j p", m=NB, j=3) for _ in range(2)]
        ABL = [take(NB * NP).rearrange("v (m p) -> v m p", m=NB) for _ in range(2)]
        ASF = [take(NB * NP).rearrange("v (m p) -> v m p", m=NB) for _ in range(2)]
        ACH = [take(NP) for _ in range(2)]
        WGT = take(2 * H * DH).rearrange("p (c n) -> p c n", c=2)

        wgt_at = pos[0] - 2 * H * DH
        pos[0] = 0
        WO = take(H * D).rearrange("p (h d) -> p h d", h=H)
        OC = take(OSC * C * NP)
        GATE = take(H * CH).rearrange("p (h n) -> p h n", h=H)
        BASEC = take(4 * D).rearrange("p (q d) -> p q d", q=4)
        SQO = take(2 * CH).rearrange("p (s n) -> p s n", s=2)
        STD = take(2 * CH).rearrange("p (s n) -> p s n", s=2)
        RSTD = take(2 * CH).rearrange("p (s n) -> p s n", s=2)
        NRM = take(2 * CH).rearrange("p (s n) -> p s n", s=2)
        AFF = take(2 * CH).rearrange("p (s n) -> p s n", s=2)
        Z = take(2 * CH).rearrange("p (s n) -> p s n", s=2)
        YT = take(2 * CH).rearrange("p (c n) -> p c n", c=2)
        centre = take(128)
        assert pos[0] <= wgt_at

        pos[0] = after_w4
        XIN = take(NX * D).rearrange("p (n d) -> p n d", n=NX)
        XNf = take(NX * D)
        XN = XNf.rearrange("p (n d) -> p n d", n=NX)
        GT = XNf[:, 0:NX * 64].rearrange("p (n a b) -> p n a b", n=NX, a=E)
        EQ = XNf[:, 1024:1024 + NX * 64].rearrange("p (n a b) -> p n a b", n=NX, a=E)
        WEXP = XNf[:, 2048:2048 + NX * LR].rearrange("p (n l) -> p n l", n=NX)
        HID = XNf[:, 0:NF * CH].rearrange("p (f t) -> p f t", f=NF)
        WG = take(2 * DFF).rearrange("p (c f) -> p c f", c=2)
        WU = take(2 * DFF).rearrange("p (c f) -> p c f", c=2)
        WD = take(NF * D).rearrange("p (f d) -> p f d", f=NF)
        BG = take(DFF)
        BU = take(DFF)
        AD = take(NF * LR).rearrange("p (f l) -> p f l", f=NF)
        AG = take(2 * LR).rearrange("p (c l) -> p c l", c=2)
        AU = take(2 * LR).rearrange("p (c l) -> p c l", c=2)
        BD = take(D)
        WT = take(NT)
        XAG = take(CH)
        XAU = take(CH)
        SG = take(2 * CH).rearrange("p (s t) -> p s t", s=2)
        SQ = SG.rearrange("p s t -> p (s t)")
        HAD = take(CH)
        BASE = take(2 * D).rearrange("p (s d) -> p s d", s=2)
        ST8 = take(8 * NX).rearrange("p (k n) -> p k n", k=8)
        SC = take(NX * E).rearrange("p (n e) -> p n e", n=NX)
        BI = take(NX * E).rearrange("p (n e) -> p n e", n=NX)
        RK = take(NX * E).rearrange("p (n e) -> p n e", n=NX)
        tri = take(E * E).rearrange("p (e f) -> p e f", e=E)

        PS = ctx.enter_context(nc.psum_tensor("PS", [128, 8 * 512], F32))

        def bank(i, n=512, k=1):
            return PS[:, 512 * i:512 * i + n * k]

        ld_x = [sem(f"ld_x{c}") for c in range(4)]
        ld_small, ld_ffn, ld_attn = sem("ld_small"), sem("ld_ffn"), sem("ld_attn")
        consts, masks = sem("consts"), sem("masks")
        ln_step, ln_var, ln_std, xn_ready = sem("ln_step"), sem("ln_var"), sem("ln_std"), sem("xn_ready")
        xnT_psum, xnT_ready = sem("xnT_psum"), sem("xnT_ready")
        logits, scores, rt_step = sem("logits"), sem("scores"), sem("rt_step")
        wT_psum, wT_ready = sem("wT_psum"), sem("wT_ready")
        xa_psum, xa_ready = sem("xa_psum"), sem("xa_ready")
        gu_psum, gu_sig, gu_silu, hid_ready = sem("gu_psum"), sem("gu_sig"), sem("gu_silu"), sem("hid_ready")
        had_psum, had_ready = sem("had_psum"), sem("had_ready")
        ffn_psum, base_ready = sem("ffn_psum"), sem("base_ready")
        base_stored = [sem(f"base_stored{i}") for i in range(2)]
        job_full, job_free = sem("job_full"), sem("job_free")
        tap_add, sig_ready, silu_done = sem("tap_add"), sem("sig_ready"), sem("silu_done")
        k_scaled, v_silu, kr_staged = sem("k_scaled"), sem("v_silu"), sem("kr_staged")
        kq_stored, kr_stored, bv_stored, a_stored = sem("kq_stored"), sem("kr_stored"), sem("bv_stored"), sem("a_stored")
        in_ready = [sem(f"in_ready{i}") for i in range(2)]
        zeros, sfx = sem("zeros"), sem("suffix_products")
        up_psum, s_updated, s_scaled = sem("up_psum"), sem("s_updated"), sem("s_scaled")
        st_psum, st_ready, ro_psum, x_ready = sem("st_psum"), sem("st_ready"), sem("ro_psum"), sem("x_ready")
        prod_ready, bcast_psum = sem("prod_ready"), sem("bcast_psum")
        wk_full, wk_free = sem("work_full"), sem("work_free")
        w_ready, x_decayed, wg_ready, x_step = sem("w_ready"), sem("x_decayed"), sem("wg_ready"), sem("x_step")
        what_ready, x_blk = sem("what_ready"), sem("x_block_decayed")
        wht_psum, wht_ready = sem("wht_psum"), sem("wht_ready")
        kp_ready, kt_psum, kt_ready = sem("kp_ready"), sem("kt_psum"), sem("kt_ready")
        p_ready, pt_psum, pt_ready, ptz_ready = sem("p_ready"), sem("pt_psum"), sem("pt_ready"), sem("ptz_ready")
        o_ready, o_stored = sem("o_ready"), sem("o_stored")
        ld_last, ld_wo, oc_in, centre_ready = sem("ld_last"), sem("ld_wo"), sem("oc_in"), sem("centre_ready")
        gate_psum, gate_raw, gate_ready, base_in = sem("gate_psum"), sem("gate_raw"), sem("gate_ready"), sem("base_in")
        cen_psum, squared, var_psum, std = sem("cen_psum"), sem("squared"), sem("var_psum"), sem("std")
        rstd, normed, affine, gated = sem("rstd"), sem("normed"), sem("affine"), sem("gated")
        y_step, y_ready, yt_psum, fin, out_stored = sem("y_step"), sem("y_ready"), sem("yt_psum"), sem("out_tile"), sem("out_stored")

        block = ctx.enter_context(nc.Block())
        x_v = x_tm.rearrange("(n p) d -> p n d", p=128)

        @block.sync
        def _(sp):
            for c in range(4):
                sp.dma_start(XIN[:, 4 * c:4 * c + 4, :], x_v[:, 4 * c:4 * c + 4, :]).then_inc(ld_x[c], 16)
            n_ffn = 0
            for dst, src in ((WG, w_gate.rearrange("(c p) f -> p c f", p=128)),
                             (WU, w_up.rearrange("(c p) f -> p c f", p=128)),
                             (AG, a_gate.rearrange("(c p) l -> p c l", p=128)),
                             (AU, a_up.rearrange("(c p) l -> p c l", p=128)),
                             (BG[0:LR, :], b_gate), (BU[0:LR, :], b_up), (BD[0:LR, :], b_down),
                             (WD[0:FW, 0:NF - 1, :], w_down[0:FW * (NF - 1), :].rearrange("(f p) d -> p f d", p=FW)),
                             (WD[0:FT[-1], NF - 1, :], w_down[FW * (NF - 1):DFF, :]),
                             (AD[0:FW, 0:NF - 1, :], a_down[0:FW * (NF - 1), :].rearrange("(f p) l -> p f l", p=FW)),
                             (AD[0:FT[-1], NF - 1, :], a_down[FW * (NF - 1):DFF, :])):
                sp.dma_start(dst, src).then_inc(ld_ffn, 16)
                n_ffn += 1
            assert n_ffn == 11
            for i, w in enumerate((wqT, wkT, wvT, waT)):
                sp.dma_start(W4[:, i, :, :], w.rearrange("(c p) n -> p c n", p=128)).then_inc(ld_attn, 16)
            for stored in base_stored + [kq_stored, kr_stored, bv_stored, a_stored, o_stored]:
                sp.sem_inc(stored, 16)
            with sp.Fori(0, NCH) as c:
                for q in range(4):
                    sp.wait_ge(base_ready, c * 4 + q + 1)
                    sp.dma_start(base_d[bass.ds(c * CH + 128 * q, 128), :], BASE[:, q % 2, :]).then_inc(base_stored[q % 2], 16)
            def store_chunk(c, which):
                for dst, tile, staged, count, stored in (
                        (kq_d, KQST, silu_done, c * NQ + 2 * NQ // 3 + 3, kq_stored),
                        (kr_d, KRST, kr_staged, c * (NQ // 3) + NQ // 3, kr_stored),
                        (bv_d, BVST, silu_done, c * NQ + NQ + 3, bv_stored),
                        (a_d, AST, job_free, c * NJ + NJ + 8, a_stored))[which]:
                    sp.wait_ge(staged, count)
                    sp.dma_start(dst[bass.ds(c * PSC, PSC)].rearrange("s k x -> k s x"),
                                 tile.rearrange("k (s x) -> k s x", s=PSC)).then_inc(stored, 16)

            with sp.Fori(0, NPC - 1) as c:
                store_chunk(c, slice(0, 4))
            store_chunk(NPC - 1, slice(0, 2))

            def load(n, c):
                for dst, src in ((KQf, kq_d), (KRf, kr_d), (BVf, bv_d), (Af, a_d)):
                    s = src[n] if isinstance(n, int) else src[bass.ds(n, 1)].rearrange("s k x -> k (s x)")
                    sp.dma_start(dst[c], s).then_inc(in_ready[c], 16)

            def store_outputs(n):
                sp.wait_ge(o_ready, n + 2)
                sp.dma_start(o_d[bass.ds(n, 1)].rearrange("s v x -> v (s x)"), OT).then_inc(o_stored, 16)

            for stored, chunks in ((kq_stored, NPC), (kr_stored, NPC), (bv_stored, NPC - 1), (a_stored, NPC - 1)):
                sp.wait_ge(stored, 16 * chunks + 16)
            load(0, 0)
            store_chunk(NPC - 1, slice(3, 4))
            store_chunk(NPC - 1, slice(2, 3))
            load(1, 1)
            for stored in (bv_stored, a_stored):
                sp.wait_ge(stored, 16 * NPC + 16)
            for stored in base_stored:
                sp.wait_ge(stored, 16 * NX // 2 + 16)
            sp.dma_start(WGT, wgT.rearrange("(c p) n -> p c n", p=128)).then_inc(ld_last, 16)
            with sp.Fori(0, NSUP // 2 - 1) as i:
                for c in range(2):
                    n = i * 2 + c
                    sp.wait_ge(x_step, n * C + C)
                    load(n + 2, c)
                    store_outputs(n)
            sp.wait_ge(x_step, (NSUP - 1) * C)
            load(0, 0)
            for c in range(2):
                sp.wait_ge(o_ready, NSUP - 2 + c + 2)
                sp.dma_start(o_d[NSUP - 2 + c], OT).then_inc(o_stored, 16)
            sp.wait_ge(o_stored, 16 * NSUP + 16)
            sp.wait_ge(wk_free, NWK * NSUP)
            sp.wait_ge(wk_full, NWK * NSUP + 2)
            sp.dma_start(WO, woT.rearrange("(h p) d -> p h d", p=128)).then_inc(ld_wo, 16)
            sp.dma_start(OC.rearrange("v (s x) -> v s x", s=OSC), o_d[0:OSC].rearrange("s v x -> v s x")).then_inc(oc_in, 16)
            sp.dma_start(BASEC[:, :, :], base_d[0:CH, :].rearrange("(q p) d -> p q d", p=128)).then_inc(base_in, 16)
            with sp.Fori(0, NCH - 1) as c:
                sp.wait_ge(cen_psum, c * H + H)
                sp.dma_start(OC.rearrange("v (s x) -> v s x", s=OSC), o_d[bass.ds(c * OSC + OSC, OSC)].rearrange("s v x -> v s x")).then_inc(oc_in, 16)
                for q in range(4):
                    sp.wait_ge(fin, c * 4 + q + 2)
                    sp.dma_start(out[bass.ds(c * CH + 128 * q, 128), :], BASEC[:, q, :]).then_inc(out_stored, 16)
                sp.wait_ge(out_stored, c * 64 + 64)
                sp.dma_start(BASEC[:, :, :], base_d[bass.ds(c * CH + CH, CH), :].rearrange("(q p) d -> p q d", p=128)).then_inc(base_in, 16)
            for q in range(4):
                sp.wait_ge(fin, (NCH - 1) * 4 + q + 2)
                sp.dma_start(out[(NCH - 1) * CH + 128 * q:(NCH - 1) * CH + 128 * (q + 1), :], BASEC[:, q, :]).then_inc(out_stored, 16)
            sp.wait_ge(out_stored, NCH * 64)

        @block.gpsimd
        def _(pool):
            pool.dma_start(SM[:, :], small).then_inc(ld_small, 16)
            nc.gpsimd.memset(ident[:, :], 0.0).then_inc(consts, 1)
            nc.gpsimd.memset(tri[:, :, :], 1.0).then_inc(consts, 1)
            nc.gpsimd.memset(ones[:, :], 1.0).then_inc(consts, 1)
            nc.gpsimd.memset(eps[:, :], 1e-5).then_inc(consts, 1)
            nc.gpsimd.memset(XNT[:, :, 0:HALO], 0.0).then_inc(consts, 1)
            pool.wait_ge(consts, 5)
            nc.gpsimd.affine_select(out=ident[:, :], in_=ident[:, :], compare_op=ALU.not_equal, fill=1.0,
                                    base=0, pattern=[[-1, 128]], channel_multiplier=1).then_inc(consts, 1)
            nc.gpsimd.affine_select(out=tri[:, :, :], in_=tri[:, :, :], compare_op=ALU.is_gt, fill=0.0,
                                    base=0, pattern=[[1, E], [-1, E]], channel_multiplier=0).then_inc(consts, 1)
            pool.wait_ge(job_full, NPC * NJ)
            nc.gpsimd.memset(S[:, :, :], 0.0).then_inc(zeros, 1)

        @block.scalar
        def _(act):
            act.wait_ge(consts, 4)
            for c in range(4):
                act.wait_ge(ln_var, c + 1)
                nc.scalar.activation(ST8[:, 2, 4 * c:4 * c + 4], ST8[:, 1, 4 * c:4 * c + 4], ACT.Sqrt,
                                     bias=eps[:, 0:1], scale=1.0 / D).then_inc(ln_std, 1)
                if c > 0:
                    for k in range(2):
                        act.wait_ge(xnT_psum, 2 * (c - 1) + k + 1)
                        nc.scalar.copy(XNT[:, k, HALO + CH * (c - 1):HALO + CH * c], bank(2 * (c - 1) + k)).then_inc(xnT_ready, 1)
            for k in range(2):
                act.wait_ge(xnT_psum, 6 + k + 1)
                nc.scalar.copy(XNT[:, k, HALO + CH * 3:HALO + CH * 4], bank(6 + k)).then_inc(xnT_ready, 1)
            act.wait_ge(logits, 1)
            nc.scalar.activation(SC[:, :, :], bank(0, 128).rearrange("p (n e) -> p n e", n=NX), ACT.Sigmoid).then_inc(scores, 1)
            for i in range(4):
                act.wait_ge(wT_psum, i + 1)
                nc.scalar.copy(WT[0:LR, CH * i:CH * (i + 1)], bank(1 + i)[0:LR, :]).then_inc(wT_ready, 1)
            with act.Fori(0, NCH) as c:
                for f in range(NF):
                    act.wait_ge(gu_psum, c * NF + f + 1)
                    if f >= 2:
                        act.wait_ge(hid_ready, c * NF + f - 1)
                    nc.scalar.activation(SG[0:FT[f], f % 2, :], bank(2 * (f % 2))[0:FT[f], :], ACT.Sigmoid).then_inc(gu_sig, 1)
            for stored in base_stored:
                act.wait_ge(stored, 16 * NX // 2 + 16)
            for _ in range(8):
                nc.scalar.nop().then_inc(job_free, 1)
            with act.Fori(0, NPC) as c:
                def job(g):
                    kind, h0, nh = JOBS[g]
                    act.wait_ge(job_full, c * NJ + g + 1)
                    bk = bank(g % 8)
                    if kind in "ab":
                        dst, bias = (BETA, BB) if kind == "b" else (AST, BA)
                        for k in range(nh):
                            ins = nc.scalar.activation(by_head(dst, h0 + k)[:, 0], bk[:, PC * k:PC * (k + 1)].rearrange("p (t b) -> p t b", b=B),
                                                       ACT.Sigmoid, bias=bias[:, h0 + k:h0 + k + 1])
                        ins.then_inc(job_free, 1)
                    else:
                        x, h = 4 * "qkv".index(kind) + h0 // 4, h0 % 4
                        nc.scalar.copy(PRE[:, x % 2, h, :], bk[:, 0:HALO + PC])
                        w = "qkv".index(kind)
                        nc.scalar.activation(ACC[:, x % 3, h, :], bk[:, HALO:HALO + PC], ACT.Identity, bias=CB[:, w, h0:h0 + 1],
                                             scale=CW[:, w, KC - 1, h0:h0 + 1]).then_inc(job_free, 1)

                def sigmoid(x):
                    act.wait_ge(tap_add, (c * NQ + x + 1) * (4 * TAPS))
                    nc.scalar.activation(SIG[:, x % 2], ACC[:, x % 3], ACT.Sigmoid).then_inc(sig_ready, 1)

                def stage_keys(x):
                    act.wait_ge(k_scaled, c * (NQ // 3) + x - NQ // 3 + 1)
                    if x == NQ // 3:
                        act.wait_ge(kr_stored, c * 16 + 16)
                    for h in range(4):
                        hh = 4 * (x - NQ // 3) + h
                        ins = nc.scalar.copy(KRST.rearrange("k (s g t b h) -> k g h s t b", s=PSC, g=2, b=B, h=8)[:, hh // 8, hh % 8],
                                             ACC[:, x % 3, h, :].rearrange("k (s t b) -> k s t b", s=PSC, b=B))
                    ins.then_inc(kr_staged, 1)

                for x in range(NQ):
                    act.wait_ge(silu_done, c * NQ + x + 1)
                    if NQ // 3 <= x - 3 < 2 * NQ // 3:
                        act.wait_ge(kr_staged, c * (NQ // 3) + x - 3 - NQ // 3 + 1)
                    for h in range(4):
                        job(FIRST[x] + h)
                    if x == 0:
                        act.wait_ge(silu_done, c * NQ + 3)
                    if x == NQ // 3:
                        act.wait_ge(a_stored, c * 16 + 16)
                    for g in EXTRA[x]:
                        job(g)
                    if x > 0:
                        sigmoid(x - 1)
                    if NQ // 3 <= x - 2 < 2 * NQ // 3:
                        stage_keys(x - 2)
                sigmoid(NQ - 1)
            act.wait_ge(zeros, 6)
            nc.scalar.nop().then_inc(o_ready, 1)
            for _ in range(8):
                nc.scalar.nop().then_inc(ptz_ready, 1)
            with act.Fori(0, NSUP // 2) as i:
                for c in range(2):
                    n = i * 2 + c
                    d = 1 - c

                    def copies(k):
                        j = k - 2
                        if 0 <= j < NR:
                            u, r = divmod(j, 4)
                            act.wait_ge(ro_psum, n * NR + j + 1)
                            for e in range(2):
                                ins = nc.scalar.copy(X[d].rearrange("v i (u a r e) -> v u r e a i", u=4, a=2, r=4)[:, u, r, e],
                                                     bank(5).rearrange("v (a e i q) -> v e q a i", a=2, e=2, q=4)[:, e, 2 * (r % 2) + e])
                            ins.then_inc(x_ready, 1)
                        j = k - 1
                        if 0 <= j < NR:
                            act.wait_ge(st_psum, n * NR + j + 1)
                            if j >= 2:
                                act.wait_ge(ro_psum, n * NR + j - 1)
                            nc.scalar.copy(STR[:, j % 2], bank(6).rearrange("k (a e v) -> k a e v", a=2, e=2)).then_inc(st_ready, 1)

                    def decay(k):
                        if k < NR:
                            u, r = divmod(k, 4)
                            act.wait_ge(s_updated, n * NR + k + 1)
                            for a in range(2):
                                for e in range(2):
                                    p = 16 * u + 8 * a + 2 * r + e
                                    ins = nc.scalar.mul(S[:, p, :], S[:, p, :], ACH[c][:, p:p + 1])
                            ins.then_inc(s_scaled, 1)

                    act.wait_ge(in_ready[c], i * 64 + 64)
                    nc.scalar.copy(KP.rearrange("k (a p) t -> k a t p", a=2), KR[c]).then_inc(kp_ready, 1)
                    act.wait_ge(o_ready, n + 1)
                    for m in range(NB):
                        for k in SLOTS[m]:
                            if m < NB - 1 and k == SLOTS[m][-1]:
                                act.wait_ge(wht_psum, n * 3 + m + 1)
                                nc.scalar.copy(WHT, bank(0, 256)).then_inc(wht_ready, 1)
                            copies(k)
                            decay(k)
                        if m < 2:
                            act.wait_ge(kt_psum, n * 2 + m + 1)
                            for s in range(4):
                                for e in range(2):
                                    ins = nc.scalar.mul(KTB[c][:, 4 * m + s, e, :], bank(0)[:, DH * s:DH * (s + 1)], maskKT[:, e:e + 1])
                            ins.then_inc(kt_ready, 1)
                    for k in range(2):
                        act.wait_ge(pt_psum, n * 2 + k + 1)
                        nc.scalar.copy(PT[:, 4 * k:4 * k + 4, :], bank(7 * k).rearrange("r (s v) -> r s v", s=4)).then_inc(pt_ready, 1)
                    act.wait_ge(pt_ready, n * 2 + 2)
                    for k in range(2):
                        for g in range(4):
                            nc.scalar.mul(PTZ[:, g, 4 * k:4 * k + 4, :], PT[:, 4 * k:4 * k + 4, :], mask4[:, g:g + 1]).then_inc(ptz_ready, 1)
                    act.wait_ge(x_step, n * C + C)
                    act.wait_ge(o_stored, n * 16 + 16)
                    nc.scalar.copy(OT.rearrange("v (t p) -> v t p", p=NP), X[c].rearrange("v (t e) p -> v e t p", e=2)[:, 1]).then_inc(o_ready, 1)
            act.wait_ge(o_stored, 16 * NSUP + 16)
            for h in range(H):
                act.wait_ge(gate_psum, h + 1)
                nc.scalar.copy(GATE[:, h, :], bank(h % 4)).then_inc(gate_raw, 1)

            def gate_sigmoid(q, count):
                act.wait_ge(gate_raw, count)
                g = GATE[:, 4 * q:4 * q + 4, :]
                nc.scalar.activation(g, g, ACT.Sigmoid).then_inc(gate_ready, 1)

            def project_out(c, more):
                for h in range(H + 4 if more else H + 2):
                    if h < H:
                        act.wait_ge(cen_psum, c * H + h + 1)
                        nc.scalar.activation(SQO[:, h % 2, :], bank(h % 3), ACT.Square).then_inc(squared, 1)
                    if 0 <= h - 1 < H:
                        act.wait_ge(var_psum, c * H + h)
                        nc.scalar.activation(STD[:, (h - 1) % 2, :], bank(4 + (h - 1) % 2), ACT.Sqrt, bias=eps[:, 0:1], scale=1.0 / DH).then_inc(std, 1)
                    if 0 <= h - 2 < H:
                        act.wait_ge(normed, c * H + h - 1)
                        nc.scalar.activation(AFF[:, h % 2, :], NRM[:, h % 2, :], ACT.Identity, bias=LNB, scale=LNG).then_inc(affine, 1)
                    if more and 0 <= h - 4:
                        j = h - 4
                        act.wait_ge(gate_psum, (c + 1) * H + j + 1)
                        act.wait_ge(gated, c * H + j + 1)
                        nc.scalar.copy(GATE[:, j, :], bank(3)).then_inc(gate_raw, 1)
                        if h >= H + 2:
                            q = h - H - 2
                            gate_sigmoid(q, (c + 1) * H + 4 * q + 4)
                act.wait_ge(y_step, c * H + H)
                for dh in range(2):
                    nc.scalar.copy(YT[:, dh, :], bank(6 + dh)).then_inc(y_ready, 1)
                if more:
                    for q in range(2, 4):
                        gate_sigmoid(q, (c + 1) * H + 4 * q + 4)

            for q in range(4):
                gate_sigmoid(q, 4 * q + 4)
            with act.Fori(0, NCH - 1) as c:
                project_out(c, True)
            project_out(NCH - 1, False)

        @block.vector
        def _(dve):
            tt = nc.vector.tensor_tensor
            for c in range(4):
                cs = slice(4 * c, 4 * c + 4)
                dve.wait_ge(ld_x[c], 16)
                nc.vector.tensor_reduce(ST8[:, 0, cs], XIN[:, cs, :], AX.X, ALU.add).then_inc(ln_step, 1)
                dve.wait_ge(ln_step, 5 * c + 1)
                nc.vector.tensor_scalar(ST8[:, 3, cs], ST8[:, 0, cs], -1.0 / D, None, ALU.mult).then_inc(ln_step, 1)
                dve.wait_ge(ln_step, 5 * c + 2)
                tt(XN[:, cs, :], XIN[:, cs, :], ST8[:, 3, cs].unsqueeze(2).to_broadcast([128, 4, D]), ALU.add).then_inc(ln_step, 1)
                dve.wait_ge(ln_step, 5 * c + 3)
                tt(SQ.rearrange("p (n d) -> p n d", n=4), XN[:, cs, :], XN[:, cs, :], ALU.mult).then_inc(ln_step, 1)
                dve.wait_ge(ln_step, 5 * c + 4)
                nc.vector.tensor_reduce(ST8[:, 1, cs], SQ.rearrange("p (n d) -> p n d", n=4), AX.X, ALU.add).then_inc(ln_var, 1)
                dve.wait_ge(ln_std, c + 1)
                nc.vector.reciprocal(ST8[:, 4, cs], ST8[:, 2, cs]).then_inc(ln_step, 1)
                dve.wait_ge(ln_step, 5 * c + 5)
                tt(XN[:, cs, :], XN[:, cs, :], ST8[:, 4, cs].unsqueeze(2).to_broadcast([128, 4, D]), ALU.mult).then_inc(xn_ready, 1)
            dve.wait_ge(consts, 7)
            nc.vector.tensor_reduce(maskG[:, :], ident[:, :].rearrange("r (j p) -> r p j", p=HALF), AX.X, ALU.add).then_inc(masks, 1)
            nc.vector.tensor_reduce(mask8[:, :], ident[:, :].rearrange("r (p t) -> r p t", p=8), AX.X, ALU.add).then_inc(masks, 1)
            nc.vector.tensor_reduce(mask4[:, :], ident[:, :].rearrange("r (g x) -> r g x", g=4), AX.X, ALU.add).then_inc(masks, 1)
            nc.vector.tensor_reduce(maskKT[:, :], ident[:, :].rearrange("r (g e i) -> r e g i", g=4, e=2), AX.XY, ALU.add).then_inc(masks, 1)
            dve.wait_ge(ld_small, 16)
            dve.wait_ge(scores, 1)
            steps = [0]

            def link(ins):
                ins.then_inc(rt_step, 1)
                steps[0] += 1
                dve.wait_ge(rt_step, steps[0])

            link(tt(BI[:, :, :], SC[:, :, :], EB.unsqueeze(1).to_broadcast([128, NX, E]), ALU.add))
            other = BI.unsqueeze(2).to_broadcast([128, NX, E, E])
            own = BI.unsqueeze(3).to_broadcast([128, NX, E, E])
            dve.wait_ge(xnT_ready, 8)
            link(tt(GT, other, own, ALU.is_gt))
            link(tt(EQ, other, own, ALU.is_equal))
            link(tt(EQ, EQ, tri[:, :, :].unsqueeze(1).to_broadcast([128, NX, E, E]), ALU.mult))
            link(tt(GT, GT, EQ, ALU.add))
            link(nc.vector.tensor_reduce(RK[:, :, :], GT, AX.X, ALU.add))
            link(nc.vector.tensor_scalar(RK[:, :, :], RK[:, :, :], 1.5, None, ALU.is_lt))
            link(tt(RK[:, :, :], RK[:, :, :], SC[:, :, :], ALU.mult))
            link(nc.vector.tensor_reduce(ST8[:, 5, :], RK[:, :, :], AX.X, ALU.add))
            link(nc.vector.tensor_scalar(ST8[:, 5, :], ST8[:, 5, :], 1e-8, None, ALU.add))
            link(nc.vector.reciprocal(ST8[:, 6, :], ST8[:, 5, :]))
            link(nc.vector.tensor_scalar(ST8[:, 6, :], ST8[:, 6, :], 1.0 / R, None, ALU.mult))
            link(tt(RK[:, :, :], RK[:, :, :], ST8[:, 6, :].unsqueeze(2).to_broadcast([128, NX, E]), ALU.mult))
            link(nc.vector.memset(WEXP[:, :, E * R:LR], 1.0 / R))
            link(nc.vector.tensor_copy(WEXP[:, :, 0:E * R].rearrange("p n (e r) -> p n e r", e=E),
                                       RK.unsqueeze(3).to_broadcast([128, NX, E, R])))
            assert steps[0] == 15
            dve.wait_ge(wT_ready, 4)
            nc.vector.nop().then_inc(had_ready, 1)
            with dve.Fori(0, NCH) as c:
                wt = WT[0:LR, bass.ds(c * CH, CH)]
                for k, dst in enumerate((XAG, XAU)):
                    dve.wait_ge(xa_psum, c * 2 + k + 1)
                    tt(dst[0:LR, :], bank(4 + k)[0:LR, :], wt, ALU.mult).then_inc(xa_ready, 1)
                for f in range(NF):
                    fr = slice(0, FT[f])
                    dve.wait_ge(gu_sig, c * NF + f + 1)
                    tt(SG[fr, f % 2, :], SG[fr, f % 2, :], bank(2 * (f % 2))[fr, :], ALU.mult).then_inc(gu_silu, 1)
                    dve.wait_ge(gu_silu, c * NF + f + 1)
                    tt(HID[fr, f, :], SG[fr, f % 2, :], bank(2 * (f % 2) + 1)[fr, :], ALU.mult).then_inc(hid_ready, 1)
                dve.wait_ge(had_psum, c + 1)
                tt(HAD[0:LR, :], bank(5)[0:LR, :], wt, ALU.mult).then_inc(had_ready, 1)
                for q in range(4):
                    dve.wait_ge(ffn_psum, c * 4 + q + 1)
                    dve.wait_ge(base_stored[q % 2], c * 32 + 16 * (q // 2) + 16)
                    tt(BASE[:, q % 2, :], bank(6 + q % 2, D), XIN[:, bass.ds(c * 4 + q, 1), :].rearrange("p a d -> p (a d)"), ALU.add).then_inc(base_ready, 1)
            for _ in range(3):
                nc.vector.nop().then_inc(silu_done, 1)
            with dve.Fori(0, NPC) as c:
                def conv(x):
                    kind = JOBS[FIRST[x]][0]
                    w = "qkv".index(kind)
                    dve.wait_ge(job_free, c * NJ + 8 + FIRST[x] + 4)
                    for i in range(TAPS):
                        for h in range(4):
                            hh = 4 * (x % (NQ // 3)) + h
                            if i > 0:
                                dve.wait_ge(tap_add, (c * NQ + x) * (4 * TAPS) + 4 * (i - 1) + h + 1)
                            acc = ACC[:, x % 3, h, :]
                            nc.vector.scalar_tensor_tensor(acc, PRE[:, x % 2, h, B * i:B * i + PC], CW[:, w, i, hh:hh + 1], acc, ALU.mult, ALU.add).then_inc(tap_add, 1)

                def finish(x):
                    kind, h0, _ = JOBS[FIRST[x]]
                    acc, sig = ACC[:, x % 3], SIG[:, x % 2]
                    acc_t = acc.rearrange("p h (t b) -> p h t b", b=B)
                    dve.wait_ge(sig_ready, c * NQ + x + 1)
                    if kind == "q":
                        if x == 0:
                            dve.wait_ge(kq_stored, c * 16 + 16)
                        tt(by_head(KQST, h0, 4, 2, 1), acc_t, sig.rearrange("p h (t b) -> p h t b", b=B), ALU.mult).then_inc(silu_done, 1)
                    elif kind == "k":
                        nc.vector.scalar_tensor_tensor(acc, sig, K_SCALE, acc, ALU.mult, ALU.mult).then_inc(k_scaled, 1)
                        dve.wait_ge(k_scaled, c * (NQ // 3) + x - NQ // 3 + 1)
                        tt(by_head(KQST, h0, 4, 2, 0), acc_t, by_head(BETA, h0, 4), ALU.mult).then_inc(silu_done, 1)
                    else:
                        tt(acc, acc, sig, ALU.mult).then_inc(v_silu, 1)
                        dve.wait_ge(v_silu, c * (NQ // 3) + x - 2 * NQ // 3 + 1)
                        if x == 2 * NQ // 3:
                            dve.wait_ge(bv_stored, c * 16 + 16)
                        tt(by_head(BVST, h0, 4), acc_t, by_head(BETA, h0, 4), ALU.mult).then_inc(silu_done, 1)

                for x in range(NQ):
                    conv(x)
                    if x > 0:
                        finish(x - 1)
                finish(NQ - 1)

            def decays(base, c):
                A4 = Af[c].rearrange("v (m j p) -> v m j p", m=NB, j=BL)
                nc.vector.tensor_copy(SFX[c][:, :, 2, :], A4[:, :, 3, :]).then_inc(sfx, 1)
                tt(SFX[c][:, :, 1, :], A4[:, :, 2, :], A4[:, :, 3, :], ALU.mult).then_inc(sfx, 1)
                dve.wait_ge(sfx, base + 2)
                tt(SFX[c][:, :, 0, :], A4[:, :, 1, :], SFX[c][:, :, 1, :], ALU.mult).then_inc(sfx, 1)
                dve.wait_ge(sfx, base + 3)
                tt(ABL[c], A4[:, :, 0, :], SFX[c][:, :, 0, :], ALU.mult).then_inc(sfx, 1)
                dve.wait_ge(sfx, base + 4)
                nc.vector.tensor_copy(ASF[c][:, 2, :], ABL[c][:, 3, :]).then_inc(sfx, 1)
                tt(ASF[c][:, 1, :], ABL[c][:, 2, :], ABL[c][:, 3, :], ALU.mult).then_inc(sfx, 1)
                dve.wait_ge(sfx, base + 6)
                tt(ASF[c][:, 0, :], ABL[c][:, 1, :], ASF[c][:, 1, :], ALU.mult).then_inc(sfx, 1)
                dve.wait_ge(sfx, base + 7)
                tt(ACH[c], ABL[c][:, 0, :], ASF[c][:, 0, :], ALU.mult).then_inc(sfx, 1)

            def prods(m, j, c):
                t = BL * m + j
                e, hi = 2 * t + 1, 2 * BL * (m + 1)
                tt(PR[:, OFF[j]:OFF[j] + hi - e, :].rearrange("k i (a p) -> k a i p", a=2), KQ[c][:, e:hi, :].rearrange("k i (a p) -> k a i p", a=2),
                   KR[c][:, :, t, :].unsqueeze(2).to_broadcast([128, 2, hi - e, HALF]), ALU.mult).then_inc(prod_ready, 1)

            dve.wait_ge(job_full, NPC * NJ)
            for tile in (PTZ[:, :, :, :], KTBf[1], Xf[0]):
                nc.vector.memset(tile, 0.0).then_inc(zeros, 1)
            dve.wait_ge(bv_stored, 16 * NPC + 16)
            dve.wait_ge(a_stored, 16 * NPC + 16)
            dve.wait_ge(in_ready[0], 64)
            for c in range(2):
                nc.vector.memset(ASF[c][:, NB - 1, :], 1.0).then_inc(zeros, 1)
            dve.wait_ge(zeros, 6)
            decays(0, 0)
            for j in range(BL):
                prods(0, j, 0)
            with dve.Fori(0, NSUP // 2) as i:
                for c in range(2):
                    n = i * 2 + c
                    d = 1 - c
                    Xc = X[c]
                    wk = n * NWK

                    def mask_piece(m, u):
                        if m < NB - 1:
                            half, a, b = PIECES[m][u]
                            k = WK0[m] + u
                            dve.wait_ge(wk_full, wk + k + 1)
                            tt(GBD[:, half, a - 8:b - 8, :], bank(3 + k % 2)[:, 0:HALF * (b - a)].rearrange("r (i p) -> r i p", p=HALF),
                               maskG[:, :].unsqueeze(1).to_broadcast([128, b - a, HALF]), ALU.mult).then_inc(wk_free, 1)
                        else:
                            k = WK0[m] + u
                            dve.wait_ge(wk_full, wk + k + 1)
                            tt(G2[:, 2 * u:2 * u + 2].rearrange("r s i p -> r (s i) p"), bank(3 + k % 2).rearrange("r (x p) -> r x p", p=8),
                               mask8[:, :].unsqueeze(1).to_broadcast([128, 2 * NI, 8]), ALU.mult).then_inc(wk_free, 1)

                    def add_updates(m, at):
                        for k, x in zip(SLOTS[m], ADD_AT[m]):
                            if x == at and k < NR:
                                u, r = divmod(k, 4)
                                dve.wait_ge(up_psum, n * NR + k + 1)
                                sv = Sr[:, u, r].rearrange("v a e k -> v a (e k)")
                                tt(sv, sv, bank(7).rearrange("v (a x) -> v a x", a=2), ALU.add).then_inc(s_updated, 1)

                    for m in range(NB):
                        hi = 2 * BL * (m + 1)
                        for j in range(BL):
                            t = BL * m + j
                            e = 2 * t + 1
                            if j > 0:
                                dve.wait_ge(x_step, n * C + t)
                            tt(W[:, :, t, :], BV[c][:, t, :].rearrange("v (a p) -> v a p", a=2), Xc[:, 2 * t, :].rearrange("v (a p) -> v a p", a=2), ALU.subtract).then_inc(w_ready, 1)
                            tt(Xc[:, e:hi, :], Xc[:, e:hi, :], A[c][:, t, :].unsqueeze(1).to_broadcast([128, hi - e, NP]), ALU.mult).then_inc(x_decayed, 1)
                            for u in range(NPIECE[m] if m < NB - 1 else NXP):
                                if (min(u + 1, BL - 1) if m > 0 else u) == j:
                                    mask_piece(m, u)
                            add_updates(m, (j, 0))
                            if j == 0:
                                dve.wait_ge(bcast_psum, n * 8 + 2 * m + 2)
                            dve.wait_ge(w_ready, n * C + t + 1)
                            g = PS[:, 512:1536].rearrange("v (a i p) -> v a i p", a=2, p=HALF)[:, :, OFF[j]:OFF[j] + hi - e, :]
                            wb = W[:, :, t, :].unsqueeze(2).to_broadcast([128, 2, hi - e, HALF])
                            tt(TT[:, :, 0:hi - e, :], g, wb, ALU.mult).then_inc(wg_ready, 1)
                            if m < NB - 1:
                                prods(m + 1, j, c)
                            else:
                                if j == 0:
                                    dve.wait_ge(in_ready[d], (i + 1 + c) * 64)
                                prods(0, j, d)
                            dve.wait_ge(wg_ready, n * C + t + 1)
                            dve.wait_ge(x_decayed, n * C + t + 1)
                            xs = Xc[:, e:hi, :].rearrange("v i (a p) -> v a i p", a=2)
                            tt(xs, xs, TT[:, :, 0:hi - e, :], ALU.add).then_inc(x_step, 1)
                            add_updates(m, (j, 1))
                        wl = W[:, :, BL * m:BL * m + 3, :]
                        tt(wl, wl, SFX[c][:, m, :, :].rearrange("v j (a p) -> v a j p", a=2), ALU.mult).then_inc(what_ready, 1)
                        if m < NB - 1:
                            tt(Xc[:, hi:NI, :], Xc[:, hi:NI, :], ABL[c][:, m, :].unsqueeze(1).to_broadcast([128, NI - hi, NP]), ALU.mult).then_inc(x_blk, 1)
                            add_updates(m, (BL - 1, 2))
                            dve.wait_ge(x_blk, n * 3 + m + 1)
                            for u, (half, a, b) in enumerate(PIECES[m]):
                                k = WK0[m] + NPIECE[m] + u
                                dve.wait_ge(wk_full, wk + k + 1)
                                xs = Xc[:, a:b, HALF * half:HALF * (half + 1)]
                                tt(xs, xs, bank(3 + k % 2)[:, 0:HALF * (b - a)].rearrange("v (i p) -> v i p", p=HALF), ALU.add).then_inc(wk_free, 1)
                            dve.wait_ge(wk_free, wk + WK0[m + 1])
                    dve.wait_ge(what_ready, n * NB + NB)
                    for a in range(2):
                        ps = slice(HALF * a, HALF * (a + 1))
                        tt(PP[:, ps, :].rearrange("v p (m j) -> v m j p", j=BL), W[:, a, :, :].rearrange("v (m j) p -> v m j p", j=BL),
                           ASF[c][:, :, ps].unsqueeze(2).to_broadcast([128, NB, BL, HALF]), ALU.mult).then_inc(p_ready, 1)
                    decays(n * 8 + 8, d)
                    dve.wait_ge(x_ready, n * NR + NR)
                    for u in range(NXP):
                        k = WK0[NB - 1] + NXP + u
                        dve.wait_ge(wk_full, wk + k + 1)
                        xs = X[d][:, :, 16 * u:16 * u + 16].rearrange("v i (a p) -> v a i p", a=2)
                        tt(xs, xs, bank(3 + u).rearrange("v (a i p) -> v a i p", a=2, p=8), ALU.add).then_inc(wk_free, 1)
                    dve.wait_ge(wk_free, wk + NWK)
            nc.vector.nop().then_inc(fin, 1)
            dve.wait_ge(oc_in, 16)
            nc.vector.tensor_scalar(centre, ident[:, :], -1.0 / DH, None, ALU.add).then_inc(centre_ready, 1)
            with dve.Fori(0, NCH) as c:
                for h in range(H + 1):
                    if h < H:
                        dve.wait_ge(std, c * H + h + 1)
                        nc.vector.reciprocal(RSTD[:, h % 2, :], STD[:, h % 2, :]).then_inc(rstd, 1)
                        dve.wait_ge(rstd, c * H + h + 1)
                        tt(NRM[:, h % 2, :], bank(h % 3), RSTD[:, h % 2, :], ALU.mult).then_inc(normed, 1)
                    if h > 0:
                        j = h - 1
                        dve.wait_ge(affine, c * H + j + 1)
                        if j % 4 == 0:
                            dve.wait_ge(gate_ready, c * 4 + j // 4 + 1)
                        if j >= 2:
                            dve.wait_ge(y_step, c * H + j - 1)
                        tt(Z[:, j % 2, :], AFF[:, j % 2, :], GATE[:, j, :], ALU.mult).then_inc(gated, 1)
                dve.wait_ge(base_in, c * 16 + 16)
                for q in range(4):
                    dve.wait_ge(yt_psum, c * 4 + 2 * (q // 2) + 2)
                    tt(BASEC[:, q, :], bank(4 + q // 2)[:, D * (q % 2):D * (q % 2 + 1)], BASEC[:, q, :], ALU.add).then_inc(fin, 1)

        @block.tensor
        def _(pe):
            mm = nc.tensor.matmul
            pe.wait_ge(consts, 7)
            for c in range(4):
                pe.wait_ge(xn_ready, c + 1)
                for k in range(2):
                    for i in range(4):
                        ins = nc.tensor.transpose(bank(2 * c + k)[:, 128 * i:128 * (i + 1)], XN[:, 4 * c + i, 128 * k:128 * (k + 1)], ident[:, :])
                    ins.then_inc(xnT_psum, 1)
            pe.wait_ge(ld_small, 16)
            pe.wait_ge(xnT_ready, 8)
            for i in range(NX):
                for k in range(2):
                    ins = mm(bank(0)[:, E * i:E * (i + 1)], XNT[:, k, HALO + 128 * i:HALO + 128 * (i + 1)], WR[:, k, :], start=(k == 0), stop=(k == 1))
            ins.then_inc(logits, 1)
            pe.wait_ge(rt_step, 15)
            for i in range(NX):
                ins = nc.tensor.transpose(bank(1 + i // 4)[0:LR, 128 * (i % 4):128 * (i % 4 + 1)], WEXP[:, i, :], ident[:, :])
                if i % 4 == 3:
                    ins.then_inc(wT_psum, 1)
            pe.wait_ge(ld_ffn, 16 * 11)
            pe.wait_ge(wT_ready, 4)
            with pe.Fori(0, NCH) as c:
                xs = [XNT[:, k, bass.ds(c * CH + HALO, CH)] for k in range(2)]
                for j, a in enumerate((AG, AU)):
                    pe.wait_ge(had_ready, c + 1)
                    for k in range(2):
                        ins = mm(bank(4 + j)[0:LR, :], a[:, k, :], xs[k], start=(k == 0), stop=(k == 1))
                    ins.then_inc(xa_psum, 1)
                for f in range(NF):
                    if f >= 2:
                        pe.wait_ge(hid_ready, c * NF + f - 1)
                    fs = slice(FW * f, FW * f + FT[f])
                    for j, (w, b, xa) in enumerate(((WG, BG, XAG), (WU, BU, XAU))):
                        o = bank(2 * (f % 2) + j)[0:FT[f], :]
                        for k in range(2):
                            mm(o, w[:, k, fs], xs[k], start=(k == 0), stop=False)
                        if f == 0:
                            pe.wait_ge(xa_ready, c * 2 + j + 1)
                        ins = mm(o, b[0:LR, fs], xa[0:LR, :], start=False, stop=True)
                    ins.then_inc(gu_psum, 1)
                for f in range(NF):
                    pe.wait_ge(hid_ready, c * NF + f + 1)
                    ins = mm(bank(5)[0:LR, :], AD[0:FT[f], f, :], HID[0:FT[f], f, :], start=(f == 0), stop=(f == NF - 1))
                ins.then_inc(had_psum, 1)
                for q in range(4):
                    if q >= 2:
                        pe.wait_ge(base_ready, c * 4 + q - 1)
                    for f in range(NF):
                        mm(bank(6 + q % 2, D), HID[0:FT[f], f, 128 * q:128 * (q + 1)], WD[0:FT[f], f, :], start=(f == 0), stop=False)
                    if q == 0:
                        pe.wait_ge(had_ready, c + 2)
                    mm(bank(6 + q % 2, D), HAD[0:LR, 128 * q:128 * (q + 1)], BD[0:LR, :], start=False, stop=True).then_inc(ffn_psum, 1)
            pe.wait_ge(base_ready, NX)
            pe.wait_ge(ld_attn, 16 * 4)
            with pe.Fori(0, NPC) as c:
                for g, (kind, h0, nh) in enumerate(JOBS):
                    pe.wait_ge(job_free, c * NJ + g + 1)
                    cols = HALO + PC if kind in "qkv" else PC
                    for k in range(nh):
                        for kt in range(2):
                            if kind == "b":
                                w = WB[:, kt, h0 + k:h0 + k + 1].to_broadcast([128, 128])
                            else:
                                w = W4[:, WSLOT[kind], kt, DH * (h0 + k):DH * (h0 + k + 1)]
                            ins = mm(bank(g % 8)[:, cols * k:cols * (k + 1)], w,
                                     XNT[:, kt, bass.ds(c * PC + (HALO + PC - cols), cols)], start=(kt == 0), stop=(kt == 1))
                    ins.then_inc(job_full, 1)

            def broadcast_products(prod_count):
                pe.wait_ge(prod_ready, prod_count)
                for a in range(2):
                    mm(bank(1 + a).rearrange("v (i p) -> v i p", p=HALF), ones[:, :], PR[:, :, HALF * a:HALF * (a + 1)], start=True, stop=True).then_inc(bcast_psum, 1)

            def key_products(m, u, c):
                half, a, b = PIECES[m][u]
                k = WK0[m] + u
                mm(bank(3 + k % 2)[:, 0:HALF * (b - a)].rearrange("r (i p) -> r i p", p=HALF), KR[c][:, half, BL * m:BL * (m + 1), :].rearrange("k t p -> k (t p)"),
                   KQ[c][:, a:b, HALF * half:HALF * (half + 1)], start=True, stop=True).then_inc(wk_full, 1)

            pe.wait_ge(in_ready[0], 64)
            pe.wait_ge(zeros, 6)
            broadcast_products(BL)
            for u in range(2):
                key_products(0, u, 0)
            with pe.Fori(0, NSUP // 2) as i:
                for c in range(2):
                    n = i * 2 + c
                    d = 1 - c
                    wk = n * NWK

                    def update(k):
                        if k < NR:
                            u, r = divmod(k, 4)
                            if k > 0:
                                pe.wait_ge(s_updated, n * NR + k)
                            if u % 2 == 0:
                                pe.wait_ge(ptz_ready, n * 8 + 4 * (u // 2) + r + 1)
                            for a in range(2):
                                s = 2 * u + a
                                ins = mm(bank(7)[:, 256 * a:256 * (a + 1)], PTZ[:, r, s, :], KTB[d][:, s].rearrange("r e k -> r (e k)"), start=True, stop=True)
                            ins.then_inc(up_psum, 1)

                    def read(k):
                        j = k - 2
                        if 0 <= j < NR:
                            u, r = divmod(j, 4)
                            if j == 0:
                                pe.wait_ge(in_ready[d], (i + 1 + c) * 64)
                            else:
                                pe.wait_ge(x_ready, n * NR + j)
                            pe.wait_ge(st_ready, n * NR + j + 1)
                            for a in range(2):
                                for e in range(2):
                                    q = 2 * a + e
                                    p0 = 16 * u + 8 * a + 4 * (r // 2)
                                    ins = mm(bank(5)[:, 4 * NI * q:4 * NI * (q + 1)].rearrange("v (i p) -> v i p", p=4), STR[:, j % 2, a, e, :],
                                             KQ[d][:, :, p0:p0 + 4], start=True, stop=True)
                            ins.then_inc(ro_psum, 1)
                        j = k - 1
                        if 0 <= j < NR:
                            u, r = divmod(j, 4)
                            pe.wait_ge(s_scaled, n * NR + j + 1)
                            if j > 0:
                                pe.wait_ge(st_ready, n * NR + j)
                            for a in range(2):
                                for e in range(2):
                                    q = 2 * a + e
                                    ins = nc.tensor.transpose(bank(6)[:, DH * q:DH * (q + 1)], Sr[:, u, r, a, e, :], ident[:, :])
                            ins.then_inc(st_psum, 1)

                    def products(m, u):
                        k = WK0[m] + u
                        pe.wait_ge(wk_free, wk + k - 1)
                        if m < NB - 1:
                            key_products(m, u, c)
                        else:
                            for a in range(2):
                                s = 2 * u + a
                                ins = mm(bank(3 + k % 2)[:, 256 * a:256 * (a + 1)].rearrange("r (i p) -> r i p", p=8), KP[:, 8 * s:8 * s + 8, :].rearrange("k p t -> k (p t)"),
                                         KQ[d][:, :, 8 * s:8 * s + 8], start=True, stop=True)
                            ins.then_inc(wk_full, 1)

                    for m in range(NB):
                        pieces = NPIECE[m] if m < NB - 1 else NXP
                        late = 1 if m > 0 else 0
                        for x, k in enumerate(SLOTS[m]):
                            update(k)
                            if m < NB - 1 and k == SLOTS[m][-1]:
                                if m > 0:
                                    pe.wait_ge(kt_ready, n * 2 + m)
                                pe.wait_ge(what_ready, n * NB + m + 1)
                                for a in range(2):
                                    ins = nc.tensor.transpose(bank(0)[:, 128 * a:128 * (a + 1)], W[:, a, BL * m:BL * (m + 1), :].rearrange("v t p -> v (t p)"), ident[:, :])
                                ins.then_inc(wht_psum, 1)
                            read(k)
                            if x >= late and 2 + x - late < pieces:
                                products(m, 2 + x - late)
                        if m < NB - 1:
                            pe.wait_ge(wht_ready, n * 3 + m + 1)
                            for u, (half, a, b) in enumerate(PIECES[m]):
                                k = WK0[m] + NPIECE[m] + u
                                pe.wait_ge(wk_free, wk + k - 1)
                                mm(bank(3 + k % 2)[:, 0:HALF * (b - a)].rearrange("r (i p) -> r i p", p=HALF), WHT[:, 128 * half:128 * (half + 1)], GBD[:, half, a - 8:b - 8, :],
                                   start=True, stop=True).then_inc(wk_full, 1)
                            pe.wait_ge(wg_ready, n * C + BL * (m + 1))
                            broadcast_products(n * C + BL * (m + 2))
                            if m < 2:
                                pe.wait_ge(kp_ready, n + 1)
                                for s in range(4):
                                    ins = nc.tensor.transpose(bank(0)[:, 128 * s:128 * (s + 1)], KP[:, 8 * (4 * m + s):8 * (4 * m + s) + 8, :].rearrange("k q t -> k (q t)"), ident[:, :])
                                ins.then_inc(kt_psum, 1)
                            for u in range(2):
                                products(m + 1, u)
                        else:
                            pe.wait_ge(wg_ready, n * C + C)
                            broadcast_products(n * C + C + BL)
                            pe.wait_ge(s_updated, n * NR + NR)
                            pe.wait_ge(p_ready, n * 2 + 2)
                            for s in range(8):
                                ins = nc.tensor.transpose(bank(7 * (s // 4))[:, 128 * (s % 4):128 * (s % 4 + 1)], PP[:, 8 * s:8 * s + 8, :].rearrange("v q t -> v (q t)"), ident[:, :])
                                if s % 4 == 3:
                                    ins.then_inc(pt_psum, 1)
                            pe.wait_ge(pt_ready, n * 2 + 2)
                            for u in range(NXP):
                                k = WK0[m] + NXP + u
                                if u < 2:
                                    pe.wait_ge(wk_free, wk + k - 1)
                                elif u == 2:
                                    pe.wait_ge(x_ready, n * NR + NR)
                                for a in range(2):
                                    s = 2 * u + a
                                    ins = mm(bank(3 + u)[:, 256 * a:256 * (a + 1)], PT[:, s, :], G2[:, s].rearrange("r i p -> r (i p)"), start=True, stop=True)
                                ins.then_inc(wk_full, 1)
                            for u in range(2):
                                pe.wait_ge(wk_free, wk + NWK - NXP + u + 1)
                                key_products(0, u, d)
            pe.wait_ge(ld_last, 16)
            pe.wait_ge(wk_free, NWK * NSUP)
            pe.wait_ge(pt_ready, 2 * NSUP)
            def gate(h, xs, b):
                for kt in range(2):
                    ins = mm(bank(b), WGT[:, kt, DH * h:DH * (h + 1)], xs[kt], start=(kt == 0), stop=(kt == 1))
                ins.then_inc(gate_psum, 1)

            def project_out(c, more):
                for h in range(H + 4 if more else H + 3):
                    if h < H:
                        if h == 0:
                            pe.wait_ge(gate_raw, c * H + H)
                            pe.wait_ge(oc_in, c * 16 + 16)
                        if h >= 3:
                            pe.wait_ge(normed, c * H + h - 2)
                        mm(bank(h % 3).rearrange("v (t b) -> v t b", b=B), centre,
                           OC.rearrange("v (t g b h) -> v g h t b", g=2, b=B, h=8)[:, h // 8, h % 8], start=True, stop=True).then_inc(cen_psum, 1)
                    j = h - 1
                    if 0 <= j < H:
                        if j == 0:
                            pe.wait_ge(fin, c * 4 + 1)
                        if j >= 2:
                            pe.wait_ge(std, c * H + j - 1)
                        pe.wait_ge(squared, c * H + j + 1)
                        mm(bank(4 + j % 2), ones[:, :], SQO[:, j % 2, :], start=True, stop=True).then_inc(var_psum, 1)
                    j = h - 3
                    if 0 <= j < H:
                        pe.wait_ge(gated, c * H + j + 1)
                        for dh in range(2):
                            ins = mm(bank(6 + dh), WO[:, j, 128 * dh:128 * (dh + 1)], Z[:, j % 2, :], start=(j == 0), stop=(j == H - 1))
                        ins.then_inc(y_step, 1)
                    j = h - 4
                    if more and j >= 0:
                        pe.wait_ge(gate_raw, (c + 1) * H + j)
                        gate(j, [XNT[:, kt, bass.ds(c * CH + HALO + CH, CH)] for kt in range(2)], 3)
                pe.wait_ge(y_ready, c * 2 + 2)
                for q in range(4):
                    for dh in range(2):
                        ins = nc.tensor.transpose(bank(4 + q // 2)[:, D * (q % 2) + 128 * dh:D * (q % 2) + 128 * (dh + 1)], YT[:, dh, 128 * q:128 * (q + 1)], ident[:, :])
                    ins.then_inc(yt_psum, 1)

            for h in range(H):
                if h >= 4:
                    pe.wait_ge(gate_raw, h - 3)
                gate(h, [XNT[:, kt, HALO:HALO + CH] for kt in range(2)], h % 4)
            pe.wait_ge(centre_ready, 1)
            pe.wait_ge(ld_wo, 16)
            with pe.Fori(0, NCH - 1) as c:
                project_out(c, True)
            project_out(NCH - 1, False)


def kernel(**inputs):
    import numpy as np
    import concourse.bacc as bacc
    from concourse.bass_utils import run_bass_kernel_spmd

    a = {k: np.asarray(v) for k, v in inputs.items()}

    def attn(k):
        return a["L0_attn_" + k]

    def ffn(k):
        return a["L0_ffn_" + k]

    def per_head(v):
        return np.moveaxis(v.reshape(H, DH, -1), 0, -1).reshape(DH, -1)

    def two_tiles(v):
        return v.reshape(2, 128, -1).transpose(1, 0, 2).reshape(128, -1)

    def rows(v):
        return np.broadcast_to(v[None, :], (128, v.shape[0]))

    def lora_a(experts, shared):
        return np.concatenate([experts.transpose(1, 0, 2).reshape(shared.shape[0], -1), shared], axis=1)

    def lora_b(experts, shared):
        return np.concatenate([experts.reshape(-1, shared.shape[1]), shared], axis=0)

    small = np.concatenate(
        [per_head(attn(f"conv_{t}_w").reshape(H * DH, KC)) for t in "qkv"]
        + [per_head(attn(f"conv_{t}_b")) for t in "qkv"]
        + [per_head(attn("ba")), rows(attn("bb")), attn("ln_g")[:, None], attn("ln_b")[:, None],
           two_tiles(attn("Wb").T), rows(ffn("expert_bias")), two_tiles(ffn("W_router"))], axis=1)
    arrays = {
        "x_tm": attn("x").transpose(1, 0, 2).reshape(NT, D),
        "wqT": attn("Wq").T, "wkT": attn("Wk").T, "wvT": attn("Wv").T, "waT": attn("Wa").T,
        "wgT": attn("Wg").T, "woT": attn("Wo").T, "small": small,
        "w_gate": ffn("W_gate"), "w_up": ffn("W_up"), "w_down": ffn("W_down"),
        "a_gate": lora_a(ffn("A_gate"), ffn("sA_gate")), "b_gate": lora_b(ffn("B_gate"), ffn("sB_gate")),
        "a_up": lora_a(ffn("A_up"), ffn("sA_up")), "b_up": lora_b(ffn("B_up"), ffn("sB_up")),
        "a_down": lora_a(ffn("A_down"), ffn("sA_down")), "b_down": lora_b(ffn("B_down"), ffn("sB_down")),
    }
    arrays = {k: np.ascontiguousarray(v) for k, v in arrays.items()}
    nc = bacc.Bacc("TRN2", target_bir_lowering=False, num_devices=1)
    args = [nc.dram_tensor(k, v.shape, mybir.dt.from_np(v.dtype), kind="ExternalInput").ap() for k, v in arrays.items()]
    args.append(nc.dram_tensor("out", (NT, D), F32, kind="ExternalOutput").ap())
    build(nc, *args)
    r = run_bass_kernel_spmd(nc, [arrays], core_ids=[0])
    y = r.results[0]["out"]
    return y.reshape(T, B, D).transpose(1, 0, 2)
```
